# Optimizing a Trainium2 kernel written in Bass

```python
import numpy as np
import jax
import jax.numpy as jnp

def _softmax(x, axis=-1):
    return jax.nn.softmax(x, axis=axis)

def _gelu(x):
    return jax.nn.gelu(x, approximate=True)

def _silu(x):
    return jax.nn.silu(x)

def _sigmoid(x):
    return jax.nn.sigmoid(x)

def _layernorm(x, axis=-1, eps=1e-05):
    m = jnp.mean(x, axis=axis, keepdims=True)
    v = jnp.var(x, axis=axis, keepdims=True)
    return (x - m) / jnp.sqrt(v + eps)

def _scatter_add(tgt, idx, src, axis=0):
    return tgt.at[idx].add(src)

def _segment_sum(src, seg, n):
    return jax.ops.segment_sum(src, seg, n)
kernel_name = 'mk_lm_tower_d1_tok_ids512_r4_7e068f'

def setup_inputs(seed: int=0):
    np.random.seed(seed)
    _w = jnp.asarray

    def _rec_inputs():
        import jax
        import jax.numpy as jnp
        _rk = jax.random.key(seed)
        x = jax.random.randint(jax.random.fold_in(_rk, 1), (4, 1024), 0, 8000, jnp.int32)
        return x
    x = _rec_inputs()

    def _L0_tok_setup():
        import jax, jax.numpy as jnp
        import numpy as np
        VOCAB = 8000
        EMB = 128
        K = 3
        B, T = (8, 1024)
        key = jax.random.key(seed)
        k_ids, k_w = jax.random.split(key)
        token_ids = jax.random.randint(k_ids, (B, T), 0, VOCAB, dtype=jnp.int64)
        conv_w = jax.random.normal(k_w, (EMB, VOCAB, K), dtype=jnp.float32) * 0.02
        return {'token_ids': token_ids, 'conv_w': conv_w}
    _L0_tok_all = _L0_tok_setup()
    _L0_tok_in = {k: v for k, v in _L0_tok_all.items() if k in ('conv_w',)}
    del _L0_tok_all

    def _L0_attn_setup():
        import jax, jax.numpy as jnp
        import numpy as np
        import math
        HEADS = 8
        DIM_HEAD = 64
        key = jax.random.key(seed)
        k1, k2, k3 = jax.random.split(key, 3)
        b, n, dim = (4, 512, 128)
        inner = HEADS * DIM_HEAD
        x = jax.random.normal(k1, (b, n, dim), dtype=jnp.float32)
        W_qkv = jax.random.normal(k2, (dim, 4 * inner), dtype=jnp.float32) * dim ** (-0.5)
        W_out = jax.random.normal(k3, (2 * inner, dim), dtype=jnp.float32) * (2 * inner) ** (-0.5)
        b_out = jnp.zeros((dim,), dtype=jnp.float32)
        return {'x': x, 'W_qkv': W_qkv, 'W_out': W_out, 'b_out': b_out}
    _L0_attn_all = _L0_attn_setup()
    _L0_attn_in = {k: v for k, v in _L0_attn_all.items() if k in ('W_qkv', 'W_out', 'b_out')}
    del _L0_attn_all

    def _L0_ffn_setup():
        import jax, jax.numpy as jnp
        import numpy as np
        B, S, D, F, E = (4, 512, 128, 512, 8)
        key = jax.random.key(seed)
        k = jax.random.split(key, 5)
        x = jax.random.normal(k[0], (B, S, D), dtype=jnp.float32)
        Ws = jax.random.normal(k[1], (D, E), dtype=jnp.float32) * 0.02
        bs = jnp.zeros((E,), dtype=jnp.float32)
        W1 = jax.random.normal(k[2], (E, D, F), dtype=jnp.float32) * 0.02
        b1 = jnp.zeros((E, F), dtype=jnp.float32)
        W2 = jax.random.normal(k[3], (E, F, D), dtype=jnp.float32) * 0.02
        b2 = jnp.zeros((E, D), dtype=jnp.float32)
        return {'x': x, 'Ws': Ws, 'bs': bs, 'W1': W1, 'b1': b1, 'W2': W2, 'b2': b2}
    _L0_ffn_all = _L0_ffn_setup()
    _L0_ffn_in = {k: v for k, v in _L0_ffn_all.items() if k in ('Ws', 'bs', 'W1', 'b1', 'W2', 'b2')}
    del _L0_ffn_all
    return {'x': x, 'L0_tok_conv_w': _L0_tok_in['conv_w'], 'L0_attn_W_qkv': _L0_attn_in['W_qkv'], 'L0_attn_W_out': _L0_attn_in['W_out'], 'L0_attn_b_out': _L0_attn_in['b_out'], 'L0_ffn_Ws': _L0_ffn_in['Ws'], 'L0_ffn_bs': _L0_ffn_in['bs'], 'L0_ffn_W1': _L0_ffn_in['W1'], 'L0_ffn_b1': _L0_ffn_in['b1'], 'L0_ffn_W2': _L0_ffn_in['W2'], 'L0_ffn_b2': _L0_ffn_in['b2']}

def reference(x, L0_tok_conv_w, L0_attn_W_qkv, L0_attn_W_out, L0_attn_b_out, L0_ffn_Ws, L0_ffn_bs, L0_ffn_W1, L0_ffn_b1, L0_ffn_W2, L0_ffn_b2):
    import jax
    import jax.numpy as jnp

    def _L0_tok_ref(token_ids, conv_w):
        import jax, jax.numpy as jnp
        import numpy as np
        VOCAB = 8000
        EMB = 128
        K = 3
        B, T = (8, 1024)
        'Equivalent to one_hot(token_ids) -> Conv1d(V->F, k=K, pad=K//2, no bias).\n\n            Because the conv input is one-hot over the vocab channel, the V-dim\n            contraction reduces to gathering one weight row per (position, tap):\n              out[b,t,f] = sum_k W[f, token[b, t+k-pad], k]   (zero outside [0,T)).\n            '
        Bn, Tn = token_ids.shape
        F_, V_, Kn = conv_w.shape
        pad = Kn // 2
        out = jnp.zeros((Bn, Tn, F_), dtype=conv_w.dtype)
        t = jnp.arange(Tn)
        for k in range(Kn):
            shift = k - pad
            src = t + shift
            valid = (src >= 0) & (src < Tn)
            src_c = jnp.clip(src, 0, Tn - 1)
            ids = token_ids[:, src_c]
            table_k = conv_w[:, :, k].T
            emb = table_k[ids]
            out = out + jnp.where(valid[None, :, None], emb, jnp.zeros((), conv_w.dtype))
        return out

    def _L0_attn_ref(x, W_qkv, W_out, b_out):
        import jax, jax.numpy as jnp
        import numpy as np
        import math
        HEADS = 8
        DIM_HEAD = 64
        b, n, d = x.shape
        h, dh = (HEADS, DIM_HEAD)
        scale = dh ** (-0.5)
        qkvt = x @ W_qkv
        q, k, v, t = jnp.split(qkvt, 4, axis=-1)

        def to_heads(z):
            return z.reshape(b, n, h, dh).transpose(0, 2, 1, 3)
        q, k, v, t = map(to_heads, (q, k, v, t))
        dots = jnp.einsum('bhid,bhjd->bhij', q, k) * scale
        attn1 = jax.nn.softmax(dots, axis=-1)
        out1 = jnp.einsum('bhij,bhjd->bhid', attn1, v)
        pos = jnp.arange(1, n + 1, dtype=x.dtype)
        tg = jnp.abs(pos[None, :] - pos[:, None])
        attn2 = jnp.exp(-tg / jnp.asarray(math.e, dtype=x.dtype))
        attn2 = attn2 / attn2.sum(-1)
        out2 = jnp.einsum('ij,bhjd->bhid', attn2, t)
        out = jnp.concatenate([out1, out2], axis=-1)
        out = out.transpose(0, 2, 1, 3).reshape(b, n, 2 * h * dh)
        return out @ W_out + b_out

    def _L0_ffn_ref(x, Ws, bs, W1, b1, W2, b2):
        import jax, jax.numpy as jnp
        import numpy as np
        B, S, D, F, E = (4, 512, 128, 512, 8)
        Bb, Ss, Dd = x.shape
        xt = x.reshape(-1, Dd)
        logits = xt @ Ws + bs
        probs = jax.nn.softmax(logits, axis=-1)
        prob_max = jnp.max(probs, axis=-1)
        routes = jnp.argmax(probs, axis=-1)
        onehot = jax.nn.one_hot(routes, W1.shape[0], dtype=xt.dtype)

        def expert_ffn(w1, bb1, w2, bb2):
            h = jax.nn.gelu(xt @ w1 + bb1, approximate=False)
            return h @ w2 + bb2
        y = jax.vmap(expert_ffn)(W1, b1, W2, b2)
        out = jnp.einsum('te,etd->td', onehot, y)
        out = out * prob_max[:, None]
        return out.reshape(Bb, Ss, Dd)
    h = _L0_tok_ref(x, L0_tok_conv_w)
    h = h + _L0_attn_ref(_layernorm(h, axis=-1), L0_attn_W_qkv, L0_attn_W_out, L0_attn_b_out)
    h = h + _L0_ffn_ref(_layernorm(h, axis=-1), L0_ffn_Ws, L0_ffn_bs, L0_ffn_W1, L0_ffn_b1, L0_ffn_W2, L0_ffn_b2)
    return h

_drawn_inputs = setup_inputs


def setup_inputs(seed=0):
    import zlib

    import numpy as np

    out = dict(_drawn_inputs(seed))
    spreads = {'L0_attn_b_out': (0.0, 0.1),
     'L0_ffn_bs': (0.0, 0.1),
     'L0_ffn_b1': (0.0, 0.472),
     'L0_ffn_b2': (0.0, 0.1)}
    factors = {}
    for name, (base, spread) in spreads.items():
        noise = np.random.default_rng([zlib.crc32(name.encode()), seed]).standard_normal(out[name].shape)
        drawn = base * np.exp(spread * noise) if base else spread * noise
        out[name] = jnp.asarray(drawn.astype(out[name].dtype))
    for name, factor in factors.items():
        out[name] = (out[name] * factor).astype(out[name].dtype)
    return out
```

```python
from contextlib import ExitStack

import numpy as np

import concourse.bass as bass
from concourse import mybir

F32 = mybir.dt.float32
F32R = mybir.dt.float32r
BF16 = mybir.dt.bfloat16
I32 = mybir.dt.int32
U32 = mybir.dt.uint32
ALU = mybir.AluOpType
ACT = mybir.ActivationFunctionType
AX = mybir.AxisListType

P = 128
BATCH, SEQ, DIM, VOCAB, TAPS = 4, 1024, 128, 8000, 3
HEADS, DHEAD, FFN, EXPERTS = 8, 64, 512, 8
TPB = SEQ // P
TILES = BATCH * TPB
PAIRS = HEADS // 2
NHEAD = BATCH * HEADS
NPAIR = NHEAD // 2
HALF = SEQ // 2
FC = FFN // P
EPS = 1e-5
SCALE = DHEAD ** -0.5
SLOT_TILES = TILES + EXPERTS
WROW = FFN + FC * DIM + FC + DIM


def stage(n):
    units = []
    for kt in range(TPB):
        score = ("score", n, kt + 1) if kt < TPB - 1 else ("score", n + 1, 0)
        units += [(*score, 0), (*score, 1), ("pv", n, kt)]
    place = [(0, ("k", n + 1, 1))]
    for j in range(2 * TPB):
        place.append((1 + j * MAX_SPAN / (2 * TPB), ("max", n + 1, j % TPB, j // TPB)))
    place += [(15, ("v", n + 1)), (17, ("row", n + 1, 0)), (18, ("row", n + 1, 1))]
    place += [(2, ("sum", n - 1)), (5, ("den", n - 1))]
    place += [(14.5 + r, ("rcp", n - 1, r)) for r in range(RCPS)] + [(19, ("norm", n - 1))]
    place += [(21, ("q", n + 2, 0)), (22, ("q", n + 2, 1)), (22.5, ("ocopy", n)), (23, ("k", n + 2, 0))]
    place.sort(key=lambda x: x[0])
    out = []
    for u, unit in enumerate(units):
        out.append(unit)
        while place and place[0][0] < u + 1:
            out.append(place.pop(0)[1])
    return [e for e in out if 0 <= e[1] < NHEAD]


MAX_SPAN = 14
RCPS = 4
PROLOGUE = ([("q", 0, 0), ("q", 0, 1), ("k", 0, 0), ("k", 0, 1), ("v", 0)]
            + [("max", 0, j % TPB, j // TPB) for j in range(2 * TPB)]
            + [("row", 0, 0), ("row", 0, 1), ("q", 1, 0), ("q", 1, 1), ("k", 1, 0), ("score", 0, 0, 0), ("score", 0, 0, 1)])
EPILOGUE = [("sum", NHEAD - 1), ("den", NHEAD - 1)] + [("rcp", NHEAD - 1, r) for r in range(RCPS)] + [("norm", NHEAD - 1)]
MISC = ("q", "k", "v", "max", "row", "den")
BANKS = 3
ACT_OPS = {"q": 2, "k": 1, "v": 1, "row": 1, "den": 1}
DVE_OPS = {"q": 1, "k": 1, "max": 1}


def count_jobs():
    pe = act = dve = 0
    counts, order = {}, []
    every = PROLOGUE + [e for n in range(NHEAD) for e in stage(n)] + EPILOGUE
    for e in every:
        if e[0] in MISC:
            pe, act, dve = pe + 1, act + ACT_OPS.get(e[0], 0), dve + DVE_OPS.get(e[0], 0)
            counts[e] = (pe, act, dve)
            order.append(e)
    before = {e: order[i - BANKS] for i, e in enumerate(order) if i >= BANKS}
    return counts, before


COUNTS, BEFORE = count_jobs()


def shifted(e, pairs):
    return (e[0], e[1] + 2 * pairs, *e[2:])


def at(i, pair, value):
    if isinstance(i, int):
        return value(i)
    step = value(pair + 1) - value(pair)
    return value(pair) + (i - pair) * step


def bcast(ap, axis, count):
    return ap.unsqueeze(axis).to_broadcast([*ap.shape[:axis], count, *ap.shape[axis:]])


class Core:
    pass


def build(nc, ids, table, wqk, wv, wt_t, wo, wsr, small, ident, decay, experts, out):
    xd = nc.dram_tensor("sorted_rows", [SLOT_TILES * P, DIM], F32, kind="Internal").ap()
    yd = nc.dram_tensor("expert_rows", [SLOT_TILES * P, DIM], F32, kind="Internal").ap()
    with ExitStack() as ctx:
        def sb(name, shape, dt=F32):
            return ctx.enter_context(nc.sbuf_tensor(name, shape, dt))

        c = Core()
        c.ident = sb("ident_f", [P, P])
        c.small = sb("small", [P, small.shape[1]])
        c.h = sb("h", [P, TILES, DIM])
        c.ov = sb("o_heads", [P, NPAIR, SEQ])
        phase_embed(nc, c, ctx, ids, table, wqk, wv, wt_t, wo, small, ident, decay, xd)
        phase_router(nc, c, wo, wsr, xd, yd, experts, out)


SM_RS = 0
SM_BOUT = SM_RS + TPB
SM_BS = SM_BOUT + DIM
SM_PRIO = SM_BS + EXPERTS
SM_TILE = SM_PRIO + EXPERTS
SM_END = SM_TILE + SLOT_TILES


def norm_rows(nc, dve, chain, src, dst, st, mv, rs, std_ready, var_ready, b):
    for t in range(TPB):
        nc.vector.bn_stats(st[:, t, :], src[:, t, :]).then_inc(chain.sem, 1)
    chain.add(TPB)
    dve.wait_ge(chain.sem, chain.n)
    for t in range(TPB):
        nc.vector.bn_aggr(mv[:, t, :], st[:, t, :]).then_inc(chain.sem, 1)
    chain.add(TPB)
    dve.wait_ge(chain.sem, chain.n)
    nc.vector.tensor_scalar(rs[:, 0, :], mv[:, :, 1], EPS, None, ALU.add).then_inc(var_ready, 1)
    dve.wait_ge(std_ready, b + 1)
    nc.vector.reciprocal(rs[:, 2, :], rs[:, 1, :]).then_inc(chain.sem, 1)
    chain.add(1)
    dve.wait_ge(chain.sem, chain.n)
    nc.vector.tensor_tensor(rs[:, 3, :], rs[:, 2, :], rs[:, 2, :], ALU.mult).then_inc(chain.sem, 1)
    chain.add(1)
    dve.wait_ge(chain.sem, chain.n)
    nc.vector.tensor_tensor(rs[:, 4, :], rs[:, 3, :], rs[:, 0, :], ALU.mult).then_inc(chain.sem, 1)
    chain.add(1)
    dve.wait_ge(chain.sem, chain.n)
    nc.vector.tensor_scalar(rs[:, 5, :], rs[:, 4, :], -0.5, 1.5, ALU.mult, ALU.add).then_inc(chain.sem, 1)
    chain.add(1)
    dve.wait_ge(chain.sem, chain.n)
    nc.vector.tensor_tensor(rs[:, 6, :], rs[:, 5, :], rs[:, 2, :], ALU.mult).then_inc(chain.sem, 1)
    chain.add(1)
    dve.wait_ge(chain.sem, chain.n)
    for t in range(TPB):
        last = nc.vector.tensor_scalar(dst[:, t, :], src[:, t, :], mv[:, t, 0:1], rs[:, 6, t:t + 1],
                                       ALU.subtract, ALU.mult)
    return last


class Count:

    def __init__(self, sem):
        self.sem, self.n = sem, 0

    def add(self, k):
        self.n += k


def phase_embed(nc, c, outer, ids, table, wqk, wv, wt_t, wo, small, ident, decay, xd):
    with ExitStack() as keep:
        def kb(name, shape, dt=F32):
            return keep.enter_context(nc.sbuf_tensor(name, shape, dt))

        c.xh = kb("x_hi", [P, BATCH * SEQ], F32R)
        c.xl = kb("x_lo", [P, BATCH * SEQ], F32R)
        c.whl = kb("w_hilo", [P, HEADS, 2, 2, DHEAD], F32R)
        c.wv = kb("w_v", [P, HEADS * DHEAD])
        with ExitStack() as ctx:
            def sb(name, shape, dt=F32):
                return ctx.enter_context(nc.sbuf_tensor(name, shape, dt))

            def pb(name, shape):
                return ctx.enter_context(nc.psum_tensor(name, shape, F32))

            def sem(name):
                return ctx.enter_context(nc.semaphore(name))

            idx = sb("idx", [P, BATCH, TPB + 2], I32)
            g = sb("rows", [P, 2, TPB + 2, TAPS * DIM])
            wqk_s = sb("wqk_s", [P, HEADS, 2, DHEAD])
            wt_s = sb("wt_s", [P, PAIRS, DIM])
            wo2_s = sb("wo2_s", [P, PAIRS, DIM])
            dec = sb("dec", [P, 2 * TPB - 1, P])
            m2 = sb("m2", [P, DIM])
            xn = sb("xn", [P, TPB, DIM])
            xf = sb("xf", [P, SEQ])
            ys = sb("ys", [P, TPB, DIM])
            zero = sb("zero", [P, DIM])
            st = sb("st", [P, TPB, 6])
            mv = sb("mv", [P, TPB, 2])
            rs = sb("rs", [P, 7, TPB])
            ps_x = pb("ps_x", [P, SEQ])
            ps_y = pb("ps_y", [P, TPB, DIM])
            ps_o = pb("ps_o", [P, TPB, DIM])
            ps_m = pb("ps_m", [P, DIM])

            ids_in, w_in, zero_out = sem("ids_in"), sem("w_in"), sem("zero_out")
            rows_in = [sem("rows_in0"), sem("rows_in1")]
            conv_done, var_ready, std_ready, xn_ready = sem("conv_done"), sem("var_ready"), sem("std_ready"), sem("xn_ready")
            xt_full, xf_ready, xh_ready, xl_done = sem("xt_full"), sem("xf_ready"), sem("xh_ready"), sem("xl_done")
            m2_full, m2_ready, y_full, y_ready = sem("m2_full"), sem("m2_ready"), sem("y_full"), sem("y_ready")
            o_full, h_done, bias_done, zero_set, w_hi = sem("o_full"), sem("h_done"), sem("bias_done"), sem("zero_set"), sem("w_hi")
            chain = Count(sem("embed_chain"))

            with nc.Block() as block:
                @block.sync
                def _(sp):
                    sp.dma_start(idx[:], ids).then_inc(ids_in, 16)
                    for dst, src in ((c.small[:], small), (c.ident[:], ident), (wt_s[:], wt_t), (wo2_s[:], wo[:, 1]),
                                     (dec[:], decay), (wqk_s[:], wqk), (c.wv[:], wv)):
                        sp.dma_start(dst, src).then_inc(w_in, 16)
                    sp.wait_ge(zero_set, 1)
                    sp.dma_start(xd.rearrange("(s p) d -> p s d", p=P), bcast(zero[:], 1, SLOT_TILES)).then_inc(zero_out, 16)
                    sp.wait_ge(zero_out, 16)

                def add_bias(pool, b):
                    if b == 0:
                        pool.wait_ge(w_in, 7 * 16)
                    pool.wait_ge(xn_ready, b + 1)
                    hb = c.h[:, b * TPB:(b + 1) * TPB, :]
                    nc.gpsimd.tensor_tensor(hb, hb, bcast(c.small[:, SM_BOUT:SM_BOUT + DIM], 1, TPB), ALU.add).then_inc(bias_done, 1)

                @block.gpsimd
                def _(pool):
                    nc.gpsimd.memset(zero[:], 0.0).then_inc(zero_set, 1)
                    pool.wait_ge(ids_in, 16)
                    for b in range(BATCH):
                        if b >= 2:
                            pool.wait_ge(conv_done, b - 1)
                        for j in range(TPB + 2):
                            nc.gpsimd.indirect_dma_start(
                                g[:, b % 2, j, :], None, table,
                                bass.IndirectOffsetOnAxis(idx[:, b, j:j + 1].bitcast(U32), 0)).then_inc(rows_in[b % 2], 16)
                        if b >= 1:
                            add_bias(pool, b - 1)
                    add_bias(pool, BATCH - 1)

                @block.scalar
                def _(act):
                    act.wait_ge(m2_full, 1)
                    nc.scalar.activation(m2[:], ps_m[:], ACT.Copy).then_inc(m2_ready, 1)
                    for b in range(BATCH):
                        act.wait_ge(var_ready, b + 1)
                        nc.scalar.activation(rs[:, 1, :], rs[:, 0, :], ACT.Sqrt).then_inc(std_ready, 1)
                        act.wait_ge(xt_full, b + 1)
                        if b >= 1:
                            act.wait_ge(y_full, b)
                        nc.scalar.activation(xf[:], ps_x[:], ACT.Copy).then_inc(xf_ready, 1)
                        nc.scalar.activation(c.xh[:, b * SEQ:(b + 1) * SEQ], ps_x[:], ACT.Copy).then_inc(xh_ready, 1)

                @block.vector
                def _(dve):
                    def front(b):
                        gb = g[:, b % 2]
                        hb = c.h[:, b * TPB:(b + 1) * TPB, :]
                        dve.wait_ge(rows_in[b % 2], 16 * (TPB + 2) * (b // 2 + 1))
                        nc.vector.tensor_tensor(hb, gb[:, 0:TPB, 0:DIM], gb[:, 1:TPB + 1, DIM:2 * DIM], ALU.add).then_inc(chain.sem, 1)
                        chain.add(1)
                        dve.wait_ge(chain.sem, chain.n)
                        nc.vector.tensor_tensor(hb, hb, gb[:, 2:TPB + 2, 2 * DIM:3 * DIM], ALU.add).then_inc(conv_done, 1)
                        dve.wait_ge(conv_done, b + 1)
                        if b >= 1:
                            dve.wait_ge(xt_full, b)
                        norm_rows(nc, dve, chain, hb, xn, st, mv, rs, std_ready, var_ready, b).then_inc(xn_ready, 1)

                    dve.wait_ge(w_in, 7 * 16)
                    front(0)
                    nc.vector.tensor_copy(c.whl[:, :, :, 0, :], wqk_s[:]).then_inc(w_hi, 1)
                    dve.wait_ge(w_hi, 1)
                    nc.vector.tensor_tensor(c.whl[:, :, :, 1, :], wqk_s[:], c.whl[:, :, :, 0, :].bitcast(F32), ALU.subtract).then_inc(w_hi, 1)
                    for b in range(BATCH):
                        xs = slice(b * SEQ, (b + 1) * SEQ)
                        dve.wait_ge(xh_ready, b + 1)
                        nc.vector.tensor_tensor(c.xl[:, xs], ps_x[:], c.xh[:, xs].bitcast(F32), ALU.subtract).then_inc(xl_done, 1)
                        dve.wait_ge(y_full, b + 1)
                        if b >= 1:
                            dve.wait_ge(o_full, b)
                        nc.vector.tensor_tensor(ys[:], ps_y[:], c.small[:, SM_RS:SM_RS + TPB].unsqueeze(2).to_broadcast([P, TPB, DIM]), ALU.mult).then_inc(y_ready, 1)
                        if b + 1 < BATCH:
                            front(b + 1)
                        dve.wait_ge(o_full, b + 1)
                        dve.wait_ge(bias_done, b + 1)
                        hb = c.h[:, b * TPB:(b + 1) * TPB, :]
                        nc.vector.tensor_tensor(hb, hb, ps_o[:], ALU.add).then_inc(h_done, 1)

                @block.tensor
                def _(pe):
                    pe.wait_ge(w_in, 7 * 16)
                    for k in range(PAIRS):
                        last = nc.tensor.matmul(ps_m[:], wt_s[:, k, :], wo2_s[:, k, :], start=(k == 0), stop=(k == PAIRS - 1))
                    last.then_inc(m2_full, 1)
                    for b in range(BATCH):
                        pe.wait_ge(xn_ready, b + 1)
                        if b >= 1:
                            pe.wait_ge(xl_done, b)
                        for t in range(TPB):
                            last = nc.tensor.transpose(ps_x[:, t * P:(t + 1) * P], xn[:, t, :], c.ident[:])
                        last.then_inc(xt_full, 1)
                        pe.wait_ge(xf_ready, b + 1)
                        if b == 0:
                            pe.wait_ge(m2_ready, 1)
                        if b >= 1:
                            pe.wait_ge(y_ready, b)
                        for t in range(TPB):
                            last = nc.tensor.matmul(ps_y[:, t, :], xf[:, t * P:(t + 1) * P], m2[:], start=True, stop=True)
                        last.then_inc(y_full, 1)
                        pe.wait_ge(y_ready, b + 1)
                        if b >= 1:
                            pe.wait_ge(h_done, b)
                        for t in range(TPB):
                            for s in range(TPB):
                                last = nc.tensor.matmul(ps_o[:, t, :], dec[:, t - s + TPB - 1, :], ys[:, s, :], start=(s == 0), stop=(s == TPB - 1))
                        last.then_inc(o_full, 1)
        phase_attention(nc, c)


def phase_attention(nc, c):
    with ExitStack() as ctx:
        def sb(name, shape, dt=F32):
            return ctx.enter_context(nc.sbuf_tensor(name, shape, dt))

        def pb(name, shape):
            return ctx.enter_context(nc.psum_tensor(name, shape, F32))

        def sem(name):
            return ctx.enter_context(nc.semaphore(name))

        two = range(2)
        qa = [sb(f"qa{p}", [P, SEQ], F32R) for p in two]
        qb = [sb(f"qb{p}", [P, SEQ], F32R) for p in two]
        ka = [sb(f"ka{p}", [P, SEQ], F32R) for p in two]
        kb = [sb(f"kb{p}", [P, SEQ], F32R) for p in two]
        wd = [sb(f"wd{p}", [P, 4, 2, DHEAD], F32R) for p in two]
        xfs = sb("xfs", [P, SEQ])
        vb = [sb(f"vb{p}", [P, TPB, DHEAD]) for p in two]
        RING = 4
        pr = sb("probs", [P, RING, SEQ])
        ps = [sb(f"psum_keys{p}", [P, SEQ]) for p in two]
        psd = sb("psum_all", [P, SEQ])
        dn = sb("den", [P, HALF])
        rd = sb("rden", [P, HALF])
        oc = sb("o_whole", [P, HALF])
        os_ = [sb(f"o_out{p}", [P, HALF]) for p in two]
        mx2 = sb("mx2", [P, TPB, 2])
        mx = sb("mx", [P, TPB])
        nm = sb("nm", [P, TPB, 2], BF16)
        idb = sb("ident_b", [P, P], BF16)
        ones = sb("ones_v", [P, DHEAD])
        s_ps = [pb(f"scores{s}", [P, SEQ]) for s in two]
        o_ps = pb("values", [P, HALF])
        m_ps = [pb(f"misc{m}", [P, HALF]) for m in range(BANKS)]

        init, kb_ones = sem("attn_init"), sem("kb_ones")
        wd_in = [sem("wd_in0"), sem("wd_in1")]
        misc_full, act_misc, dve_misc = sem("misc_full"), sem("act_misc"), sem("dve_misc")
        s_full, exp_done, pv_done = sem("scores_full"), sem("exp_done"), sem("pv_done")
        key_sums, all_sums, xf_set = sem("key_sums"), sem("all_sums"), sem("xf_set")
        o_copied, rd_done = sem("o_copied"), sem("rd_done")
        nm_chain, nm_set, norm_done = sem("nm_chain"), sem("nm_set"), sem("norm_done")
        o_out = [sem("o_out0"), sem("o_out1")]

        job_at = {}
        k = 0
        for e in PROLOGUE + [e for n in range(NHEAD) for e in stage(n)] + EPILOGUE:
            if e[0] in MISC:
                job_at[e] = k
                k += 1

        def each(eng, handle):
            for e in PROLOGUE:
                handle(eng, e, 0, 0)
            for e in stage(0) + stage(1):
                handle(eng, e, 0, 0)
            with eng.Fori(1, NPAIR - 1) as i:
                for e in stage(2) + stage(3):
                    handle(eng, e, i, 1)
            for e in stage(NHEAD - 2) + stage(NHEAD - 1) + EPILOGUE:
                handle(eng, e, NPAIR - 1, NPAIR - 1)

        def of(e, i, pair, which):
            return at(i, pair, lambda x: COUNTS[shifted(e, x - pair)][which])

        def num(i, pair, n, per_head, offset):
            return per_head * n + offset + (i - pair) * (2 * per_head)

        with nc.Block() as block:
            @block.sync
            def _(sp):
                def load_w(m, i, pair):
                    h = (m + 2 * (i - pair)) % HEADS if not isinstance(i, int) else m % HEADS
                    src = c.whl[:, bass.ds(h, 1)] if not isinstance(h, int) else c.whl[:, h:h + 1]
                    src = src.rearrange("p a b c d -> p (a b c) d")
                    for copy in two:
                        sp.dma_start(wd[m % 2][:, :, copy, :].bitcast(F32), src.bitcast(F32)).then_inc(wd_in[m % 2], 16)

                load_w(0, 0, 0)
                load_w(1, 0, 0)

                def store(n, i, pair):
                    p = n % 2
                    sp.wait_ge(norm_done, num(i, pair, n, 1, 1))
                    u = n // 2 + (i - pair)
                    for half in two:
                        dst = c.ov[p * DHEAD:(p + 1) * DHEAD, bass.ds(u, 1) if not isinstance(u, int) else slice(u, u + 1),
                                   half * HALF:(half + 1) * HALF]
                        sp.dma_start(dst.rearrange("p a b -> p (a b)"), os_[p][half * DHEAD:(half + 1) * DHEAD, :]).then_inc(o_out[p], 16)

                def run(i, pair, first=False, last=False):
                    for n in (2 * pair, 2 * pair + 1):
                        if n + 2 < NHEAD:
                            sp.wait_ge(misc_full, of(("k", n, 1), i, pair, 0))
                            load_w(n + 2, i, pair)
                        if not (first and n == 0):
                            store(n - 1, i, pair)
                    if last:
                        store(NHEAD - 1, i, pair)

                run(0, 0, first=True)
                with sp.Fori(1, NPAIR - 1) as i:
                    run(i, 1)
                run(NPAIR - 1, NPAIR - 1, last=True)
                for p in two:
                    sp.wait_ge(o_out[p], 32 * NPAIR)

            @block.gpsimd
            def _(pool):
                nc.gpsimd.memset(ones[:], 1.0).then_inc(init, 1)
                nc.gpsimd.tensor_copy(idb[:], c.ident[:]).then_inc(init, 1)

                def set_x(m, i, pair):
                    if m > 0:
                        pool.wait_ge(misc_full, of(("v", m - 1), i, pair, 0))
                    b = m // HEADS if isinstance(i, int) else (i + (m // 2 - pair)) // PAIRS
                    cols = slice(b * SEQ, (b + 1) * SEQ) if isinstance(b, int) else bass.ds(b * SEQ, SEQ)
                    nc.gpsimd.tensor_tensor(xfs[:], c.xh[:, cols].bitcast(F32), c.xl[:, cols].bitcast(F32), ALU.add).then_inc(xf_set, 1)

                pool.wait_ge(init, 2)
                set_x(0, 0, 0)

                def run(i, pair):
                    for n in (2 * pair, 2 * pair + 1):
                        p = n % 2
                        for kt in range(1, TPB - 1):
                            pool.wait_ge(exp_done, num(i, pair, n, TPB, kt + 1))
                            if kt == 1:
                                if n >= 2:
                                    pool.wait_ge(all_sums, num(i, pair, n - 2, 1, 1))
                                a = pr[:, 0, :]
                            else:
                                pool.wait_ge(key_sums, num(i, pair, n, TPB - 2, kt - 1))
                                a = ps[p][:]
                            nc.gpsimd.tensor_tensor(ps[p][:], a, pr[:, kt % RING, :], ALU.add).then_inc(key_sums, 1)
                            if kt == 1 and p == 1 and n + 1 < NHEAD:
                                set_x(n + 1, i, pair)

                run(0, 0)
                with pool.Fori(1, NPAIR - 1) as i:
                    run(i, 1)
                run(NPAIR - 1, NPAIR - 1)

            @block.scalar
            def _(act):
                def exp(n, kt, i, pair):
                    act.wait_ge(s_full, num(i, pair, n, TPB, kt + 1))
                    idx = n * TPB + kt
                    if idx >= RING:
                        act.wait_ge(pv_done, num(i, pair, n, TPB, kt + 1 - RING))
                        r, adds = kt - RING, TPB - 2
                        if kt < RING - 1:
                            act.wait_ge(key_sums, num(i, pair, n - 1, adds, kt + RING))
                        elif kt < RING:
                            act.wait_ge(all_sums, num(i, pair, n - 1, 1, 1))
                        else:
                            act.wait_ge(key_sums, num(i, pair, n, adds, max(r, 1)))
                    nc.scalar.activation(pr[:, kt % RING, :], s_ps[kt % 2][:], ACT.Exp, scale=SCALE).then_inc(exp_done, 1)

                def handle(act, e, i, pair):
                    kind, m = e[0], e[1]
                    p = m % 2
                    if kind == "score":
                        if e[3] == 1:
                            exp(m, e[2], i, pair)
                        return
                    if kind == "ocopy":
                        act.wait_ge(pv_done, num(i, pair, m, TPB, TPB))
                        if m > 0:
                            act.wait_ge(norm_done, num(i, pair, m, 1, 0))
                        nc.scalar.activation(oc[:], o_ps[:], ACT.Copy).then_inc(o_copied, 1)
                        return
                    if kind not in ACT_OPS:
                        return
                    bank = m_ps[job_at[e] % BANKS]
                    act.wait_ge(misc_full, of(e, i, pair, 0))
                    half = slice(e[2] * HALF, (e[2] + 1) * HALF) if len(e) > 2 else None
                    if kind == "q":
                        nc.scalar.activation(qa[p][:, half], bank[:], ACT.Copy).then_inc(act_misc, 1)
                        nc.scalar.activation(qb[p][0:DHEAD, half], bank[0:DHEAD, :], ACT.Copy).then_inc(act_misc, 1)
                    elif kind == "k":
                        nc.scalar.activation(ka[p][:, half], bank[:], ACT.Copy).then_inc(act_misc, 1)
                    elif kind == "v":
                        nc.scalar.activation(vb[p][:].rearrange("p a b -> p (a b)"), bank[:], ACT.Copy).then_inc(act_misc, 1)
                    elif kind == "den":
                        if m > 0:
                            act.wait_ge(rd_done, num(i, pair, m, RCPS, 0))
                        nc.scalar.activation(dn[:], bank[:], ACT.Copy).then_inc(act_misc, 1)
                    else:
                        nc.scalar.activation(qb[p][DHEAD:DHEAD + 2, half], bank[DHEAD:DHEAD + 2, :], ACT.Copy).then_inc(act_misc, 1)

                each(act, handle)

            @block.vector
            def _(dve):
                def handle(dve, e, i, pair):
                    kind, m = e[0], e[1]
                    p = m % 2
                    if kind == "sum":
                        dve.wait_ge(exp_done, num(i, pair, m, TPB, TPB))
                        dve.wait_ge(key_sums, num(i, pair, m, TPB - 2, TPB - 2))
                        if m > 0:
                            dve.wait_ge(misc_full, of(("den", m - 1), i, pair, 0))
                        nc.vector.tensor_tensor(psd[:], ps[p][:], pr[:, (TPB - 1) % RING, :], ALU.add).then_inc(all_sums, 1)
                        return
                    if kind == "rcp":
                        if e[2] == 0:
                            dve.wait_ge(act_misc, of(("den", m), i, pair, 1))
                            if m > 0:
                                dve.wait_ge(norm_done, num(i, pair, m, 1, 0))
                        cols = slice(e[2] * HALF // RCPS, (e[2] + 1) * HALF // RCPS)
                        nc.vector.reciprocal(rd[:, cols], dn[:, cols]).then_inc(rd_done, 1)
                        return
                    if kind == "norm":
                        dve.wait_ge(rd_done, num(i, pair, m, RCPS, RCPS))
                        dve.wait_ge(o_copied, num(i, pair, m, 1, 1))
                        if m >= 2:
                            dve.wait_ge(o_out[p], num(i, pair, m, 16, 0) - 16 * p)
                        nc.vector.tensor_tensor(os_[p][:], oc[:], rd[:], ALU.mult).then_inc(norm_done, 1)
                        return
                    if kind not in DVE_OPS:
                        return
                    bank = m_ps[job_at[e] % BANKS]
                    dve.wait_ge(misc_full, of(e, i, pair, 0))
                    if kind == "q":
                        half = slice(e[2] * HALF, (e[2] + 1) * HALF)
                        dve.wait_ge(act_misc, of(e, i, pair, 1) + -1)
                        lo = qa[p][DHEAD:P, half]
                        nc.vector.tensor_tensor(lo, bank[DHEAD:P, :], lo.bitcast(F32), ALU.subtract).then_inc(dve_misc, 1)
                    elif kind == "k":
                        half = slice(e[2] * HALF, (e[2] + 1) * HALF)
                        dve.wait_ge(act_misc, of(e, i, pair, 1))
                        nc.vector.tensor_tensor(kb[p][0:DHEAD, half], bank[0:DHEAD, :], ka[p][0:DHEAD, half].bitcast(F32),
                                                ALU.subtract).then_inc(dve_misc, 1)
                    else:
                        t, half = e[2], e[3]
                        if t == 0 and half == 0 and m > 0:
                            dve.wait_ge(nm_chain, num(i, pair, m - 1, 2, 2))
                        nc.vector.tensor_reduce(mx2[:, t, half:half + 1], bank[:], AX.X, ALU.max).then_inc(dve_misc, 1)
                        if (t, half) == (TPB - 1, 1):
                            dve.wait_ge(dve_misc, of(e, i, pair, 2))
                            if m > 0:
                                dve.wait_ge(nm_set, num(i, pair, m - 1, 1, 1))
                            nc.vector.tensor_reduce(mx[:], mx2[:], AX.X, ALU.max).then_inc(nm_chain, 1)
                            dve.wait_ge(nm_chain, num(i, pair, m, 2, 1))
                            if m > 0:
                                dve.wait_ge(misc_full, of(("row", m - 1, 1), i, pair, 0))
                            nc.vector.tensor_scalar(nm[:, :, 0], mx[:], -1.0, None, ALU.mult).then_inc(nm_chain, 1)
                            dve.wait_ge(nm_chain, num(i, pair, m, 2, 2))
                            nc.vector.scalar_tensor_tensor(nm[:, :, 1], mx[:], -1.0, nm[:, :, 0], ALU.mult, ALU.subtract).then_inc(nm_set, 1)

                for p in two:
                    nc.vector.memset(kb[p][DHEAD:P, :].bitcast(F32), 1.0).then_inc(kb_ones, 1)
                each(dve, handle)

            @block.tensor
            def _(pe):
                pe.wait_ge(init, 2)
                pe.wait_ge(kb_ones, 2)

                def handle(pe, e, i, pair):
                    kind, m = e[0], e[1]
                    p = m % 2
                    if kind == "score":
                        kt = e[2]
                        idx = m * TPB + kt
                        half = e[3]
                        if kt == 0 and half == 0:
                            pe.wait_ge(act_misc, of(("row", m, 1), i, pair, 1))
                            pe.wait_ge(dve_misc, of(("k", m, 1), i, pair, 2))
                        if idx >= 2 and half == 0:
                            pe.wait_ge(exp_done, num(i, pair, m, TPB, kt - 1))
                        keys = slice(kt * P, (kt + 1) * P)
                        cols = slice(half * HALF, (half + 1) * HALF)
                        dst = s_ps[kt % 2][:, cols]
                        nc.tensor.matmul(dst, ka[p][:, keys], qa[p][:, cols], start=True, stop=False)
                        last = nc.tensor.matmul(dst, kb[p][0:DHEAD + 2, keys], qb[p][0:DHEAD + 2, cols], start=False, stop=True)
                        if half == 1:
                            last.then_inc(s_full, 1)
                        return
                    if kind == "pv":
                        kt = e[2]
                        pe.wait_ge(exp_done, num(i, pair, m, TPB, kt + 1))
                        if kt == 0:
                            pe.wait_ge(act_misc, of(("v", m), i, pair, 1))
                            if m > 0:
                                pe.wait_ge(o_copied, num(i, pair, m, 1, 0))
                        for half in two:
                            last = nc.tensor.matmul(o_ps[half * DHEAD:(half + 1) * DHEAD, :], vb[p][:, kt, :],
                                                    pr[:, kt % RING, half * HALF:(half + 1) * HALF],
                                                    start=(kt == 0), stop=(kt == TPB - 1))
                        last.then_inc(pv_done, 1)
                        return
                    if kind not in MISC:
                        return
                    bank = m_ps[job_at[e] % BANKS]
                    if e in BEFORE:
                        before = BEFORE[e]
                        if before[0] in ACT_OPS:
                            pe.wait_ge(act_misc, of(before, i, pair, 1))
                        if before[0] in DVE_OPS:
                            pe.wait_ge(dve_misc, of(before, i, pair, 2))
                    if kind in "qk":
                        if e[2] == 0 and kind == "q":
                            pe.wait_ge(wd_in[p], num(i, pair, m, 16, 32) - 16 * p)
                        w = wd[p][:, :, :, :].rearrange("p a b c -> p a (b c)")
                        hi, lo = (w[:, 0, :], w[:, 1, :]) if kind == "q" else (w[:, 2, :], w[:, 3, :])
                        b = m // HEADS if isinstance(i, int) else (i + (m // 2 - pair)) // PAIRS
                        off = b * SEQ + e[2] * HALF
                        cols = slice(off, off + HALF) if isinstance(off, int) else bass.ds(off, HALF)
                        nc.tensor.matmul(bank[:], hi, c.xh[:, cols], start=True, stop=False)
                        nc.tensor.matmul(bank[:], lo, c.xh[:, cols], start=False, stop=False)
                        last = nc.tensor.matmul(bank[:], hi, c.xl[:, cols], start=False, stop=True)
                    elif kind == "v":
                        pair_of = m // 2 if isinstance(i, int) else i + (m // 2 - pair)
                        pe.wait_ge(xf_set, pair_of + 1)
                        off = (pair_of % PAIRS) * 2 * DHEAD + p * DHEAD
                        cols = slice(off, off + DHEAD) if isinstance(off, int) else bass.ds(off, DHEAD)
                        for kt in range(TPB):
                            last = nc.tensor.matmul(bank[:, kt * DHEAD:(kt + 1) * DHEAD], xfs[:, kt * P:(kt + 1) * P], c.wv[:, cols],
                                                    start=True, stop=True)
                    elif kind == "max":
                        if e[2] == 0:
                            pe.wait_ge(act_misc, of(("k", m, e[3]), i, pair, 1))
                            if e[3] == 0:
                                pe.wait_ge(dve_misc, of(("q", m, 1), i, pair, 2))
                        last = nc.tensor.matmul(bank[:], qa[p][:, e[2] * P:(e[2] + 1) * P], ka[p][:, e[3] * HALF:(e[3] + 1) * HALF],
                                                start=True, stop=True)
                    elif kind == "row":
                        pe.wait_ge(nm_set, num(i, pair, m, 1, 1))
                        for t in range(TPB // 2):
                            last = nc.tensor.matmul(bank[DHEAD:DHEAD + 2, t * P:(t + 1) * P], nm[:, e[2] * TPB // 2 + t, :], idb[:],
                                                    start=True, stop=True)
                    else:
                        pe.wait_ge(all_sums, num(i, pair, m, 1, 1))
                        for half in two:
                            last = nc.tensor.matmul(bank[half * DHEAD:(half + 1) * DHEAD, :], ones[:], psd[:, half * HALF:(half + 1) * HALF],
                                                    start=True, stop=True)
                    last.then_inc(misc_full, 1)

                each(pe, handle)


def phase_router(nc, c, wo, wsr, xd, yd, experts, out):
    with ExitStack() as ctx:
        def sb(name, shape, dt=F32):
            return ctx.enter_context(nc.sbuf_tensor(name, shape, dt))

        def sem(name):
            return ctx.enter_context(nc.semaphore(name))

        xn = sb("xn2", [P, TILES, DIM])
        slot = sb("slot", [P, TILES], I32)
        pmax = sb("pmax", [P, TILES])
        te = sb("tile_expert", [P, SLOT_TILES], I32)
        with ExitStack() as inner:
            def isb(name, shape, dt=F32):
                return inner.enter_context(nc.sbuf_tensor(name, shape, dt))

            def ipb(name, shape, dt=F32):
                return inner.enter_context(nc.psum_tensor(name, shape, dt))

            def isem(name):
                return inner.enter_context(nc.semaphore(name))

            PAD = TILES // 2
            wo1_s = isb("wo1_s", [P, PAIRS, DIM])
            ws_s = isb("ws_s", [P, EXPERTS])
            xt = [isb(f"xt{p}", [P, SEQ]) for p in range(2)]
            st = isb("st2", [P, TPB, 6])
            mv = isb("mv2", [P, TPB, 2])
            rs = isb("rs2", [P, 7, TPB])
            lg = isb("logits", [P, TILES, EXPERTS])
            ex = isb("ex", [P, TILES, EXPERTS])
            pri = isb("prio", [P, TILES, EXPERTS])
            oh = isb("onehot", [P, TILES, EXPERTS])
            ohb = isb("onehot_b", [P, TILES, EXPERTS], BF16)
            t1 = isb("t1", [P, TILES])
            z = isb("z", [P, TILES])
            cum = [isb(f"cum{p}", [P, PAD + TILES, EXPERTS]) for p in range(2)]
            tot = isb("tot", [P, TILES, EXPERTS])
            slf = isb("slf", [P, TILES, EXPERTS])
            ntile = isb("ntile", [P, EXPERTS])
            nti = isb("nti", [P, EXPERTS], I32)
            be = [isb(f"be{p}", [P, 2 * EXPERTS]) for p in range(2)]
            base = isb("base", [P, EXPERTS])
            cmp = isb("cmp", [P, SLOT_TILES, EXPERTS])
            tef = isb("tef", [P, SLOT_TILES])
            up = isb("upper", [P, P], BF16)
            on = isb("ones_b", [P, P], BF16)
            ps_a = [ipb(f"ps_a{p}", [P, TPB, DIM]) for p in range(2)]
            ps_x = ipb("ps_x2", [P, SEQ])
            ps_l = ipb("ps_l", [P, TPB, EXPERTS])
            ps_r = ipb("ps_r", [P, 2, TILES * EXPERTS])

            w_in, a_full, h_done = isem("w2_in"), isem("a_full"), isem("h2_done")
            var_ready, std_ready, xn_ready = isem("var2_ready"), isem("std2_ready"), isem("xn2_ready")
            xt_full, xt_ready, l_full, l_done = isem("xt2_full"), isem("xt2_ready"), isem("l_full"), isem("l_done")
            ex_in, ex_done, oh_done, r_full, consts = isem("ex_in"), isem("ex_done"), isem("oh_done"), isem("r_full"), isem("consts")
            chain = Count(isem("router_chain"))

            with nc.Block() as block:
                @block.sync
                def _(sp):
                    sp.dma_start(wo1_s[:], wo[:, 0]).then_inc(w_in, 16)
                    sp.dma_start(ws_s[:], wsr).then_inc(w_in, 16)
                    sp.wait_ge(w_in, 32)

                @block.gpsimd
                def _(pool):
                    nc.gpsimd.memset(on[:], 1.0).then_inc(consts, 1)
                    for p in range(2):
                        nc.gpsimd.memset(cum[p][:, 0:PAD, :], 0.0).then_inc(consts, 1)
                        nc.gpsimd.memset(be[p][:, 0:EXPERTS], 0.0).then_inc(consts, 1)
                    pool.wait_ge(consts, 5)
                    nc.gpsimd.affine_select(out=up[:], in_=on[:], compare_op=ALU.is_gt, fill=0.0, base=0,
                                            pattern=[[1, P]], channel_multiplier=-1).then_inc(consts, 1)

                @block.scalar
                def _(act):
                    for b in range(BATCH):
                        act.wait_ge(var_ready, b + 1)
                        nc.scalar.activation(rs[:, 1, :], rs[:, 0, :], ACT.Sqrt).then_inc(std_ready, 1)
                        act.wait_ge(xt_full, b + 1)
                        if b >= 2:
                            act.wait_ge(l_full, b - 1)
                        nc.scalar.activation(xt[b % 2][:], ps_x[:], ACT.Copy).then_inc(xt_ready, 1)
                    act.wait_ge(ex_in, 1)
                    nc.scalar.activation(ex[:], lg[:], ACT.Exp).then_inc(ex_done, 1)

                @block.tensor
                def _(pe):
                    pe.wait_ge(w_in, 32)

                    def project(b):
                        if b >= 2:
                            pe.wait_ge(h_done, b - 1)
                        for t in range(TPB):
                            for k in range(PAIRS):
                                last = nc.tensor.matmul(ps_a[b % 2][:, t, :], c.ov[:, b * PAIRS + k, t * P:(t + 1) * P], wo1_s[:, k, :],
                                                        start=(k == 0), stop=(k == PAIRS - 1))
                        last.then_inc(a_full, 1)

                    project(0)
                    for b in range(BATCH):
                        if b + 1 < BATCH:
                            project(b + 1)
                        pe.wait_ge(xn_ready, b + 1)
                        if b >= 1:
                            pe.wait_ge(xt_ready, b)
                        for t in range(TPB):
                            last = nc.tensor.transpose(ps_x[:, t * P:(t + 1) * P], xn[:, b * TPB + t, :], c.ident[:])
                        last.then_inc(xt_full, 1)
                        pe.wait_ge(xt_ready, b + 1)
                        if b >= 1:
                            pe.wait_ge(l_done, b)
                        for t in range(TPB):
                            last = nc.tensor.matmul(ps_l[:, t, :], xt[b % 2][:, t * P:(t + 1) * P], ws_s[:], start=True, stop=True)
                        last.then_inc(l_full, 1)
                    pe.wait_ge(consts, 6)
                    pe.wait_ge(oh_done, 1)
                    nc.tensor.matmul(ps_r[:, 0, :], up[:], ohb[:].rearrange("p a b -> p (a b)"), start=True, stop=True)
                    nc.tensor.matmul(ps_r[:, 1, :], on[:], ohb[:].rearrange("p a b -> p (a b)"), start=True, stop=True).then_inc(r_full, 1)

                @block.vector
                def _(dve):
                    def link(ins):
                        ins.then_inc(chain.sem, 1)
                        chain.add(1)
                        dve.wait_ge(chain.sem, chain.n)

                    def logits(b):
                        dve.wait_ge(l_full, b + 1)
                        nc.vector.tensor_tensor(lg[:, b * TPB:(b + 1) * TPB, :], ps_l[:],
                                                bcast(c.small[:, SM_BS:SM_BS + EXPERTS], 1, TPB), ALU.add).then_inc(l_done, 1)

                    for b in range(BATCH):
                        hb = c.h[:, b * TPB:(b + 1) * TPB, :]
                        dve.wait_ge(a_full, b + 1)
                        nc.vector.tensor_tensor(hb, hb, ps_a[b % 2][:], ALU.add).then_inc(h_done, 1)
                        dve.wait_ge(h_done, b + 1)
                        norm_rows(nc, dve, chain, hb, xn[:, b * TPB:(b + 1) * TPB, :], st, mv, rs, std_ready, var_ready, b).then_inc(xn_ready, 1)
                        if b >= 1:
                            logits(b - 1)
                    logits(BATCH - 1)
                    dve.wait_ge(l_done, BATCH)
                    dve.wait_ge(consts, 5)

                    def over_e(ap):
                        return ap.unsqueeze(2).to_broadcast([P, TILES, EXPERTS])

                    def over_t(ap, n=TILES):
                        return bcast(ap, 1, n)

                    link(nc.vector.tensor_reduce(t1[:], lg[:], AX.X, ALU.max))
                    nc.vector.tensor_tensor(lg[:], lg[:], over_e(t1[:]), ALU.subtract).then_inc(ex_in, 1)
                    dve.wait_ge(ex_in, 1)
                    link(nc.vector.tensor_scalar(pri[:], lg[:], 0.0, None, ALU.is_ge))
                    link(nc.vector.tensor_tensor(pri[:], pri[:], over_t(c.small[:, SM_PRIO:SM_PRIO + EXPERTS]), ALU.mult))
                    link(nc.vector.tensor_reduce(t1[:], pri[:], AX.X, ALU.max))
                    link(nc.vector.tensor_tensor(oh[:], pri[:], over_e(t1[:]), ALU.is_equal))
                    nc.vector.tensor_copy(ohb[:], oh[:]).then_inc(oh_done, 1)
                    dve.wait_ge(ex_done, 1)
                    link(nc.vector.tensor_reduce(z[:], ex[:], AX.X, ALU.add))
                    link(nc.vector.reciprocal(pmax[:], z[:]))
                    dve.wait_ge(r_full, 1)
                    link(nc.vector.tensor_copy(tot[:].rearrange("p a b -> p (a b)"), ps_r[:, 1, :]))
                    link(nc.vector.tensor_copy(cum[0][:, PAD:, :], tot[:]))
                    s, k = 1, 0
                    while s < TILES:
                        a, d = cum[k % 2], cum[(k + 1) % 2]
                        link(nc.vector.tensor_tensor(d[:, PAD:, :], a[:, PAD:, :], a[:, PAD - s:PAD - s + TILES, :], ALU.add))
                        s, k = 2 * s, k + 1
                    inc = cum[k % 2][:, PAD:, :]
                    link(nc.vector.tensor_scalar(nti[:], inc[:, TILES - 1, :], float(P - 1), None, ALU.add))
                    link(nc.vector.tensor_scalar(nti[:], nti[:], P.bit_length() - 1, None, ALU.arith_shift_right))
                    link(nc.vector.tensor_copy(ntile[:], nti[:]))
                    link(nc.vector.tensor_copy(be[0][:, EXPERTS:], ntile[:]))
                    s, k = 1, 0
                    while s < EXPERTS:
                        a, d = be[k % 2], be[(k + 1) % 2]
                        link(nc.vector.tensor_tensor(d[:, EXPERTS:], a[:, EXPERTS:], a[:, EXPERTS - s:2 * EXPERTS - s], ALU.add))
                        s, k = 2 * s, k + 1
                    link(nc.vector.tensor_tensor(base[:], be[k % 2][:, EXPERTS:], ntile[:], ALU.subtract))
                    link(nc.vector.tensor_tensor(slf[:], inc, tot[:], ALU.subtract))
                    link(nc.vector.tensor_tensor(slf[:].rearrange("p a b -> p (a b)"), slf[:].rearrange("p a b -> p (a b)"), ps_r[:, 0, :], ALU.add))
                    link(nc.vector.scalar_tensor_tensor(slf[:], over_t(base[:]), float(P), slf[:], ALU.mult, ALU.add))
                    link(nc.vector.tensor_tensor(slf[:], slf[:], oh[:], ALU.mult))
                    link(nc.vector.tensor_reduce(t1[:], slf[:], AX.X, ALU.add))
                    link(nc.vector.tensor_copy(slot[:], t1[:]))
                    tiles = c.small[:, SM_TILE:SM_TILE + SLOT_TILES].unsqueeze(2).to_broadcast([P, SLOT_TILES, EXPERTS])
                    link(nc.vector.tensor_tensor(cmp[:], tiles, over_t(base[:], SLOT_TILES), ALU.is_ge))
                    link(nc.vector.tensor_reduce(tef[:], cmp[:], AX.X, ALU.add))
                    link(nc.vector.tensor_scalar(te[:], tef[:], -1.0, None, ALU.add))
        phase_experts(nc, c, xn, slot, pmax, te, xd, yd, experts, out)


def phase_experts(nc, c, xn, slot, pmax, te, xd, yd, experts, out):
    with ExitStack() as ctx:
        def sb(name, shape, dt=F32):
            return ctx.enter_context(nc.sbuf_tensor(name, shape, dt))

        def pb(name, shape):
            return ctx.enter_context(nc.psum_tensor(name, shape, F32))

        def sem(name):
            return ctx.enter_context(nc.semaphore(name))

        two = range(2)
        w = [sb(f"expert{p}", [P, WROW]) for p in two]
        xs = [sb(f"xs{p}", [P, DIM]) for p in two]
        xt = [sb(f"xst{p}", [P, P]) for p in two]
        hid = [sb(f"hid{p}", [P, FC, P]) for p in two]
        yo = [sb(f"yo{p}", [P, DIM]) for p in two]
        yg = sb("yg", [P, TILES, DIM])
        res = sb("res", [P, TILES, DIM])
        ps_x = [pb(f"ps_xs{p}", [P, P]) for p in two]
        ps_h = [pb(f"ps_h{p}", [P, FC, P]) for p in two]
        ps_y = [pb(f"ps_ye{p}", [P, DIM]) for p in two]

        sorted_ = sem("sorted")
        w_in, x_in = [sem("ew_in0"), sem("ew_in1")], [sem("ex_in0"), sem("ex_in1")]
        xt_full, xt_ready, h_full, hid_ready = sem("ext_full"), sem("ext_ready"), sem("eh_full"), sem("hid_ready")
        y_full, y_ready, y_out = sem("ey_full"), sem("ey_ready"), [sem("ey_out0"), sem("ey_out1")]
        back, res_done, stored = sem("rows_back"), sem("res_done"), sem("stored")
        W2, B1, B2 = FFN, FFN + FC * DIM, FFN + FC * DIM + FC

        with nc.Block() as block:
            @block.sync
            def _(sp):
                def load(s, p, i):
                    if i is not None:
                        sp.wait_ge(y_ready, s + -1)
                    e = sp.value_load(te[0:1, bass.ds(s, 1)] if i is not None else te[0:1, s:s + 1], min_val=0, max_val=EXPERTS - 1)
                    sp.dma_start(w[p][:], experts[bass.ds(e, 1)].rearrange("a p c -> (a p) c")).then_inc(w_in[p], 16)
                    if i is None and s == 0:
                        sp.wait_ge(sorted_, 16 * TILES)
                    src = xd[bass.ds(s * P, P), :] if i is not None else xd[s * P:(s + 1) * P, :]
                    sp.dma_start(xs[p][:], src).then_inc(x_in[p], 16)

                load(0, 0, None)
                load(1, 1, None)
                with sp.Fori(1, SLOT_TILES // 2) as i:
                    for p in two:
                        load(2 * i + p, p, i)
                for b in range(BATCH):
                    sp.wait_ge(res_done, b + 1)
                    sp.dma_start(out[b].rearrange("(p t) d -> p t d", t=TPB), res[:, b * TPB:(b + 1) * TPB, :]).then_inc(stored, 16)
                sp.wait_ge(stored, 16 * BATCH)

            @block.gpsimd
            def _(pool):
                for t in range(TILES):
                    nc.gpsimd.indirect_dma_start(xd, bass.IndirectOffsetOnAxis(slot[:, t:t + 1].bitcast(U32), 0), xn[:, t, :], None).then_inc(sorted_, 16)
                for p in two:
                    pool.wait_ge(y_out[p], 16 * (SLOT_TILES // 2))
                for t in range(TILES):
                    nc.gpsimd.indirect_dma_start(yg[:, t, :], None, yd, bass.IndirectOffsetOnAxis(slot[:, t:t + 1].bitcast(U32), 0)).then_inc(back, 16)

            def both(eng, tile):
                for p in two:
                    tile(p, p, 0)
                with eng.Fori(1, SLOT_TILES // 2) as i:
                    for p in two:
                        tile(2 * i + p, p, i)

            def first(i):
                return isinstance(i, int)

            @block.scalar
            def _(act):
                def tile(s, p, i):
                    act.wait_ge(h_full, s + 1)
                    if not first(i):
                        act.wait_ge(y_full, s + -1)
                    for f in range(FC):
                        last = nc.scalar.activation(hid[p][:, f, :], ps_h[p][:, f, :], ACT.Gelu, bias=w[p][:, B1 + f:B1 + f + 1])
                    last.then_inc(hid_ready, 1)
                    act.wait_ge(y_ready, s + 1)
                    rows = slice(s * P, (s + 1) * P) if first(i) else bass.ds(s * P, P)
                    act.dma_start(yd[rows, :], yo[p][:]).then_inc(y_out[p], 16)

                both(act, tile)

            @block.vector
            def _(dve):
                def tile(s, p, i):
                    dve.wait_ge(xt_full, s + 1)
                    nc.vector.tensor_copy(xt[p][:], ps_x[p][:]).then_inc(xt_ready, 1)
                    dve.wait_ge(y_full, s + 1)
                    if not first(i):
                        dve.wait_ge(y_out[p], i * 16)
                    nc.vector.tensor_tensor(yo[p][:], ps_y[p][:], w[p][:, B2:B2 + DIM], ALU.add).then_inc(y_ready, 1)

                both(dve, tile)
                dve.wait_ge(back, 16 * TILES)
                for b in range(BATCH):
                    for t in range(b * TPB, (b + 1) * TPB):
                        last = nc.vector.scalar_tensor_tensor(res[:, t, :], yg[:, t, :], pmax[:, t:t + 1], c.h[:, t, :], ALU.mult, ALU.add)
                    last.then_inc(res_done, 1)

            @block.tensor
            def _(pe):
                def tile(s, p, i):
                    pe.wait_ge(x_in[p], i * 16 + 16)
                    pe.wait_ge(w_in[p], i * 16 + 16)
                    if not first(i):
                        pe.wait_ge(xt_ready, s + -1)
                    nc.tensor.transpose(ps_x[p][:], xs[p][:], c.ident[:]).then_inc(xt_full, 1)
                    pe.wait_ge(xt_ready, s + 1)
                    if not first(i):
                        pe.wait_ge(hid_ready, s + -1)
                    for f in range(FC):
                        last = nc.tensor.matmul(ps_h[p][:, f, :], w[p][:, f * P:(f + 1) * P], xt[p][:], start=True, stop=True)
                    last.then_inc(h_full, 1)
                    pe.wait_ge(hid_ready, s + 1)
                    if not first(i):
                        pe.wait_ge(y_ready, s + -1)
                    for f in range(FC):
                        last = nc.tensor.matmul(ps_y[p][:], hid[p][:, f, :], w[p][:, W2 + f * DIM:W2 + (f + 1) * DIM],
                                                start=(f == 0), stop=(f == FC - 1))
                    last.then_inc(y_full, 1)

                both(pe, tile)


def constants():
    pos = np.arange(SEQ)
    decay = np.exp(-np.abs(pos[:, None] - pos[None, :]) / np.e)
    rows = decay.sum(-1)
    q = np.arange(P)
    diff = TPB * (q[:, None] - q[None, :])
    dec = np.stack([np.exp(-np.abs(diff - d) / np.e) for d in range(1 - TPB, TPB)], 1).astype(np.float32)
    small = np.zeros((P, SM_END), np.float32)
    small[:, SM_RS:SM_RS + TPB] = (1.0 / rows).reshape(P, TPB)
    small[:, SM_PRIO:SM_PRIO + EXPERTS] = np.arange(EXPERTS, 0, -1)
    small[:, SM_TILE:SM_TILE + SLOT_TILES] = np.arange(SLOT_TILES)
    return dec, small


def kernel(x, L0_tok_conv_w, L0_attn_W_qkv, L0_attn_W_out, L0_attn_b_out, L0_ffn_Ws, L0_ffn_bs,
           L0_ffn_W1, L0_ffn_b1, L0_ffn_W2, L0_ffn_b2):
    import numpy as np
    import concourse.bacc as bacc
    from concourse import mybir
    from concourse.bass_utils import run_bass_kernel_spmd

    x = np.asarray(x)
    dec, small = constants()
    padded = np.pad(x, ((0, 0), (1, 1)), constant_values=VOCAB)
    window = (np.arange(P) * TPB)[:, None] + np.arange(TPB + 2)[None, :]
    ids = np.ascontiguousarray(padded[:, window].transpose(1, 0, 2))
    cw = np.asarray(L0_tok_conv_w)
    table = np.concatenate([cw.transpose(1, 2, 0).reshape(VOCAB, TAPS * DIM), np.zeros((1, TAPS * DIM), cw.dtype)])
    wq, wk, wv, wt = np.split(np.asarray(L0_attn_W_qkv), 4, axis=1)
    wqk = np.stack([wq.reshape(DIM, HEADS, DHEAD), wk.reshape(DIM, HEADS, DHEAD)], 2)
    wt_t = wt.T.reshape(PAIRS, P, DIM).transpose(1, 0, 2)
    wo = np.asarray(L0_attn_W_out).reshape(PAIRS, 2, 2, DHEAD, DIM).transpose(1, 3, 2, 0, 4).reshape(P, 2, PAIRS, DIM)
    small[:, SM_BOUT:SM_BOUT + DIM] = np.asarray(L0_attn_b_out)[None, :]
    small[:, SM_BS:SM_BS + EXPERTS] = np.asarray(L0_ffn_bs)[None, :]
    w2 = np.asarray(L0_ffn_W2).reshape(EXPERTS, FC, P, DIM).transpose(0, 2, 1, 3).reshape(EXPERTS, P, FC * DIM)
    b1 = np.asarray(L0_ffn_b1).reshape(EXPERTS, FC, P).transpose(0, 2, 1)
    b2 = np.broadcast_to(np.asarray(L0_ffn_b2)[:, None, :], (EXPERTS, P, DIM))
    experts = np.concatenate([np.asarray(L0_ffn_W1), w2, b1, b2], axis=2)

    arrays = {"ids": ids, "table": table, "wqk": wqk, "wv": wv, "wt_t": wt_t, "wo": wo, "wsr": np.asarray(L0_ffn_Ws),
              "small_in": small, "ident_in": np.eye(P, dtype=np.float32), "decay": dec, "experts": experts}
    arrays = {name: np.ascontiguousarray(a) for name, a in arrays.items()}
    nc = bacc.Bacc("TRN2", target_bir_lowering=False, num_devices=1)
    aps = [nc.dram_tensor(name, a.shape, mybir.dt.from_np(a.dtype), kind="ExternalInput").ap() for name, a in arrays.items()]
    out = nc.dram_tensor("out", (BATCH, SEQ, DIM), mybir.dt.float32, kind="ExternalOutput").ap()
    build(nc, *aps, out)
    r = run_bass_kernel_spmd(nc, [arrays], core_ids=[0])
    return r.results[0]["out"]
```

```python
from contextlib import ExitStack

import numpy as np

import concourse.bass as bass
from concourse import mybir

F32 = mybir.dt.float32
F32R = mybir.dt.float32r
BF16 = mybir.dt.bfloat16
I32 = mybir.dt.int32
U32 = mybir.dt.uint32
ALU = mybir.AluOpType
ACT = mybir.ActivationFunctionType
AX = mybir.AxisListType

P = 128
BATCH, SEQ, DIM, VOCAB, TAPS = 4, 1024, 128, 8000, 3
HEADS, DHEAD, FFN, EXPERTS = 8, 64, 512, 8
TPB = SEQ // P
TILES = BATCH * TPB
PAIRS = HEADS // 2
NHEAD = BATCH * HEADS
NPAIR = NHEAD // 2
HALF = SEQ // 2
FC = FFN // P
EPS = 1e-5
SCALE = DHEAD ** -0.5
SLOT_TILES = TILES + EXPERTS
TOKENS = BATCH * SEQ
REGION = TOKENS + P
PAD_ROW = EXPERTS * REGION
ROW_H, ROW_P, ROW_ID, ROW = DIM, 2 * DIM, 2 * DIM + 1, 2 * DIM + 2
W_B1, W_W2, W_B2, W_END = FFN, FFN + FC, FFN + FC + FC * DIM, FFN + FC + FC * DIM + DIM


def stage(n):
    units = []
    for kt in range(TPB):
        score = ("score", n, kt + 1) if kt < TPB - 1 else ("score", n + 1, 0)
        units += [(*score, 0), (*score, 1), ("pv", n, kt)]
    place = [(0, ("k", n + 1, 1))]
    for j in range(2 * TPB):
        place.append((1 + j * MAX_SPAN / (2 * TPB), ("max", n + 1, j % TPB, j // TPB)))
    place += [(15, ("v", n + 1)), (17, ("row", n + 1, 0)), (18, ("row", n + 1, 1))]
    place += [(2, ("sum", n - 1)), (5, ("den", n - 1))]
    place += [(14.5 + r, ("rcp", n - 1, r)) for r in range(RCPS)] + [(19, ("norm", n - 1))]
    place += [(21, ("q", n + 2, 0)), (22, ("q", n + 2, 1)), (22.5, ("ocopy", n)), (23, ("k", n + 2, 0))]
    place.sort(key=lambda x: x[0])
    out = []
    for u, unit in enumerate(units):
        out.append(unit)
        while place and place[0][0] < u + 1:
            out.append(place.pop(0)[1])
    return [e for e in out if 0 <= e[1] < NHEAD]


MAX_SPAN = 14
RCPS = 4
PROLOGUE = ([("q", 0, 0), ("q", 0, 1), ("k", 0, 0), ("k", 0, 1), ("v", 0)]
            + [("max", 0, j % TPB, j // TPB) for j in range(2 * TPB)]
            + [("row", 0, 0), ("row", 0, 1), ("q", 1, 0), ("q", 1, 1), ("k", 1, 0), ("score", 0, 0, 0), ("score", 0, 0, 1)])
EPILOGUE = [("sum", NHEAD - 1), ("den", NHEAD - 1)] + [("rcp", NHEAD - 1, r) for r in range(RCPS)] + [("norm", NHEAD - 1)]
MISC = ("q", "k", "v", "max", "row", "den")
BANKS = 3
ACT_OPS = {"q": 2, "k": 1, "v": 1, "row": 1, "den": 1}
DVE_OPS = {"q": 1, "k": 1, "max": 1}


def count_jobs():
    pe = act = dve = 0
    counts, order = {}, []
    every = PROLOGUE + [e for n in range(NHEAD) for e in stage(n)] + EPILOGUE
    for e in every:
        if e[0] in MISC:
            pe, act, dve = pe + 1, act + ACT_OPS.get(e[0], 0), dve + DVE_OPS.get(e[0], 0)
            counts[e] = (pe, act, dve)
            order.append(e)
    before = {e: order[i - BANKS] for i, e in enumerate(order) if i >= BANKS}
    return counts, before


COUNTS, BEFORE = count_jobs()


def shifted(e, pairs):
    return (e[0], e[1] + 2 * pairs, *e[2:])


def at(i, pair, value):
    if isinstance(i, int):
        return value(i)
    step = value(pair + 1) - value(pair)
    return value(pair) + (i - pair) * step


def bcast(ap, axis, count):
    return ap.unsqueeze(axis).to_broadcast([*ap.shape[:axis], count, *ap.shape[axis:]])


class Core:
    pass


def build(nc, ids, table, wqk, wv, wt_t, wo, wsr, small, ident, decay, experts, row_ids, pad_row, out):
    xd = nc.dram_tensor("sorted_rows", [PAD_ROW + P, ROW], F32, kind="Internal").ap()
    with ExitStack() as ctx:
        def sb(name, shape, dt=F32):
            return ctx.enter_context(nc.sbuf_tensor(name, shape, dt))

        c = Core()
        c.ident = sb("ident_f", [P, P])
        c.small = sb("small", [P, small.shape[1]])
        c.h = sb("h", [P, TILES, DIM])
        c.ov = sb("o_heads", [P, NPAIR, SEQ])
        phase_embed(nc, c, ctx, ids, table, wqk, wv, wt_t, wo, small, ident, decay)
        phase_router(nc, c, wo, wsr, xd, experts, row_ids, pad_row, out)


SM_RS = 0
SM_BOUT = SM_RS + TPB
SM_BS = SM_BOUT + DIM
SM_PRIO = SM_BS + EXPERTS
SM_TILE = SM_PRIO + EXPERTS
SM_REGION = SM_TILE + SLOT_TILES
SM_PAD = SM_REGION + EXPERTS
SM_END = SM_PAD + EXPERTS


def norm_stats(nc, dve, chain, src, st, mv, rs, var_ready):
    for t in range(TPB):
        nc.vector.bn_stats(st[:, t, :], src[:, t, :]).then_inc(chain.sem, 1)
    chain.add(TPB)
    dve.wait_ge(chain.sem, chain.n)
    for t in range(TPB):
        nc.vector.bn_aggr(mv[:, t, :], st[:, t, :]).then_inc(chain.sem, 1)
    chain.add(TPB)
    dve.wait_ge(chain.sem, chain.n)
    nc.vector.tensor_scalar(rs[:, 0, :], mv[:, :, 1], EPS, None, ALU.add).then_inc(var_ready, 1)


def norm_rows(nc, dve, chain, src, dst, mv, rs, std_ready, b):
    dve.wait_ge(std_ready, b + 1)
    nc.vector.reciprocal(rs[:, 2, :], rs[:, 1, :]).then_inc(chain.sem, 1)
    chain.add(1)
    dve.wait_ge(chain.sem, chain.n)
    nc.vector.tensor_tensor(rs[:, 3, :], rs[:, 2, :], rs[:, 2, :], ALU.mult).then_inc(chain.sem, 1)
    chain.add(1)
    dve.wait_ge(chain.sem, chain.n)
    nc.vector.tensor_tensor(rs[:, 4, :], rs[:, 3, :], rs[:, 0, :], ALU.mult).then_inc(chain.sem, 1)
    chain.add(1)
    dve.wait_ge(chain.sem, chain.n)
    nc.vector.tensor_scalar(rs[:, 5, :], rs[:, 4, :], -0.5, 1.5, ALU.mult, ALU.add).then_inc(chain.sem, 1)
    chain.add(1)
    dve.wait_ge(chain.sem, chain.n)
    nc.vector.tensor_tensor(rs[:, 6, :], rs[:, 5, :], rs[:, 2, :], ALU.mult).then_inc(chain.sem, 1)
    chain.add(1)
    dve.wait_ge(chain.sem, chain.n)
    for t in range(TPB):
        last = nc.vector.tensor_scalar(dst[:, t, :], src[:, t, :], mv[:, t, 0:1], rs[:, 6, t:t + 1],
                                       ALU.subtract, ALU.mult)
    return last


class Count:

    def __init__(self, sem):
        self.sem, self.n = sem, 0

    def add(self, k):
        self.n += k


def phase_embed(nc, c, outer, ids, table, wqk, wv, wt_t, wo, small, ident, decay):
    with ExitStack() as keep:
        def kb(name, shape, dt=F32):
            return keep.enter_context(nc.sbuf_tensor(name, shape, dt))

        c.xh = kb("x_hi", [P, BATCH * SEQ], F32R)
        c.xl = kb("x_lo", [P, BATCH * SEQ], F32R)
        c.whl = kb("w_hilo", [P, HEADS, 2, 2, DHEAD], F32R)
        c.wv = kb("w_v", [P, HEADS * DHEAD])
        with ExitStack() as ctx:
            def sb(name, shape, dt=F32):
                return ctx.enter_context(nc.sbuf_tensor(name, shape, dt))

            def pb(name, shape):
                return ctx.enter_context(nc.psum_tensor(name, shape, F32))

            def sem(name):
                return ctx.enter_context(nc.semaphore(name))

            idx = sb("idx", [P, BATCH, TPB + 2], I32)
            g = sb("rows", [P, 2, TPB + 2, TAPS * DIM])
            wqk_s = sb("wqk_s", [P, HEADS, 2, DHEAD])
            wt_s = sb("wt_s", [P, PAIRS, DIM])
            wo2_s = sb("wo2_s", [P, PAIRS, DIM])
            dec = sb("dec", [P, 2 * TPB - 1, P])
            m2 = sb("m2", [P, DIM])
            xn = sb("xn", [P, TPB, DIM])
            xf = sb("xf", [P, SEQ])
            ys = sb("ys", [P, TPB, DIM])
            st = sb("st", [P, TPB, 6])
            mv = sb("mv", [P, TPB, 2])
            rs = sb("rs", [P, 7, TPB])
            ps_x = pb("ps_x", [P, SEQ])
            ps_y = pb("ps_y", [P, TPB, DIM])
            ps_o = pb("ps_o", [P, TPB, DIM])
            ps_m = pb("ps_m", [P, DIM])

            ids_in, w_in = sem("ids_in"), sem("w_in")
            rows_in = [sem("rows_in0"), sem("rows_in1")]
            conv_done, var_ready, std_ready, xn_ready = sem("conv_done"), sem("var_ready"), sem("std_ready"), sem("xn_ready")
            xt_full, xf_ready, xh_ready, xl_done = sem("xt_full"), sem("xf_ready"), sem("xh_ready"), sem("xl_done")
            m2_full, m2_ready, y_full, y_ready = sem("m2_full"), sem("m2_ready"), sem("y_full"), sem("y_ready")
            o_full, h_done, bias_done, w_hi = sem("o_full"), sem("h_done"), sem("bias_done"), sem("w_hi")
            chain = Count(sem("embed_chain"))

            with nc.Block() as block:
                @block.sync
                def _(sp):
                    sp.dma_start(idx[:], ids).then_inc(ids_in, 16)
                    for dst, src in ((c.small[:], small), (c.ident[:], ident), (wt_s[:], wt_t), (wo2_s[:], wo[:, 1]),
                                     (dec[:], decay), (wqk_s[:], wqk), (c.wv[:], wv)):
                        sp.dma_start(dst, src).then_inc(w_in, 16)

                def add_bias(pool, b):
                    if b == 0:
                        pool.wait_ge(w_in, 7 * 16)
                    pool.wait_ge(xn_ready, b + 1)
                    hb = c.h[:, b * TPB:(b + 1) * TPB, :]
                    nc.gpsimd.tensor_tensor(hb, hb, bcast(c.small[:, SM_BOUT:SM_BOUT + DIM], 1, TPB), ALU.add).then_inc(bias_done, 1)

                @block.gpsimd
                def _(pool):
                    pool.wait_ge(ids_in, 16)
                    for b in range(BATCH):
                        if b >= 2:
                            pool.wait_ge(conv_done, b - 1)
                        for j in range(TPB + 2):
                            nc.gpsimd.indirect_dma_start(
                                g[:, b % 2, j, :], None, table,
                                bass.IndirectOffsetOnAxis(idx[:, b, j:j + 1].bitcast(U32), 0)).then_inc(rows_in[b % 2], 16)
                        if b >= 1:
                            add_bias(pool, b - 1)
                    add_bias(pool, BATCH - 1)

                @block.scalar
                def _(act):
                    act.wait_ge(m2_full, 1)
                    nc.scalar.activation(m2[:], ps_m[:], ACT.Copy).then_inc(m2_ready, 1)
                    for b in range(BATCH):
                        act.wait_ge(var_ready, b + 1)
                        nc.scalar.activation(rs[:, 1, :], rs[:, 0, :], ACT.Sqrt).then_inc(std_ready, 1)
                        act.wait_ge(xt_full, b + 1)
                        if b >= 1:
                            act.wait_ge(y_full, b)
                        nc.scalar.activation(xf[:], ps_x[:], ACT.Copy).then_inc(xf_ready, 1)
                        nc.scalar.activation(c.xh[:, b * SEQ:(b + 1) * SEQ], ps_x[:], ACT.Copy).then_inc(xh_ready, 1)

                @block.vector
                def _(dve):
                    def front(b):
                        gb = g[:, b % 2]
                        hb = c.h[:, b * TPB:(b + 1) * TPB, :]
                        dve.wait_ge(rows_in[b % 2], 16 * (TPB + 2) * (b // 2 + 1))
                        nc.vector.tensor_tensor(hb, gb[:, 0:TPB, 0:DIM], gb[:, 1:TPB + 1, DIM:2 * DIM], ALU.add).then_inc(chain.sem, 1)
                        chain.add(1)
                        dve.wait_ge(chain.sem, chain.n)
                        nc.vector.tensor_tensor(hb, hb, gb[:, 2:TPB + 2, 2 * DIM:3 * DIM], ALU.add).then_inc(conv_done, 1)
                        dve.wait_ge(conv_done, b + 1)
                        if b >= 1:
                            dve.wait_ge(xt_full, b)
                        norm_stats(nc, dve, chain, hb, st, mv, rs, var_ready)
                        norm_rows(nc, dve, chain, hb, xn, mv, rs, std_ready, b).then_inc(xn_ready, 1)

                    dve.wait_ge(w_in, 7 * 16)
                    front(0)
                    nc.vector.tensor_copy(c.whl[:, :, :, 0, :], wqk_s[:]).then_inc(w_hi, 1)
                    dve.wait_ge(w_hi, 1)
                    nc.vector.tensor_tensor(c.whl[:, :, :, 1, :], wqk_s[:], c.whl[:, :, :, 0, :].bitcast(F32), ALU.subtract).then_inc(w_hi, 1)
                    for b in range(BATCH):
                        xs = slice(b * SEQ, (b + 1) * SEQ)
                        dve.wait_ge(xh_ready, b + 1)
                        nc.vector.tensor_tensor(c.xl[:, xs], ps_x[:], c.xh[:, xs].bitcast(F32), ALU.subtract).then_inc(xl_done, 1)
                        dve.wait_ge(y_full, b + 1)
                        if b >= 1:
                            dve.wait_ge(o_full, b)
                        nc.vector.tensor_tensor(ys[:], ps_y[:], c.small[:, SM_RS:SM_RS + TPB].unsqueeze(2).to_broadcast([P, TPB, DIM]), ALU.mult).then_inc(y_ready, 1)
                        if b + 1 < BATCH:
                            front(b + 1)
                        dve.wait_ge(o_full, b + 1)
                        dve.wait_ge(bias_done, b + 1)
                        hb = c.h[:, b * TPB:(b + 1) * TPB, :]
                        nc.vector.tensor_tensor(hb, hb, ps_o[:], ALU.add).then_inc(h_done, 1)

                @block.tensor
                def _(pe):
                    pe.wait_ge(w_in, 7 * 16)
                    for k in range(PAIRS):
                        last = nc.tensor.matmul(ps_m[:], wt_s[:, k, :], wo2_s[:, k, :], start=(k == 0), stop=(k == PAIRS - 1))
                    last.then_inc(m2_full, 1)
                    for b in range(BATCH):
                        pe.wait_ge(xn_ready, b + 1)
                        if b >= 1:
                            pe.wait_ge(xl_done, b)
                        for t in range(TPB):
                            last = nc.tensor.transpose(ps_x[:, t * P:(t + 1) * P], xn[:, t, :], c.ident[:])
                        last.then_inc(xt_full, 1)
                        pe.wait_ge(xf_ready, b + 1)
                        if b == 0:
                            pe.wait_ge(m2_ready, 1)
                        if b >= 1:
                            pe.wait_ge(y_ready, b)
                        for t in range(TPB):
                            last = nc.tensor.matmul(ps_y[:, t, :], xf[:, t * P:(t + 1) * P], m2[:], start=True, stop=True)
                        last.then_inc(y_full, 1)
                        pe.wait_ge(y_ready, b + 1)
                        if b >= 1:
                            pe.wait_ge(h_done, b)
                        for t in range(TPB):
                            for s in range(TPB):
                                last = nc.tensor.matmul(ps_o[:, t, :], dec[:, t - s + TPB - 1, :], ys[:, s, :], start=(s == 0), stop=(s == TPB - 1))
                        last.then_inc(o_full, 1)
        phase_attention(nc, c)


def phase_attention(nc, c):
    with ExitStack() as ctx:
        def sb(name, shape, dt=F32):
            return ctx.enter_context(nc.sbuf_tensor(name, shape, dt))

        def pb(name, shape):
            return ctx.enter_context(nc.psum_tensor(name, shape, F32))

        def sem(name):
            return ctx.enter_context(nc.semaphore(name))

        two = range(2)
        qa = [sb(f"qa{p}", [P, SEQ], F32R) for p in two]
        qb = [sb(f"qb{p}", [P, SEQ], F32R) for p in two]
        ka = [sb(f"ka{p}", [P, SEQ], F32R) for p in two]
        kb = [sb(f"kb{p}", [P, SEQ], F32R) for p in two]
        wd = [sb(f"wd{p}", [P, 4, 2, DHEAD], F32R) for p in two]
        xfs = sb("xfs", [P, SEQ])
        vb = [sb(f"vb{p}", [P, TPB, DHEAD]) for p in two]
        RING = 4
        pr = sb("probs", [P, RING, SEQ])
        ps = [sb(f"psum_keys{p}", [P, SEQ]) for p in two]
        psd = sb("psum_all", [P, SEQ])
        dn = sb("den", [P, HALF])
        rd = sb("rden", [P, HALF])
        oc = sb("o_whole", [P, HALF])
        os_ = [sb(f"o_out{p}", [P, HALF]) for p in two]
        mx2 = sb("mx2", [P, TPB, 2])
        mx = sb("mx", [P, TPB])
        nm = sb("nm", [P, TPB, 2], BF16)
        idb = sb("ident_b", [P, P], BF16)
        ones = sb("ones_v", [P, DHEAD])
        s_ps = [pb(f"scores{s}", [P, SEQ]) for s in two]
        o_ps = pb("values", [P, HALF])
        m_ps = [pb(f"misc{m}", [P, HALF]) for m in range(BANKS)]

        init, kb_ones = sem("attn_init"), sem("kb_ones")
        wd_in = [sem("wd_in0"), sem("wd_in1")]
        misc_full, act_misc, dve_misc = sem("misc_full"), sem("act_misc"), sem("dve_misc")
        s_full, exp_done, pv_done = sem("scores_full"), sem("exp_done"), sem("pv_done")
        key_sums, all_sums, xf_set = sem("key_sums"), sem("all_sums"), sem("xf_set")
        o_copied, rd_done = sem("o_copied"), sem("rd_done")
        nm_chain, nm_set, norm_done = sem("nm_chain"), sem("nm_set"), sem("norm_done")
        o_out = [sem("o_out0"), sem("o_out1")]

        job_at = {}
        k = 0
        for e in PROLOGUE + [e for n in range(NHEAD) for e in stage(n)] + EPILOGUE:
            if e[0] in MISC:
                job_at[e] = k
                k += 1

        def each(eng, handle):
            for e in PROLOGUE:
                handle(eng, e, 0, 0)
            for e in stage(0) + stage(1):
                handle(eng, e, 0, 0)
            with eng.Fori(1, NPAIR - 1) as i:
                for e in stage(2) + stage(3):
                    handle(eng, e, i, 1)
            for e in stage(NHEAD - 2) + stage(NHEAD - 1) + EPILOGUE:
                handle(eng, e, NPAIR - 1, NPAIR - 1)

        def of(e, i, pair, which):
            return at(i, pair, lambda x: COUNTS[shifted(e, x - pair)][which])

        def num(i, pair, n, per_head, offset):
            return per_head * n + offset + (i - pair) * (2 * per_head)

        with nc.Block() as block:
            @block.sync
            def _(sp):
                def load_w(m, i, pair):
                    h = (m + 2 * (i - pair)) % HEADS if not isinstance(i, int) else m % HEADS
                    src = c.whl[:, bass.ds(h, 1)] if not isinstance(h, int) else c.whl[:, h:h + 1]
                    src = src.rearrange("p a b c d -> p (a b c) d")
                    for copy in two:
                        sp.dma_start(wd[m % 2][:, :, copy, :].bitcast(F32), src.bitcast(F32)).then_inc(wd_in[m % 2], 16)

                load_w(0, 0, 0)
                load_w(1, 0, 0)

                def store(n, i, pair):
                    p = n % 2
                    sp.wait_ge(norm_done, num(i, pair, n, 1, 1))
                    u = n // 2 + (i - pair)
                    for half in two:
                        dst = c.ov[p * DHEAD:(p + 1) * DHEAD, bass.ds(u, 1) if not isinstance(u, int) else slice(u, u + 1),
                                   half * HALF:(half + 1) * HALF]
                        sp.dma_start(dst.rearrange("p a b -> p (a b)"), os_[p][half * DHEAD:(half + 1) * DHEAD, :]).then_inc(o_out[p], 16)

                def run(i, pair, first=False, last=False):
                    for n in (2 * pair, 2 * pair + 1):
                        if n + 2 < NHEAD:
                            sp.wait_ge(misc_full, of(("k", n, 1), i, pair, 0))
                            load_w(n + 2, i, pair)
                        if not (first and n == 0):
                            store(n - 1, i, pair)
                    if last:
                        store(NHEAD - 1, i, pair)

                run(0, 0, first=True)
                with sp.Fori(1, NPAIR - 1) as i:
                    run(i, 1)
                run(NPAIR - 1, NPAIR - 1, last=True)
                for p in two:
                    sp.wait_ge(o_out[p], 32 * NPAIR)

            @block.gpsimd
            def _(pool):
                nc.gpsimd.memset(ones[:], 1.0).then_inc(init, 1)
                nc.gpsimd.tensor_copy(idb[:], c.ident[:]).then_inc(init, 1)

                def set_x(m, i, pair):
                    if m > 0:
                        pool.wait_ge(misc_full, of(("v", m - 1), i, pair, 0))
                    b = m // HEADS if isinstance(i, int) else (i + (m // 2 - pair)) // PAIRS
                    cols = slice(b * SEQ, (b + 1) * SEQ) if isinstance(b, int) else bass.ds(b * SEQ, SEQ)
                    nc.gpsimd.tensor_tensor(xfs[:], c.xh[:, cols].bitcast(F32), c.xl[:, cols].bitcast(F32), ALU.add).then_inc(xf_set, 1)

                pool.wait_ge(init, 2)
                set_x(0, 0, 0)

                def run(i, pair):
                    for n in (2 * pair, 2 * pair + 1):
                        p = n % 2
                        for kt in range(1, TPB - 1):
                            pool.wait_ge(exp_done, num(i, pair, n, TPB, kt + 1))
                            if kt == 1:
                                if n >= 2:
                                    pool.wait_ge(all_sums, num(i, pair, n - 2, 1, 1))
                                a = pr[:, 0, :]
                            else:
                                pool.wait_ge(key_sums, num(i, pair, n, TPB - 2, kt - 1))
                                a = ps[p][:]
                            nc.gpsimd.tensor_tensor(ps[p][:], a, pr[:, kt % RING, :], ALU.add).then_inc(key_sums, 1)
                            if kt == 1 and p == 1 and n + 1 < NHEAD:
                                set_x(n + 1, i, pair)

                run(0, 0)
                with pool.Fori(1, NPAIR - 1) as i:
                    run(i, 1)
                run(NPAIR - 1, NPAIR - 1)

            @block.scalar
            def _(act):
                def exp(n, kt, i, pair):
                    act.wait_ge(s_full, num(i, pair, n, TPB, kt + 1))
                    idx = n * TPB + kt
                    if idx >= RING:
                        act.wait_ge(pv_done, num(i, pair, n, TPB, kt + 1 - RING))
                        r, adds = kt - RING, TPB - 2
                        if kt < RING - 1:
                            act.wait_ge(key_sums, num(i, pair, n - 1, adds, kt + RING))
                        elif kt < RING:
                            act.wait_ge(all_sums, num(i, pair, n - 1, 1, 1))
                        else:
                            act.wait_ge(key_sums, num(i, pair, n, adds, max(r, 1)))
                    nc.scalar.activation(pr[:, kt % RING, :], s_ps[kt % 2][:], ACT.Exp, scale=SCALE).then_inc(exp_done, 1)

                def handle(act, e, i, pair):
                    kind, m = e[0], e[1]
                    p = m % 2
                    if kind == "score":
                        if e[3] == 1:
                            exp(m, e[2], i, pair)
                        return
                    if kind == "ocopy":
                        act.wait_ge(pv_done, num(i, pair, m, TPB, TPB))
                        if m > 0:
                            act.wait_ge(norm_done, num(i, pair, m, 1, 0))
                        nc.scalar.activation(oc[:], o_ps[:], ACT.Copy).then_inc(o_copied, 1)
                        return
                    if kind not in ACT_OPS:
                        return
                    bank = m_ps[job_at[e] % BANKS]
                    act.wait_ge(misc_full, of(e, i, pair, 0))
                    half = slice(e[2] * HALF, (e[2] + 1) * HALF) if len(e) > 2 else None
                    if kind == "q":
                        nc.scalar.activation(qa[p][:, half], bank[:], ACT.Copy).then_inc(act_misc, 1)
                        nc.scalar.activation(qb[p][0:DHEAD, half], bank[0:DHEAD, :], ACT.Copy).then_inc(act_misc, 1)
                    elif kind == "k":
                        nc.scalar.activation(ka[p][:, half], bank[:], ACT.Copy).then_inc(act_misc, 1)
                    elif kind == "v":
                        nc.scalar.activation(vb[p][:].rearrange("p a b -> p (a b)"), bank[:], ACT.Copy).then_inc(act_misc, 1)
                    elif kind == "den":
                        if m > 0:
                            act.wait_ge(rd_done, num(i, pair, m, RCPS, 0))
                        nc.scalar.activation(dn[:], bank[:], ACT.Copy).then_inc(act_misc, 1)
                    else:
                        nc.scalar.activation(qb[p][DHEAD:DHEAD + 2, half], bank[DHEAD:DHEAD + 2, :], ACT.Copy).then_inc(act_misc, 1)

                each(act, handle)

            @block.vector
            def _(dve):
                def handle(dve, e, i, pair):
                    kind, m = e[0], e[1]
                    p = m % 2
                    if kind == "sum":
                        dve.wait_ge(exp_done, num(i, pair, m, TPB, TPB))
                        dve.wait_ge(key_sums, num(i, pair, m, TPB - 2, TPB - 2))
                        if m > 0:
                            dve.wait_ge(misc_full, of(("den", m - 1), i, pair, 0))
                        nc.vector.tensor_tensor(psd[:], ps[p][:], pr[:, (TPB - 1) % RING, :], ALU.add).then_inc(all_sums, 1)
                        return
                    if kind == "rcp":
                        if e[2] == 0:
                            dve.wait_ge(act_misc, of(("den", m), i, pair, 1))
                            if m > 0:
                                dve.wait_ge(norm_done, num(i, pair, m, 1, 0))
                        cols = slice(e[2] * HALF // RCPS, (e[2] + 1) * HALF // RCPS)
                        nc.vector.reciprocal(rd[:, cols], dn[:, cols]).then_inc(rd_done, 1)
                        return
                    if kind == "norm":
                        dve.wait_ge(rd_done, num(i, pair, m, RCPS, RCPS))
                        dve.wait_ge(o_copied, num(i, pair, m, 1, 1))
                        if m >= 2:
                            dve.wait_ge(o_out[p], num(i, pair, m, 16, 0) - 16 * p)
                        nc.vector.tensor_tensor(os_[p][:], oc[:], rd[:], ALU.mult).then_inc(norm_done, 1)
                        return
                    if kind not in DVE_OPS:
                        return
                    bank = m_ps[job_at[e] % BANKS]
                    dve.wait_ge(misc_full, of(e, i, pair, 0))
                    if kind == "q":
                        half = slice(e[2] * HALF, (e[2] + 1) * HALF)
                        dve.wait_ge(act_misc, of(e, i, pair, 1) + -1)
                        lo = qa[p][DHEAD:P, half]
                        nc.vector.tensor_tensor(lo, bank[DHEAD:P, :], lo.bitcast(F32), ALU.subtract).then_inc(dve_misc, 1)
                    elif kind == "k":
                        half = slice(e[2] * HALF, (e[2] + 1) * HALF)
                        dve.wait_ge(act_misc, of(e, i, pair, 1))
                        nc.vector.tensor_tensor(kb[p][0:DHEAD, half], bank[0:DHEAD, :], ka[p][0:DHEAD, half].bitcast(F32),
                                                ALU.subtract).then_inc(dve_misc, 1)
                    else:
                        t, half = e[2], e[3]
                        if t == 0 and half == 0 and m > 0:
                            dve.wait_ge(nm_chain, num(i, pair, m - 1, 2, 2))
                        nc.vector.tensor_reduce(mx2[:, t, half:half + 1], bank[:], AX.X, ALU.max).then_inc(dve_misc, 1)
                        if (t, half) == (TPB - 1, 1):
                            dve.wait_ge(dve_misc, of(e, i, pair, 2))
                            if m > 0:
                                dve.wait_ge(nm_set, num(i, pair, m - 1, 1, 1))
                            nc.vector.tensor_reduce(mx[:], mx2[:], AX.X, ALU.max).then_inc(nm_chain, 1)
                            dve.wait_ge(nm_chain, num(i, pair, m, 2, 1))
                            if m > 0:
                                dve.wait_ge(misc_full, of(("row", m - 1, 1), i, pair, 0))
                            nc.vector.tensor_scalar(nm[:, :, 0], mx[:], -1.0, None, ALU.mult).then_inc(nm_chain, 1)
                            dve.wait_ge(nm_chain, num(i, pair, m, 2, 2))
                            nc.vector.scalar_tensor_tensor(nm[:, :, 1], mx[:], -1.0, nm[:, :, 0], ALU.mult, ALU.subtract).then_inc(nm_set, 1)

                for p in two:
                    nc.vector.memset(kb[p][DHEAD:P, :].bitcast(F32), 1.0).then_inc(kb_ones, 1)
                each(dve, handle)

            @block.tensor
            def _(pe):
                pe.wait_ge(init, 2)
                pe.wait_ge(kb_ones, 2)

                def handle(pe, e, i, pair):
                    kind, m = e[0], e[1]
                    p = m % 2
                    if kind == "score":
                        kt = e[2]
                        idx = m * TPB + kt
                        half = e[3]
                        if kt == 0 and half == 0:
                            pe.wait_ge(act_misc, of(("row", m, 1), i, pair, 1))
                            pe.wait_ge(dve_misc, of(("k", m, 1), i, pair, 2))
                        if idx >= 2 and half == 0:
                            pe.wait_ge(exp_done, num(i, pair, m, TPB, kt - 1))
                        keys = slice(kt * P, (kt + 1) * P)
                        cols = slice(half * HALF, (half + 1) * HALF)
                        dst = s_ps[kt % 2][:, cols]
                        nc.tensor.matmul(dst, ka[p][:, keys], qa[p][:, cols], start=True, stop=False)
                        last = nc.tensor.matmul(dst, kb[p][0:DHEAD + 2, keys], qb[p][0:DHEAD + 2, cols], start=False, stop=True)
                        if half == 1:
                            last.then_inc(s_full, 1)
                        return
                    if kind == "pv":
                        kt = e[2]
                        pe.wait_ge(exp_done, num(i, pair, m, TPB, kt + 1))
                        if kt == 0:
                            pe.wait_ge(act_misc, of(("v", m), i, pair, 1))
                            if m > 0:
                                pe.wait_ge(o_copied, num(i, pair, m, 1, 0))
                        for half in two:
                            last = nc.tensor.matmul(o_ps[half * DHEAD:(half + 1) * DHEAD, :], vb[p][:, kt, :],
                                                    pr[:, kt % RING, half * HALF:(half + 1) * HALF],
                                                    start=(kt == 0), stop=(kt == TPB - 1))
                        last.then_inc(pv_done, 1)
                        return
                    if kind not in MISC:
                        return
                    bank = m_ps[job_at[e] % BANKS]
                    if e in BEFORE:
                        before = BEFORE[e]
                        if before[0] in ACT_OPS:
                            pe.wait_ge(act_misc, of(before, i, pair, 1))
                        if before[0] in DVE_OPS:
                            pe.wait_ge(dve_misc, of(before, i, pair, 2))
                    if kind in "qk":
                        if e[2] == 0 and kind == "q":
                            pe.wait_ge(wd_in[p], num(i, pair, m, 16, 32) - 16 * p)
                        w = wd[p][:, :, :, :].rearrange("p a b c -> p a (b c)")
                        hi, lo = (w[:, 0, :], w[:, 1, :]) if kind == "q" else (w[:, 2, :], w[:, 3, :])
                        b = m // HEADS if isinstance(i, int) else (i + (m // 2 - pair)) // PAIRS
                        off = b * SEQ + e[2] * HALF
                        cols = slice(off, off + HALF) if isinstance(off, int) else bass.ds(off, HALF)
                        nc.tensor.matmul(bank[:], hi, c.xh[:, cols], start=True, stop=False)
                        nc.tensor.matmul(bank[:], lo, c.xh[:, cols], start=False, stop=False)
                        last = nc.tensor.matmul(bank[:], hi, c.xl[:, cols], start=False, stop=True)
                    elif kind == "v":
                        pair_of = m // 2 if isinstance(i, int) else i + (m // 2 - pair)
                        pe.wait_ge(xf_set, pair_of + 1)
                        off = (pair_of % PAIRS) * 2 * DHEAD + p * DHEAD
                        cols = slice(off, off + DHEAD) if isinstance(off, int) else bass.ds(off, DHEAD)
                        for kt in range(TPB):
                            last = nc.tensor.matmul(bank[:, kt * DHEAD:(kt + 1) * DHEAD], xfs[:, kt * P:(kt + 1) * P], c.wv[:, cols],
                                                    start=True, stop=True)
                    elif kind == "max":
                        if e[2] == 0:
                            pe.wait_ge(act_misc, of(("k", m, e[3]), i, pair, 1))
                            if e[3] == 0:
                                pe.wait_ge(dve_misc, of(("q", m, 1), i, pair, 2))
                        last = nc.tensor.matmul(bank[:], qa[p][:, e[2] * P:(e[2] + 1) * P], ka[p][:, e[3] * HALF:(e[3] + 1) * HALF],
                                                start=True, stop=True)
                    elif kind == "row":
                        pe.wait_ge(nm_set, num(i, pair, m, 1, 1))
                        for t in range(TPB // 2):
                            last = nc.tensor.matmul(bank[DHEAD:DHEAD + 2, t * P:(t + 1) * P], nm[:, e[2] * TPB // 2 + t, :], idb[:],
                                                    start=True, stop=True)
                    else:
                        pe.wait_ge(all_sums, num(i, pair, m, 1, 1))
                        for half in two:
                            last = nc.tensor.matmul(bank[half * DHEAD:(half + 1) * DHEAD, :], ones[:], psd[:, half * HALF:(half + 1) * HALF],
                                                    start=True, stop=True)
                    last.then_inc(misc_full, 1)

                each(pe, handle)


def phase_router(nc, c, wo, wsr, xd, experts, row_ids, pad_row, out):
    with ExitStack() as ctx:
        def sb(name, shape, dt=F32):
            return ctx.enter_context(nc.sbuf_tensor(name, shape, dt))

        ew = sb("expert_weights", [P, EXPERTS, W_END])
        te = sb("tile_expert", [P, SLOT_TILES], I32)
        first_row = sb("tile_first_row", [P, SLOT_TILES], I32)
        with ExitStack() as inner:
            def isb(name, shape, dt=F32):
                return inner.enter_context(nc.sbuf_tensor(name, shape, dt))

            def ipb(name, shape, dt=F32):
                return inner.enter_context(nc.psum_tensor(name, shape, dt))

            def isem(name):
                return inner.enter_context(nc.semaphore(name))

            two = range(2)
            rows = isb("token_rows", [P, TILES, ROW])
            pad = isb("pad_row_s", [P, ROW])
            ids_s = isb("row_ids_s", [P, TILES], I32)
            slot = isb("slot", [P, TILES], I32)
            pad_slot = isb("pad_slot", [P, EXPERTS], I32)
            wo1_s = isb("wo1_s", [P, PAIRS, DIM])
            ws_s = isb("ws_s", [P, EXPERTS])
            xt = [isb(f"xt{p}", [P, SEQ]) for p in two]
            st = isb("st2", [P, TPB, 6])
            mv = [isb(f"mv2{p}", [P, TPB, 2]) for p in two]
            rs = [isb(f"rs2{p}", [P, 7, TPB]) for p in two]
            lg = isb("logits", [P, TPB, EXPERTS])
            lm = [isb(f"logits_less_max{p}", [P, TPB, EXPERTS]) for p in two]
            ex = [isb(f"ex{p}", [P, TPB, EXPERTS]) for p in two]
            pri = isb("prio", [P, TPB, EXPERTS])
            oh = [isb(f"onehot{p}", [P, TPB, EXPERTS]) for p in two]
            ohb = [isb(f"onehot_b{p}", [P, TPB, EXPERTS], BF16) for p in two]
            t1 = isb("t1", [P, TPB])
            z = isb("z", [P, TPB])
            mine = isb("mine", [P, BATCH, EXPERTS])
            acc = isb("acc", [P, BATCH, EXPERTS], BF16)
            slf = isb("slf", [P, TPB, EXPERTS])
            cnt = isb("cnt", [P, EXPERTS])
            ntile = isb("ntile", [P, EXPERTS])
            nti = isb("nti", [P, EXPERTS], I32)
            be = [isb(f"be{p}", [P, 2 * EXPERTS]) for p in two]
            base = isb("base", [P, EXPERTS])
            cmp = isb("cmp", [P, SLOT_TILES, EXPERTS])
            tef = isb("tef", [P, SLOT_TILES])
            tbase = isb("tbase", [P, SLOT_TILES])
            live = isb("live", [P, SLOT_TILES])
            up = isb("upper", [P, P], BF16)
            on = isb("ones_b", [P, P], BF16)
            ps_a = [ipb(f"ps_a{p}", [P, TPB, DIM]) for p in two]
            ps_x = ipb("ps_x2", [P, SEQ])
            ps_l = ipb("ps_l", [P, TPB, EXPERTS])
            ps_r = ipb("ps_r", [P, 3, TPB * EXPERTS])

            w_in, a_full, h_done = isem("w2_in"), isem("a_full"), isem("h2_done")
            var_ready, std_ready, xn_ready = isem("var2_ready"), isem("std2_ready"), isem("xn2_ready")
            xt_full, xt_ready, l_full, l_done = isem("xt2_full"), isem("xt2_ready"), isem("l_full"), isem("l_done")
            ex_in, ex_done, oh_done, r_full, consts = isem("ex_in"), isem("ex_done"), isem("oh_done"), isem("r_full"), isem("consts")
            acc_done, slot_done, pad_ready, scattered, ew_in = isem("acc_done"), isem("slot_done"), isem("pad_ready"), isem("scattered"), isem("ew_in")
            pad_out, slots_read = isem("pad_out"), isem("slots_read")
            chain = Count(isem("router_chain"))

            with nc.Block() as block:
                @block.sync
                def _(sp):
                    for dst, src in ((wo1_s[:], wo[:, 0]), (ws_s[:], wsr), (ids_s[:], row_ids), (pad[:], pad_row)):
                        sp.dma_start(dst, src).then_inc(w_in, 16)
                    for e in range(EXPERTS):
                        sp.dma_start(ew[:, e, :], experts[e]).then_inc(ew_in, 16)
                    sp.wait_ge(w_in, 64)
                    sp.dma_start(xd[PAD_ROW:PAD_ROW + P, :], pad[:]).then_inc(pad_out, 16)
                    sp.wait_ge(pad_out, 16)
                    sp.wait_ge(ew_in, 16 * EXPERTS)

                @block.gpsimd
                def _(pool):
                    nc.gpsimd.memset(on[:], 1.0).then_inc(consts, 1)
                    for p in two:
                        nc.gpsimd.memset(be[p][:, 0:EXPERTS], 0.0).then_inc(consts, 1)
                    pool.wait_ge(consts, 3)
                    nc.gpsimd.affine_select(out=up[:], in_=on[:], compare_op=ALU.is_gt, fill=0.0, base=0,
                                            pattern=[[1, P]], channel_multiplier=-1).then_inc(consts, 1)
                    pool.wait_ge(w_in, 64)
                    for b in range(BATCH):
                        pool.wait_ge(slot_done, b + 1)
                        for t in range(b * TPB, (b + 1) * TPB):
                            nc.gpsimd.indirect_dma_start(xd, bass.IndirectOffsetOnAxis(slot[:, t:t + 1].bitcast(U32), 0),
                                                         rows[:, t, :], None).then_inc(scattered, 16)
                    pool.wait_ge(pad_ready, 1)
                    for e in range(EXPERTS):
                        nc.gpsimd.indirect_dma_start(xd, bass.IndirectOffsetOnAxis(pad_slot[:, e:e + 1].bitcast(U32), 0),
                                                     pad[:], None).then_inc(scattered, 16)
                    pool.wait_ge(scattered, 16 * (TILES + EXPERTS))

                @block.scalar
                def _(act):
                    def root(b):
                        act.wait_ge(var_ready, b + 1)
                        nc.scalar.activation(rs[b % 2][:, 1, :], rs[b % 2][:, 0, :], ACT.Sqrt).then_inc(std_ready, 1)

                    root(0)
                    for b in range(BATCH):
                        act.wait_ge(xt_full, b + 1)
                        if b >= 2:
                            act.wait_ge(l_full, b - 1)
                        nc.scalar.activation(xt[b % 2][:], ps_x[:], ACT.Copy).then_inc(xt_ready, 1)
                        if b + 1 < BATCH:
                            root(b + 1)
                        act.wait_ge(ex_in, b + 1)
                        nc.scalar.activation(ex[b % 2][:], lm[b % 2][:], ACT.Exp).then_inc(ex_done, 1)

                @block.tensor
                def _(pe):
                    pe.wait_ge(w_in, 64)

                    def project(b):
                        if b >= 2:
                            pe.wait_ge(h_done, b - 1)
                        for t in range(TPB):
                            for k in range(PAIRS):
                                last = nc.tensor.matmul(ps_a[b % 2][:, t, :], c.ov[:, b * PAIRS + k, t * P:(t + 1) * P], wo1_s[:, k, :],
                                                        start=(k == 0), stop=(k == PAIRS - 1))
                        last.then_inc(a_full, 1)

                    def ranks(b):
                        pe.wait_ge(oh_done, b + 1)
                        if b >= 1:
                            pe.wait_ge(acc_done, b)
                        if b >= 1:
                            pe.wait_ge(slot_done, b)
                        dst, one = ps_r[:, b % 2, :], ohb[b % 2]
                        last = nc.tensor.matmul(dst, up[:], one[:].rearrange("p a b -> p (a b)"), start=True, stop=False)
                        for d in range(1, TPB):
                            last = nc.tensor.matmul(dst[:, d * EXPERTS:], on[:], one[:, 0:TPB - d, :].rearrange("p a b -> p (a b)"),
                                                    start=False, stop=(b == 0 and d == TPB - 1))
                        if b > 0:
                            for t in range(TPB):
                                last = nc.tensor.matmul(dst[:, t * EXPERTS:(t + 1) * EXPERTS], on[:], acc[:, b - 1, :],
                                                        start=False, stop=(t == TPB - 1))
                        last.then_inc(r_full, 1)

                    project(0)
                    project(1)
                    pe.wait_ge(consts, 4)
                    for b in range(BATCH):
                        pe.wait_ge(xn_ready, b + 1)
                        if b >= 1:
                            pe.wait_ge(xt_ready, b)
                        for t in range(TPB):
                            last = nc.tensor.transpose(ps_x[:, t * P:(t + 1) * P], rows[:, b * TPB + t, 0:DIM], c.ident[:])
                        last.then_inc(xt_full, 1)
                        pe.wait_ge(xt_ready, b + 1)
                        if b >= 1:
                            pe.wait_ge(l_done, b)
                        for t in range(TPB):
                            last = nc.tensor.matmul(ps_l[:, t, :], xt[b % 2][:, t * P:(t + 1) * P], ws_s[:], start=True, stop=True)
                        last.then_inc(l_full, 1)
                        if b + 2 < BATCH:
                            project(b + 2)
                        ranks(b)
                    pe.wait_ge(acc_done, BATCH)
                    pe.wait_ge(slot_done, BATCH)
                    nc.tensor.matmul(ps_r[:, 2, 0:EXPERTS], on[:], acc[:, BATCH - 1, :], start=True, stop=True).then_inc(r_full, 1)

                @block.vector
                def _(dve):
                    def link(ins):
                        ins.then_inc(chain.sem, 1)
                        chain.add(1)
                        dve.wait_ge(chain.sem, chain.n)

                    def tiles_of(b):
                        return slice(b * TPB, (b + 1) * TPB)

                    def front(b):
                        dve.wait_ge(a_full, b + 1)
                        nc.vector.tensor_tensor(rows[:, tiles_of(b), ROW_H:ROW_H + DIM], c.h[:, tiles_of(b), :], ps_a[b % 2][:], ALU.add).then_inc(h_done, 1)
                        dve.wait_ge(h_done, b + 1)
                        norm_stats(nc, dve, chain, rows[:, tiles_of(b), ROW_H:ROW_H + DIM], st, mv[b % 2], rs[b % 2], var_ready)

                    def norm(b):
                        norm_rows(nc, dve, chain, rows[:, tiles_of(b), ROW_H:ROW_H + DIM], rows[:, tiles_of(b), 0:DIM],
                                  mv[b % 2], rs[b % 2], std_ready, b).then_inc(xn_ready, 1)

                    def over_e(ap, n=TPB):
                        return ap.unsqueeze(2).to_broadcast([P, n, EXPERTS])

                    def over_t(ap, n=TPB):
                        return bcast(ap, 1, n)

                    def const(at, n=EXPERTS):
                        return c.small[:, at:at + n]

                    def choose(b):
                        p = b % 2
                        dve.wait_ge(l_full, b + 1)
                        nc.vector.tensor_tensor(lg[:], ps_l[:], over_t(const(SM_BS)), ALU.add).then_inc(l_done, 1)
                        dve.wait_ge(l_done, b + 1)
                        link(nc.vector.tensor_reduce(t1[:], lg[:], AX.X, ALU.max))
                        nc.vector.tensor_tensor(lm[p][:], lg[:], over_e(t1[:]), ALU.subtract).then_inc(ex_in, 1)
                        dve.wait_ge(ex_in, b + 1)
                        link(nc.vector.scalar_tensor_tensor(pri[:], lm[p][:], 0.0, over_t(const(SM_PRIO)), ALU.is_ge, ALU.mult))
                        link(nc.vector.tensor_reduce(t1[:], pri[:], AX.X, ALU.max))
                        nc.vector.tensor_tensor(ohb[p][:], pri[:], over_e(t1[:]), ALU.is_equal).then_inc(oh_done, 1)
                        dve.wait_ge(oh_done, b + 1)
                        nc.vector.tensor_copy(oh[p][:], ohb[p][:]).then_inc(chain.sem, 1)
                        chain.add(1)
                        link(nc.vector.tensor_reduce(mine[:, b, :], ohb[p][:].rearrange("p t e -> p e t"), AX.X, ALU.add))
                        if b == 0:
                            nc.vector.tensor_copy(acc[:, 0, :], mine[:, 0, :]).then_inc(acc_done, 1)
                        else:
                            nc.vector.tensor_tensor(acc[:, b, :], mine[:, b, :], acc[:, b - 1, :], ALU.add).then_inc(acc_done, 1)
                        dve.wait_ge(acc_done, b + 1)

                    def place(b):
                        p = b % 2
                        dve.wait_ge(ex_done, b + 1)
                        link(nc.vector.tensor_reduce(z[:], ex[p][:], AX.X, ALU.add))
                        link(nc.vector.reciprocal(rows[:, tiles_of(b), ROW_P], z[:]))
                        dve.wait_ge(r_full, b + 1)
                        link(nc.vector.tensor_tensor(slf[:], ps_r[:, p, :].rearrange("p (a b) -> p a b", b=EXPERTS), over_t(const(SM_REGION)), ALU.add))
                        link(nc.vector.tensor_tensor(slf[:], slf[:], oh[p][:], ALU.mult))
                        link(nc.vector.tensor_reduce(t1[:], slf[:], AX.X, ALU.add))
                        nc.vector.tensor_copy(slot[:, tiles_of(b)], t1[:]).then_inc(slot_done, 1)
                        dve.wait_ge(slot_done, b + 1)

                    dve.wait_ge(w_in, 64)
                    nc.vector.tensor_copy(rows[:, :, ROW_ID].bitcast(I32), ids_s[:]).then_inc(chain.sem, 1)
                    chain.add(1)
                    front(0)
                    norm(0)
                    for b in range(BATCH):
                        if b + 1 < BATCH:
                            front(b + 1)
                        choose(b)
                        if b + 1 < BATCH:
                            norm(b + 1)
                        place(b)
                    dve.wait_ge(r_full, BATCH + 1)
                    dve.wait_ge(consts, 4)
                    link(nc.vector.tensor_copy(cnt[:], ps_r[:, 2, 0:EXPERTS]))
                    nc.vector.tensor_tensor(pad_slot[:], cnt[:], const(SM_PAD), ALU.add).then_inc(pad_ready, 1)
                    link(nc.vector.tensor_scalar(nti[:], cnt[:], float(P - 1), None, ALU.add))
                    link(nc.vector.tensor_scalar(nti[:], nti[:], P.bit_length() - 1, None, ALU.arith_shift_right))
                    link(nc.vector.tensor_copy(ntile[:], nti[:]))
                    link(nc.vector.tensor_copy(be[0][:, EXPERTS:], ntile[:]))
                    s, k = 1, 0
                    while s < EXPERTS:
                        a, d = be[k % 2], be[(k + 1) % 2]
                        link(nc.vector.tensor_tensor(d[:, EXPERTS:], a[:, EXPERTS:], a[:, EXPERTS - s:2 * EXPERTS - s], ALU.add))
                        s, k = 2 * s, k + 1
                    total = be[k % 2][:, 2 * EXPERTS - 1:2 * EXPERTS]
                    link(nc.vector.tensor_tensor(base[:], be[k % 2][:, EXPERTS:], ntile[:], ALU.subtract))
                    tile = const(SM_TILE, SLOT_TILES)
                    link(nc.vector.tensor_tensor(cmp[:], over_e(tile, SLOT_TILES), over_t(base[:], SLOT_TILES), ALU.is_ge))
                    link(nc.vector.tensor_reduce(tef[:], cmp[:], AX.X, ALU.add))
                    link(nc.vector.tensor_scalar(tef[:], tef[:], -1.0, None, ALU.add))
                    link(nc.vector.tensor_copy(te[:], tef[:]))
                    link(nc.vector.tensor_tensor(cmp[:], cmp[:], over_t(base[:], SLOT_TILES), ALU.mult))
                    link(nc.vector.tensor_reduce(tbase[:], cmp[:], AX.X, ALU.max))
                    link(nc.vector.tensor_tensor(tbase[:], tile, tbase[:], ALU.subtract))
                    link(nc.vector.tensor_scalar(tbase[:], tbase[:], float(P), float(-PAD_ROW), ALU.mult, ALU.add))
                    link(nc.vector.scalar_tensor_tensor(tbase[:], tef[:], float(REGION), tbase[:], ALU.mult, ALU.add))
                    link(nc.vector.tensor_scalar(live[:], tile, total, None, ALU.is_lt))
                    link(nc.vector.tensor_tensor(tbase[:], tbase[:], live[:], ALU.mult))
                    link(nc.vector.tensor_scalar(first_row[:], tbase[:], float(PAD_ROW), None, ALU.add))
        phase_experts(nc, c, ew, te, first_row, xd, out)


def phase_experts(nc, c, ew, te, first_row, xd, out):
    with ExitStack() as ctx:
        def sb(name, shape, dt=F32):
            return ctx.enter_context(nc.sbuf_tensor(name, shape, dt))

        def pb(name, shape):
            return ctx.enter_context(nc.psum_tensor(name, shape, F32))

        def sem(name):
            return ctx.enter_context(nc.semaphore(name))

        RING, two = 4, range(2)
        w1 = [sb(f"w1_{p}", [P, W_W2]) for p in two]
        w2 = [sb(f"w2_{p}", [P, W_END - W_W2]) for p in two]
        xs = [sb(f"xs{r}", [P, ROW]) for r in range(RING)]
        xt = [sb(f"xst{p}", [P, P]) for p in two]
        hid = [sb(f"hid{p}", [P, FC, P]) for p in two]
        yb = [sb(f"yb{p}", [P, DIM]) for p in two]
        ro = [sb(f"row_out{r}", [P, DIM]) for r in range(RING)]
        rid = [sb(f"row_id{r}", [P, 1], I32) for r in range(RING)]
        none = sb("none", [P, 1], I32)
        ps_x = [pb(f"ps_xs{p}", [P, P]) for p in two]
        ps_h = [pb(f"ps_h{p}", [P, FC, P]) for p in two]
        ps_y = [pb(f"ps_ye{p}", [P, DIM]) for p in two]

        x_in, y_out = [sem(f"ex_in{r}") for r in range(RING)], [sem(f"ey_out{r}") for r in range(RING)]
        id_done, none_set = sem("eid_done"), sem("none_set")
        w1_ready, w2_ready, xt_full, xt_ready = sem("w1_ready"), sem("w2_ready"), sem("ext_full"), sem("ext_ready")
        h_full, hid_ready, y_full, y_sum, y_ready = sem("eh_full"), sem("hid_ready"), sem("ey_full"), sem("ey_sum"), sem("ey_ready")

        def each(eng, step):
            groups = SLOT_TILES // RING
            for r in range(RING):
                step(r, r, 0)
            with eng.Fori(1, groups - 1) as i:
                for r in range(RING):
                    step(RING * i + r, r, i)
            for r in range(RING):
                step(RING * (groups - 1) + r, r, groups - 1)

        def isn(s):
            return isinstance(s, int)

        def has(s, ahead):
            return not isn(s) or s + ahead < SLOT_TILES

        def past(s, back):
            return not isn(s) or s >= back

        def pick(table, s):
            return table[0:1, s:s + 1] if isn(s) else table[0:1, bass.ds(s, 1)]

        with nc.Block() as block:
            @block.sync
            def _(sp):
                def load(s, r, i):
                    if past(s, RING):
                        sp.wait_ge(y_ready, s + 1 - RING)
                        sp.wait_ge(id_done, s + 1 - RING)
                    row = sp.value_load(pick(first_row, s), min_val=0, max_val=PAD_ROW)
                    sp.dma_start(xs[r][:], xd[bass.ds(row, P), :]).then_inc(x_in[r], 16)

                each(sp, load)

            @block.gpsimd
            def _(pool):
                last_token = pool.alloc_register("last_token")
                pool.reg_mov(last_token, TOKENS - 1)

                def take_ids(s, r, i):
                    pool.wait_ge(x_in[r], i * 16 + 16)
                    if past(s, RING):
                        pool.wait_ge(y_out[r], i * 16)
                    if past(s, 1):
                        pool.wait_ge(id_done, s)
                        pool.wait_ge(y_ready, s)
                    nc.gpsimd.tensor_tensor(rid[r][:], xs[r][:, ROW_ID:ROW_ID + 1].bitcast(I32), none[:], ALU.add).then_inc(id_done, 1)

                def give(s, r, i):
                    if has(s, 1):
                        take_ids(s + 1, (r + 1) % RING, i + (r + 1) // RING)
                    else:
                        pool.wait_ge(id_done, SLOT_TILES)
                        pool.wait_ge(y_ready, SLOT_TILES)
                    nc.gpsimd.indirect_dma_start(out.rearrange("b t d -> (b t) d"), bass.IndirectOffsetOnAxis(rid[r][:].bitcast(U32), 0),
                                                 ro[r][:], None, bounds_check=last_token, oob_is_err=False).then_inc(y_out[r], 16)

                nc.gpsimd.memset(none[:], 0).then_inc(none_set, 1)
                pool.wait_ge(none_set, 1)
                take_ids(0, 0, 0)
                each(pool, give)
                for r in range(RING):
                    pool.wait_ge(y_out[r], 16 * (SLOT_TILES // RING))

            @block.scalar
            def _(act):
                def transposed(s, p):
                    act.wait_ge(xt_full, s + 1)
                    if past(s, 2):
                        act.wait_ge(h_full, s + -1)
                    nc.scalar.activation(xt[p][:], ps_x[p][:], ACT.Copy).then_inc(xt_ready, 1)

                def gelu(s, p):
                    act.wait_ge(h_full, s + 1)
                    act.wait_ge(w1_ready, s + 1)
                    if past(s, 2):
                        act.wait_ge(y_full, s + -1)
                    for f in range(FC):
                        last = nc.scalar.activation(hid[p][:, f, :], ps_h[p][:, f, :], ACT.Gelu, bias=w1[p][:, W_B1 + f:W_B1 + f + 1])
                    last.then_inc(hid_ready, 1)

                def step(s, r, i):
                    if has(s, 2):
                        transposed(s + 2, r % 2)
                    if has(s, 1):
                        gelu(s + 1, (r + 1) % 2)

                transposed(0, 0)
                gelu(0, 0)
                transposed(1, 1)
                each(act, step)

            @block.vector
            def _(dve):
                def take_w1(s, p):
                    e = dve.value_load(pick(te, s), min_val=0, max_val=EXPERTS - 1)
                    if past(s, 2):
                        dve.wait_ge(hid_ready, s + -1)
                    nc.vector.tensor_copy(w1[p][:], ew[:, bass.ds(e, 1), 0:W_W2].rearrange("p a b -> p (a b)")).then_inc(w1_ready, 1)

                def take_w2(s, p):
                    e = dve.value_load(pick(te, s), min_val=0, max_val=EXPERTS - 1)
                    if past(s, 2):
                        dve.wait_ge(y_sum, s + -1)
                    nc.vector.tensor_copy(w2[p][:], ew[:, bass.ds(e, 1), W_W2:W_END].rearrange("p a b -> p (a b)")).then_inc(w2_ready, 1)

                def step(s, r, i):
                    p = r % 2
                    if has(s, 2):
                        take_w1(s + 2, p)
                    if has(s, 1):
                        take_w2(s + 1, 1 - p)
                    dve.wait_ge(y_full, s + 1)
                    dve.wait_ge(w2_ready, s + 1)
                    if past(s, 2):
                        dve.wait_ge(y_ready, s + -1)
                    nc.vector.tensor_tensor(yb[p][:], ps_y[p][:], w2[p][:, FC * DIM:], ALU.add).then_inc(y_sum, 1)
                    dve.wait_ge(y_sum, s + 1)
                    dve.wait_ge(x_in[r], i * 16 + 16)
                    if past(s, RING):
                        dve.wait_ge(y_out[r], i * 16)
                    nc.vector.scalar_tensor_tensor(ro[r][:], yb[p][:], xs[r][:, ROW_P:ROW_P + 1], xs[r][:, ROW_H:ROW_H + DIM],
                                                   ALU.mult, ALU.add).then_inc(y_ready, 1)

                take_w1(0, 0)
                take_w1(1, 1)
                take_w2(0, 0)
                each(dve, step)

            @block.tensor
            def _(pe):
                def transpose(s, r, i):
                    pe.wait_ge(x_in[r], i * 16 + 16)
                    if past(s, 2):
                        pe.wait_ge(xt_ready, s + -1)
                    nc.tensor.transpose(ps_x[r % 2][:], xs[r][:, 0:DIM], c.ident[:]).then_inc(xt_full, 1)

                def hidden(s, p):
                    pe.wait_ge(xt_ready, s + 1)
                    pe.wait_ge(w1_ready, s + 1)
                    if past(s, 2):
                        pe.wait_ge(hid_ready, s + -1)
                    for f in range(FC):
                        last = nc.tensor.matmul(ps_h[p][:, f, :], w1[p][:, f * P:(f + 1) * P], xt[p][:], start=True, stop=True)
                    last.then_inc(h_full, 1)

                def output(s, p):
                    pe.wait_ge(hid_ready, s + 1)
                    pe.wait_ge(w2_ready, s + 1)
                    if past(s, 2):
                        pe.wait_ge(y_sum, s + -1)
                    for f in range(FC):
                        last = nc.tensor.matmul(ps_y[p][:], hid[p][:, f, :], w2[p][:, f * DIM:(f + 1) * DIM],
                                                start=(f == 0), stop=(f == FC - 1))
                    last.then_inc(y_full, 1)

                def step(s, r, i):
                    if has(s, 2):
                        transpose(s + 2, (r + 2) % RING, i + (r + 2) // RING)
                    if has(s, 1):
                        hidden(s + 1, (r + 1) % 2)
                    output(s, r % 2)

                transpose(0, 0, 0)
                hidden(0, 0)
                transpose(1, 1, 0)
                each(pe, step)


def constants():
    pos = np.arange(SEQ)
    decay = np.exp(-np.abs(pos[:, None] - pos[None, :]) / np.e)
    rows = decay.sum(-1)
    q = np.arange(P)
    diff = TPB * (q[:, None] - q[None, :])
    dec = np.stack([np.exp(-np.abs(diff - d) / np.e) for d in range(1 - TPB, TPB)], 1).astype(np.float32)
    small = np.zeros((P, SM_END), np.float32)
    small[:, SM_RS:SM_RS + TPB] = (1.0 / rows).reshape(P, TPB)
    small[:, SM_PRIO:SM_PRIO + EXPERTS] = np.arange(EXPERTS, 0, -1)
    small[:, SM_TILE:SM_TILE + SLOT_TILES] = np.arange(SLOT_TILES)
    small[:, SM_REGION:SM_REGION + EXPERTS] = np.arange(EXPERTS) * REGION
    small[:, SM_PAD:SM_PAD + EXPERTS] = np.arange(EXPERTS)[None, :] * REGION + q[:, None]
    row_ids = (np.arange(BATCH)[None, :, None] * SEQ + q[:, None, None] * TPB + np.arange(TPB)).astype(np.int32).reshape(P, TILES)
    pad_row = np.zeros((P, ROW), np.float32)
    pad_row[:, ROW_ID] = (TOKENS + q).astype(np.int32).view(np.float32)
    return dec, small, row_ids, pad_row


def kernel(x, L0_tok_conv_w, L0_attn_W_qkv, L0_attn_W_out, L0_attn_b_out, L0_ffn_Ws, L0_ffn_bs,
           L0_ffn_W1, L0_ffn_b1, L0_ffn_W2, L0_ffn_b2):
    import numpy as np
    import concourse.bacc as bacc
    from concourse import mybir
    from concourse.bass_utils import run_bass_kernel_spmd

    x = np.asarray(x)
    dec, small, row_ids, pad_row = constants()
    padded = np.pad(x, ((0, 0), (1, 1)), constant_values=VOCAB)
    window = (np.arange(P) * TPB)[:, None] + np.arange(TPB + 2)[None, :]
    ids = np.ascontiguousarray(padded[:, window].transpose(1, 0, 2))
    cw = np.asarray(L0_tok_conv_w)
    table = np.concatenate([cw.transpose(1, 2, 0).reshape(VOCAB, TAPS * DIM), np.zeros((1, TAPS * DIM), cw.dtype)])
    wq, wk, wv, wt = np.split(np.asarray(L0_attn_W_qkv), 4, axis=1)
    wqk = np.stack([wq.reshape(DIM, HEADS, DHEAD), wk.reshape(DIM, HEADS, DHEAD)], 2)
    wt_t = wt.T.reshape(PAIRS, P, DIM).transpose(1, 0, 2)
    wo = np.asarray(L0_attn_W_out).reshape(PAIRS, 2, 2, DHEAD, DIM).transpose(1, 3, 2, 0, 4).reshape(P, 2, PAIRS, DIM)
    small[:, SM_BOUT:SM_BOUT + DIM] = np.asarray(L0_attn_b_out)[None, :]
    small[:, SM_BS:SM_BS + EXPERTS] = np.asarray(L0_ffn_bs)[None, :]
    w2 = np.asarray(L0_ffn_W2).reshape(EXPERTS, FC, P, DIM).transpose(0, 2, 1, 3).reshape(EXPERTS, P, FC * DIM)
    b1 = np.asarray(L0_ffn_b1).reshape(EXPERTS, FC, P).transpose(0, 2, 1)
    b2 = np.broadcast_to(np.asarray(L0_ffn_b2)[:, None, :], (EXPERTS, P, DIM))
    experts = np.concatenate([np.asarray(L0_ffn_W1), b1, w2, b2], axis=2)

    arrays = {"ids": ids, "table": table, "wqk": wqk, "wv": wv, "wt_t": wt_t, "wo": wo, "wsr": np.asarray(L0_ffn_Ws),
              "small_in": small, "ident_in": np.eye(P, dtype=np.float32), "decay": dec, "experts": experts,
              "row_ids": row_ids, "pad_row": pad_row}
    arrays = {name: np.ascontiguousarray(a) for name, a in arrays.items()}
    nc = bacc.Bacc("TRN2", target_bir_lowering=False, num_devices=1)
    aps = [nc.dram_tensor(name, a.shape, mybir.dt.from_np(a.dtype), kind="ExternalInput").ap() for name, a in arrays.items()]
    out = nc.dram_tensor("out", (BATCH, SEQ, DIM), mybir.dt.float32, kind="ExternalOutput").ap()
    build(nc, *aps, out)
    r = run_bass_kernel_spmd(nc, [arrays], core_ids=[0])
    return r.results[0]["out"]
```

```python
from contextlib import ExitStack

import numpy as np

import concourse.bass as bass
from concourse import mybir

F32 = mybir.dt.float32
F32R = mybir.dt.float32r
BF16 = mybir.dt.bfloat16
I32 = mybir.dt.int32
U32 = mybir.dt.uint32
ALU = mybir.AluOpType
ACT = mybir.ActivationFunctionType
AX = mybir.AxisListType

P = 128
BATCH, SEQ, DIM, VOCAB, TAPS = 4, 1024, 128, 8000, 3
HEADS, DHEAD, FFN, EXPERTS = 8, 64, 512, 8
TPB = SEQ // P
TILES = BATCH * TPB
DECAY = float(np.exp(-1 / np.e))
PAIRS = HEADS // 2
NHEAD = BATCH * HEADS
NPAIR = NHEAD // 2
HALF = SEQ // 2
FC = FFN // P
EPS = 1e-5
SCALE = DHEAD ** -0.5
SLOT_TILES = (BATCH * SEQ + EXPERTS * (P - 1)) // P
TOKENS = BATCH * SEQ
REGION = TOKENS + P
ROW_H, ROW_P, ROW_ID, ROW = DIM, 2 * DIM, 2 * DIM + 1, 2 * DIM + 2
W_B1, W_W2, W_B2, W_END = FFN, FFN + FC, FFN + FC + FC * DIM, FFN + FC + FC * DIM + DIM


UNITS = 3 * TPB
RCPS = 4
BOTH = {("ksplit", 0): 11.5, ("qsplit", 0): 18.5, ("qsplit", 1): 21.0, ("ksplit", 1): 27.5, ("row", 0): 41.0, ("row", 1): 41.5,
        ("ocopy",): 70.1, ("sum",): 74.0, ("den",): 77.0, ("norm",): 91.0}
PAIR = {("k", 0): 7.2, ("q", 0): 12.2, ("q", 1): 14.2, ("k", 1): 15.7, ("v", 0): 39.0, ("v", 1): 43.0, ("vmove",): 49.2}
FIRST = {("k", 0): -9.0, ("q", 0): -8.0, ("ksplit", 0): -7.0, ("qsplit", 0): -6.0, ("q", 1): -5.0, ("k", 1): -4.0,
         ("qsplit", 1): 27.4, ("ksplit", 1): 30.8}
MAX_FIRST, MAX_SPAN, RCP_FIRST, RCP_STEP = 24.0, 14.0, 86.8, 1.0


def schedule():
    timed = []
    for n in range(NHEAD):
        for kt in range(TPB):
            for half in range(2):
                timed.append((UNITS * n + 3 * (kt - 1) + half, ("score", n, kt, half)))
            timed.append((UNITS * n + 3 * kt + 2, ("pv", n, kt)))
        start = UNITS * (n - 2)
        places = dict(BOTH)
        if n % 2 == 0:
            places.update(PAIR)
        if n == 0:
            places.update(FIRST)
        places.update({("max", j % TPB, j // TPB): MAX_FIRST + j * MAX_SPAN / (2 * TPB) for j in range(2 * TPB)})
        places.update({("rcp", r): RCP_FIRST + r * RCP_STEP for r in range(RCPS)})
        timed += [(start + x, (e[0], n, *e[1:])) for e, x in places.items()]
    timed.sort(key=lambda x: (x[0], x[1][0] not in ("score", "pv")))
    parts = [[] for _ in range(NHEAD + 2)]
    for x, e in timed:
        parts[min(max(int(x // UNITS) + 1, 0), NHEAD + 1)].append(e)
    return parts[0], parts[1:-1], parts[-1]


PROLOGUE, STAGES, EPILOGUE = schedule()
MISC = ("q", "k", "v", "max", "row", "den")
BANKS = 3
ACT_OPS = {"q": 1, "k": 1, "v": 2, "row": 1, "den": 1}
DVE_OPS = {"max": 1}
SPLITS = {("ksplit", 0): 1, ("qsplit", 0): 2, ("qsplit", 1): 3, ("ksplit", 1): 4}


def count_jobs():
    pe = act = dve = 0
    counts, bank, before, last = {}, {}, {}, {}
    for part in [PROLOGUE] + [STAGES[n] + STAGES[n + 1] for n in range(0, NHEAD, 2)] + [EPILOGUE]:
        jobs = [e for e in part if e[0] in MISC]
        for j, e in enumerate(jobs):
            pe, act, dve = pe + 1, act + ACT_OPS.get(e[0], 0), dve + DVE_OPS.get(e[0], 0)
            counts[e] = (pe, act, dve)
            bank[e] = j % BANKS
            if bank[e] in last:
                before[e] = last[bank[e]]
            last[bank[e]] = e
    return counts, bank, before


COUNTS, BANK, BEFORE = count_jobs()


def shifted(e, pairs):
    return (e[0], e[1] + 2 * pairs, *e[2:])


def at(i, pair, value):
    if isinstance(i, int):
        return value(i)
    step = value(pair + 1) - value(pair)
    return value(pair) + (i - pair) * step


def bcast(ap, axis, count):
    return ap.unsqueeze(axis).to_broadcast([*ap.shape[:axis], count, *ap.shape[axis:]])


class Core:
    pass


def build(nc, ids, table, wqk, wv, wt_t, wo, wsr, small, ident, inv_sums, experts, b_out, row_ids, pad_row, out):
    xd = nc.dram_tensor("sorted_rows", [(EXPERTS + 1) * REGION, ROW], F32, kind="Internal").ap()
    with ExitStack() as ctx:
        def sb(name, shape, dt=F32):
            return ctx.enter_context(nc.sbuf_tensor(name, shape, dt))

        c = Core()
        c.ident = sb("ident_f", [P, P])
        c.small = sb("small", [P, small.shape[1]])
        c.h = sb("h", [P, TILES, DIM])
        c.ov = sb("o_heads", [P, NPAIR, SEQ])
        c.wo1 = sb("w_out_softmax", [P, PAIRS, DIM])
        c.wsr = sb("w_router", [P, EXPERTS])
        phase_embed(nc, c, ctx, ids, table, wqk, wv, wt_t, wo, wsr, small, ident, inv_sums, b_out)
        phase_router(nc, c, wo, wsr, xd, experts, row_ids, pad_row, out)


SM_BS = 0
SM_PRIO = SM_BS + EXPERTS
SM_TILE = SM_PRIO + EXPERTS
SM_REGION = SM_TILE + SLOT_TILES
SM_END = SM_REGION + EXPERTS


def norm_stats(nc, dve, chain, src, st, mv, rs, var_ready):
    for t in range(TPB):
        nc.vector.bn_stats(st[:, t, :], src[:, t, :]).then_inc(chain.sem, 1)
    chain.add(TPB)
    dve.wait_ge(chain.sem, chain.n)
    for t in range(TPB):
        nc.vector.bn_aggr(mv[:, t, :], st[:, t, :]).then_inc(chain.sem, 1)
    chain.add(TPB)
    dve.wait_ge(chain.sem, chain.n)
    nc.vector.tensor_scalar(rs[:, 0, :], mv[:, :, 1], EPS, None, ALU.add).then_inc(var_ready, 1)


def norm_scale(nc, dve, chain, mv, rs, std_ready, b, scale_ready):
    dve.wait_ge(std_ready, b + 1)
    nc.vector.reciprocal(rs[:, 2, :], rs[:, 1, :]).then_inc(chain.sem, 1)
    chain.add(1)
    dve.wait_ge(chain.sem, chain.n)
    nc.vector.tensor_tensor(rs[:, 3, :], rs[:, 2, :], rs[:, 2, :], ALU.mult).then_inc(chain.sem, 1)
    chain.add(1)
    dve.wait_ge(chain.sem, chain.n)
    nc.vector.tensor_tensor(rs[:, 4, :], rs[:, 3, :], rs[:, 0, :], ALU.mult).then_inc(chain.sem, 1)
    chain.add(1)
    dve.wait_ge(chain.sem, chain.n)
    nc.vector.tensor_scalar(rs[:, 5, :], rs[:, 4, :], -0.5, 1.5, ALU.mult, ALU.add).then_inc(chain.sem, 1)
    chain.add(1)
    dve.wait_ge(chain.sem, chain.n)
    nc.vector.tensor_tensor(rs[:, 6, :], rs[:, 5, :], rs[:, 2, :], ALU.mult).then_inc(chain.sem, 1)
    chain.add(1)
    dve.wait_ge(chain.sem, chain.n)
    nc.vector.scalar_tensor_tensor(rs[:, 7, :], mv[:, :, 0], -1.0, rs[:, 6, :], ALU.mult, ALU.mult).then_inc(scale_ready, 1)


def norm_rows(nc, act, dst, src, rs, scale_ready, xn_ready, b, tiles=TPB):
    act.wait_ge(scale_ready, b + 1)
    for t in range(tiles):
        nc.scalar.activation(dst[:, t, :], src[:, t, :], ACT.Identity, bias=rs[:, 7, t:t + 1], scale=rs[:, 6, t:t + 1]).then_inc(xn_ready, 1)


class Count:

    def __init__(self, sem):
        self.sem, self.n = sem, 0

    def add(self, k):
        self.n += k


def phase_embed(nc, c, outer, ids, table, wqk, wv, wt_t, wo, wsr, small, ident, inv_sums, b_out):
    with ExitStack() as keep:
        def kb(name, shape, dt=F32):
            return keep.enter_context(nc.sbuf_tensor(name, shape, dt))

        c.xh = kb("x_hi", [P, BATCH * SEQ], F32R)
        c.xl = kb("x_lo", [P, BATCH * SEQ], F32R)
        c.whl = kb("w_hilo", [P, 2 * PAIRS, 2, 2 * DHEAD], F32R)
        c.wv = kb("w_v", [P, HEADS * DHEAD])
        c.wd = kb("w_pair", [P, 4, 2 * DHEAD], F32R)
        with ExitStack() as ctx:
            def sb(name, shape, dt=F32):
                return ctx.enter_context(nc.sbuf_tensor(name, shape, dt))

            def pb(name, shape):
                return ctx.enter_context(nc.psum_tensor(name, shape, F32))

            def sem(name):
                return ctx.enter_context(nc.semaphore(name))

            two = range(2)
            idx = sb("idx", [P, BATCH, TPB], I32)
            g = [sb(f"rows{p}", [P, TPB + 2, TAPS * DIM]) for p in two]
            wqk_s = sb("wqk_s", [P, 2 * PAIRS, 2 * DHEAD])
            wt_s = sb("wt_s", [P, PAIRS, DIM])
            wo2_s = sb("wo2_s", [P, PAIRS, DIM])
            inv_s = sb("inv_sums_s", [P, SEQ])
            rate = sb("rate", [P, SEQ])
            bout_s = sb("b_out_s", [P, DIM])
            m2 = sb("m2", [P, DIM])
            xn = sb("xn", [P, TPB, DIM])
            xf = sb("xf", [P, SEQ])
            xs = sb("x_scaled", [P, SEQ + 1])
            fwd = [sb(f"from_left{p}", [P, SEQ]) for p in two]
            bwd = [sb(f"from_right{p}", [P, SEQ]) for p in two]
            st = sb("st", [P, TPB, 6])
            mv = [sb(f"mv{p}", [P, TPB, 2]) for p in two]
            rs = [sb(f"rs{p}", [P, 8, TPB]) for p in two]
            ps_x = [pb(f"ps_x{p}", [P, SEQ]) for p in two]
            ps_o = [pb(f"ps_o{p}", [P, TPB, DIM]) for p in two]
            ps_m = ps_o[1][:, 0, :]

            wd_first = sem("wd_first")
            ids_in, w_in, edge_set = sem("ids_in"), sem("w_in"), sem("edge_set")
            ends_in, rows_in, edge_in = [sem("ends_in0"), sem("ends_in1")], [sem("rows_in0"), sem("rows_in1")], [sem("edge_in0"), sem("edge_in1")]
            scale_ready = sem("scale_ready")
            conv_done, var_ready, std_ready, xn_ready = sem("conv_done"), sem("var_ready"), sem("std_ready"), sem("xn_ready")
            xt_full, xh_ready, xl_done, x_read = sem("xt_full"), sem("xh_ready"), sem("xl_done"), sem("x_read")
            m2_full, m2_ready, scanned = sem("m2_full"), sem("m2_ready"), sem("scanned")
            bias_done, last_conv = sem("bias_done"), sem("last_conv")
            o_full, h_done, w_hi, rate_set = sem("o_full"), sem("h_done"), sem("w_hi"), sem("rate_set")
            chain = Count(sem("embed_chain"))

            with nc.Block() as block:
                @block.sync
                def _(sp):
                    sp.dma_start(idx[:], ids).then_inc(ids_in, 16)
                    for dst, src in ((c.small[:], small), (c.ident[:], ident), (inv_s[:], inv_sums), (wt_s[:], wt_t), (wo2_s[:], wo[:, 1]),
                                     (wqk_s[:], wqk), (c.wv[:], wv), (c.wo1[:], wo[:, 0]), (c.wsr[:], wsr), (bout_s[:], b_out)):
                        sp.dma_start(dst, src).then_inc(w_in, 16)
                    sp.wait_ge(w_hi, 2)
                    sp.dma_start(c.wd[:].bitcast(F32), c.whl[:, 0:2].rearrange("p a b c -> p (a b) c").bitcast(F32)).then_inc(wd_first, 16)
                    sp.wait_ge(edge_set, 4)
                    for b in range(BATCH):
                        gb = g[b % 2]
                        sp.wait_ge(ends_in[b % 2], 32 * (b // 2 + 1))
                        sp.dma_start(gb[1:P, 0, 0:DIM], gb[0:P - 1, TPB, 0:DIM]).then_inc(edge_in[b % 2], 16)
                        sp.dma_start(gb[0:P - 1, TPB + 1, 2 * DIM:3 * DIM], gb[1:P, 1, 2 * DIM:3 * DIM]).then_inc(edge_in[b % 2], 16)
                    sp.wait_ge(wd_first, 16)

                @block.gpsimd
                def _(pool):
                    pool.wait_ge(ids_in, 16)
                    for b in range(BATCH):
                        if b >= 2:
                            pool.wait_ge(conv_done, b - 1)
                        for t in (TPB - 1, *range(TPB - 1)):
                            nc.gpsimd.indirect_dma_start(
                                g[b % 2][:, t + 1, :], None, table,
                                bass.IndirectOffsetOnAxis(idx[:, b, t:t + 1].bitcast(U32), 0)).then_inc((ends_in if t in (0, TPB - 1) else rows_in)[b % 2], 16)
                    pool.wait_ge(w_in, 10 * 16)

                    def after_norm(b):
                        pool.wait_ge(xn_ready, TPB * (b + 1))
                        hb = c.h[:, b * TPB:(b + 1) * TPB, :]
                        nc.gpsimd.tensor_tensor(hb, hb, bcast(bout_s[:], 1, TPB), ALU.add).then_inc(bias_done, 1)
                        cols = slice(b * SEQ, (b + 1) * SEQ)
                        pool.wait_ge(xh_ready, 2 * b + 2)
                        nc.gpsimd.tensor_tensor(c.xl[:, cols], xf[:], c.xh[:, cols].bitcast(F32), ALU.subtract).then_inc(xl_done, 1)

                    after_norm(0)
                    b = BATCH - 1
                    gb, hb = g[b % 2], c.h[:, b * TPB:(b + 1) * TPB, :]
                    pool.wait_ge(ends_in[b % 2], 32 * (b // 2 + 1))
                    pool.wait_ge(rows_in[b % 2], 16 * (TPB - 2) * (b // 2 + 1))
                    pool.wait_ge(edge_in[b % 2], 32 * (b // 2 + 1))
                    nc.gpsimd.tensor_tensor(hb, gb[:, 0:TPB, 0:DIM], gb[:, 1:TPB + 1, DIM:2 * DIM], ALU.add).then_inc(last_conv, 1)
                    pool.wait_ge(last_conv, 1)
                    nc.gpsimd.tensor_tensor(hb, hb, gb[:, 2:TPB + 2, 2 * DIM:3 * DIM], ALU.add).then_inc(last_conv, 1)
                    for b in range(1, BATCH):
                        after_norm(b)

                @block.scalar
                def _(act):
                    act.wait_ge(m2_full, 1)
                    nc.scalar.activation(m2[:], ps_m, ACT.Copy).then_inc(m2_ready, 1)

                    def hi(b):
                        act.wait_ge(x_read, b + 1)
                        nc.scalar.activation(c.xh[:, b * SEQ:(b + 1) * SEQ], ps_x[b % 2][:], ACT.Copy).then_inc(xh_ready, 1)
                        if b >= 1:
                            act.wait_ge(xl_done, b)
                        nc.scalar.activation(xf[:], ps_x[b % 2][:], ACT.Copy).then_inc(xh_ready, 1)

                    for b in range(BATCH):
                        act.wait_ge(var_ready, b + 1)
                        nc.scalar.activation(rs[b % 2][:, 1, :], rs[b % 2][:, 0, :], ACT.Sqrt).then_inc(std_ready, 1)
                        if b >= 1:
                            act.wait_ge(xt_full, b)
                        norm_rows(nc, act, xn, c.h[:, b * TPB:(b + 1) * TPB, :], rs[b % 2], scale_ready, xn_ready, b)
                        if b >= 1:
                            hi(b - 1)
                    hi(BATCH - 1)

                @block.vector
                def _(dve):
                    def front(b):
                        gb = g[b % 2]
                        hb = c.h[:, b * TPB:(b + 1) * TPB, :]
                        if b < BATCH - 1:
                            dve.wait_ge(ends_in[b % 2], 32 * (b // 2 + 1))
                            dve.wait_ge(rows_in[b % 2], 16 * (TPB - 2) * (b // 2 + 1))
                            dve.wait_ge(edge_in[b % 2], 32 * (b // 2 + 1))
                            nc.vector.tensor_tensor(hb, gb[:, 0:TPB, 0:DIM], gb[:, 1:TPB + 1, DIM:2 * DIM], ALU.add).then_inc(chain.sem, 1)
                            chain.add(1)
                            dve.wait_ge(chain.sem, chain.n)
                            nc.vector.tensor_tensor(hb, hb, gb[:, 2:TPB + 2, 2 * DIM:3 * DIM], ALU.add).then_inc(conv_done, 1)
                            dve.wait_ge(conv_done, b + 1)
                        else:
                            dve.wait_ge(last_conv, 2)
                        if b >= 2:
                            dve.wait_ge(xn_ready, TPB * (b - 1))
                        norm_stats(nc, dve, chain, hb, st, mv[b % 2], rs[b % 2], var_ready)
                        norm_scale(nc, dve, chain, mv[b % 2], rs[b % 2], std_ready, b, scale_ready)

                    def parts(b):
                        p = b % 2
                        dve.wait_ge(xt_full, b + 1)
                        if b >= 1:
                            dve.wait_ge(scanned, 2 * b)
                        nc.vector.tensor_tensor(xs[:, 0:SEQ].rearrange("p (q t) -> p t q", t=TPB), ps_x[p][:].rearrange("p (t q) -> p t q", t=TPB),
                                                inv_s[:].rearrange("p (q t) -> p t q", t=TPB), ALU.mult).then_inc(x_read, 1)
                        dve.wait_ge(x_read, b + 1)
                        if b >= 2:
                            dve.wait_ge(o_full, b - 1)
                        nc.vector.tensor_tensor_scan(fwd[p][:], rate[:], xs[:, 0:SEQ], 0.0, ALU.mult, ALU.add).then_inc(scanned, 1)
                        nc.vector.tensor_tensor_scan(bwd[p][:, ::-1], xs[:, 1:SEQ + 1][:, ::-1], rate[:], 0.0, ALU.add, ALU.mult).then_inc(scanned, 1)

                    def add(b):
                        hb = c.h[:, b * TPB:(b + 1) * TPB, :]
                        dve.wait_ge(o_full, b + 1)
                        dve.wait_ge(bias_done, b + 1)
                        nc.vector.tensor_tensor(hb, hb, ps_o[b % 2][:], ALU.add).then_inc(h_done, 1)

                    for p in two:
                        nc.vector.memset(g[p][:, 0, 0:DIM], 0.0).then_inc(edge_set, 1)
                        nc.vector.memset(g[p][:, TPB + 1, 2 * DIM:3 * DIM], 0.0).then_inc(edge_set, 1)
                    nc.vector.memset(rate[:], DECAY).then_inc(rate_set, 1)
                    nc.vector.memset(xs[:, SEQ:SEQ + 1], 0.0).then_inc(rate_set, 1)
                    dve.wait_ge(rate_set, 2)
                    dve.wait_ge(w_in, 10 * 16)
                    nc.vector.tensor_copy(c.whl[:, :, 0, :], wqk_s[:]).then_inc(w_hi, 1)
                    dve.wait_ge(w_hi, 1)
                    nc.vector.tensor_tensor(c.whl[:, :, 1, :], wqk_s[:], c.whl[:, :, 0, :].bitcast(F32), ALU.subtract).then_inc(w_hi, 1)
                    front(0)
                    for b in range(BATCH):
                        if b + 1 < BATCH:
                            front(b + 1)
                        parts(b)
                        if b >= 1:
                            add(b - 1)
                    add(BATCH - 1)

                @block.tensor
                def _(pe):
                    pe.wait_ge(w_in, 10 * 16)
                    for k in range(PAIRS):
                        last = nc.tensor.matmul(ps_m, wt_s[:, k, :], wo2_s[:, k, :], start=(k == 0), stop=(k == PAIRS - 1))
                    last.then_inc(m2_full, 1)

                    def project(b):
                        pe.wait_ge(scanned, 2 * b + 2)
                        pe.wait_ge(m2_ready, 1)
                        if b >= 2:
                            pe.wait_ge(h_done, b - 1)
                        for t in range(TPB):
                            nc.tensor.matmul(ps_o[b % 2][:, t, :], fwd[b % 2][:, t::TPB], m2[:], start=True, stop=False)
                            last = nc.tensor.matmul(ps_o[b % 2][:, t, :], bwd[b % 2][:, t::TPB], m2[:], start=False, stop=True)
                        last.then_inc(o_full, 1)

                    for b in range(BATCH):
                        if b >= 2:
                            pe.wait_ge(xh_ready, 2 * (b - 1))
                        for t in range(TPB):
                            pe.wait_ge(xn_ready, b * TPB + t + 1)
                            last = nc.tensor.transpose(ps_x[b % 2][:, t * P:(t + 1) * P], xn[:, t, :], c.ident[:])
                        last.then_inc(xt_full, 1)
                        if b >= 1:
                            project(b - 1)
                    project(BATCH - 1)
        c.s_ps = [outer.enter_context(nc.psum_tensor(f"scores{p}", [P, SEQ], F32)) for p in range(2)]
        phase_attention(nc, c)


def out_project(nc, c, b, tiles):
    for t in tiles:
        for k in range(PAIRS):
            last = nc.tensor.matmul(c.s_ps[b % 2][:, t * DIM:(t + 1) * DIM], c.ov[:, b * PAIRS + k, t * P:(t + 1) * P], c.wo1[:, k, :],
                                    start=(k == 0), stop=(k == PAIRS - 1))
    return last


def phase_attention(nc, c):
    with ExitStack() as ctx:
        def sb(name, shape, dt=F32):
            return ctx.enter_context(nc.sbuf_tensor(name, shape, dt))

        def pb(name, shape):
            return ctx.enter_context(nc.psum_tensor(name, shape, F32))

        def sem(name):
            return ctx.enter_context(nc.semaphore(name))

        two = range(2)
        qs = sb("q_pair", [P, SEQ])
        ks = sb("k_pair", [P, SEQ])
        qa = [sb(f"qa{p}", [P, SEQ], F32R) for p in two]
        qb = [sb(f"qb{p}", [P, SEQ], F32R) for p in two]
        ka = [sb(f"ka{p}", [P, SEQ], F32R) for p in two]
        kb = [sb(f"kb{p}", [P, SEQ], F32R) for p in two]
        own = [slice(0, DHEAD), slice(DHEAD, P)]
        other = [slice(DHEAD, P), slice(0, DHEAD)]
        mrows = [slice(DHEAD, DHEAD + 2), slice(0, 2)]
        kk = [slice(0, DHEAD + 2), slice(0, P)]
        wd = c.wd
        xfs = sb("xfs", [P, SEQ])
        vb = [sb(f"vb{p}", [P, TPB, DHEAD]) for p in two]
        vnext = sb("v_next", [P, TPB, DHEAD])
        RING = 4
        pr = sb("probs", [P, RING, SEQ])
        ps = [sb(f"psum_keys{p}", [P, SEQ]) for p in two]
        dn = sb("den", [P, HALF])
        oc = [sb(f"o_out{p}", [P, HALF]) for p in two]
        mx2 = sb("mx2", [P, TPB, 2])
        mx = sb("mx", [P, TPB])
        nm = sb("nm", [P, TPB, 2], BF16)
        idb = sb("ident_b", [P, P], BF16)
        ones = sb("ones_v", [P, DHEAD])
        s_ps = c.s_ps
        o_ps = pb("values", [P, HALF])
        m_ps = [pb(f"misc{m}", [P, HALF]) for m in range(BANKS)]

        init, kb_ones, kb_rows = sem("attn_init"), sem("kb_ones"), sem("kb_rows")
        wd_in = sem("wd_in")
        hi_done, lo_done, v_moved = sem("hi_done"), sem("lo_done"), sem("v_moved")
        misc_full, act_misc, dve_misc = sem("misc_full"), sem("act_misc"), sem("dve_misc")
        s_full, exp_done, pv_done = sem("scores_full"), sem("exp_done"), sem("pv_done")
        key_sums, all_sums, xf_set = sem("key_sums"), sem("all_sums"), sem("xf_set")
        o_copied, rd_done = sem("o_copied"), sem("rd_done")
        nm_chain, nm_set, norm_done = sem("nm_chain"), sem("nm_set"), sem("norm_done")
        o_out = [sem("o_out0"), sem("o_out1")]

        def each(eng, handle):
            for e in PROLOGUE:
                handle(eng, e, 0, 0)
            for e in STAGES[0] + STAGES[1]:
                handle(eng, e, 0, 0)
            with eng.Fori(1, NPAIR - 1) as i:
                for e in STAGES[2] + STAGES[3]:
                    handle(eng, e, i, 1)
            for e in STAGES[NHEAD - 2] + STAGES[NHEAD - 1] + EPILOGUE:
                handle(eng, e, NPAIR - 1, NPAIR - 1)

        def of(e, i, pair, which):
            return at(i, pair, lambda x: COUNTS[shifted(e, x - pair)][which])

        def num(i, pair, n, per_head, offset):
            return per_head * n + offset + (i - pair) * (2 * per_head)

        def pair_no(i, pair, m):
            return m // 2 if isinstance(i, int) else i + (m // 2 - pair)

        def batch_cols(i, pair, m, part, size):
            off = pair_no(i, pair, m) // PAIRS * SEQ + part * size
            return slice(off, off + size) if isinstance(off, int) else bass.ds(off, size)

        with nc.Block() as block:
            @block.sync
            def _(sp):
                def load_w(m, i, pair):
                    u = pair_no(i, pair, m) % PAIRS * 2
                    src = c.whl[:, slice(u, u + 2) if isinstance(u, int) else bass.ds(u, 2)]
                    sp.dma_start(wd[:].bitcast(F32), src.rearrange("p a b c -> p (a b) c").bitcast(F32)).then_inc(wd_in, 16)

                def store(n, i, pair):
                    p = n % 2
                    sp.wait_ge(norm_done, num(i, pair, n, 1, 1))
                    u = n // 2 + (i - pair)
                    for half in two:
                        dst = c.ov[p * DHEAD:(p + 1) * DHEAD, bass.ds(u, 1) if not isinstance(u, int) else slice(u, u + 1),
                                   half * HALF:(half + 1) * HALF]
                        sp.dma_start(dst.rearrange("p a b -> p (a b)"), oc[p][half * DHEAD:(half + 1) * DHEAD, :]).then_inc(o_out[p], 16)

                def run(i, pair, first=False, last=False):
                    for n in (2 * pair, 2 * pair + 1):
                        if n % 2 == 0 and n + 2 < NHEAD:
                            sp.wait_ge(misc_full, of(("k", n, 1), i, pair, 0))
                            load_w(n + 2, i, pair)
                        if not (first and n == 0):
                            store(n - 1, i, pair)
                    if last:
                        store(NHEAD - 1, i, pair)

                run(0, 0, first=True)
                with sp.Fori(1, NPAIR - 1) as i:
                    run(i, 1)
                run(NPAIR - 1, NPAIR - 1, last=True)
                for p in two:
                    sp.wait_ge(o_out[p], 32 * NPAIR)

            @block.gpsimd
            def _(pool):
                nc.gpsimd.memset(ones[:], 1.0).then_inc(init, 1)
                nc.gpsimd.tensor_copy(idb[:], c.ident[:]).then_inc(init, 1)

                def set_x(m, i, pair):
                    if m > 0:
                        pool.wait_ge(misc_full, of(("v", m - 2, 1), i, pair, 0))
                    cols = batch_cols(i, pair, m, 0, SEQ)
                    nc.gpsimd.tensor_tensor(xfs[:], c.xh[:, cols].bitcast(F32), c.xl[:, cols].bitcast(F32), ALU.add).then_inc(xf_set, 1)

                pool.wait_ge(init, 2)
                set_x(0, 0, 0)
                nc.gpsimd.memset(kb[1][0:DHEAD, :].bitcast(F32), 0.0).then_inc(kb_rows, 1)
                nc.gpsimd.memset(qb[1][0:DHEAD, :].bitcast(F32), 0.0).then_inc(kb_rows, 1)
                pool.wait_ge(kb_rows, 2)
                nc.gpsimd.memset(kb[1][0:2, :].bitcast(F32), 1.0).then_inc(kb_rows, 1)

                def run(i, pair):
                    for n in (2 * pair, 2 * pair + 1):
                        p = n % 2
                        for kt in range(1, TPB - 1):
                            pool.wait_ge(exp_done, num(i, pair, n, TPB, kt + 1))
                            if kt == 1:
                                if n >= 2:
                                    pool.wait_ge(misc_full, of(("den", n - 2), i, pair, 0))
                                a = pr[:, 0, :]
                            else:
                                pool.wait_ge(key_sums, num(i, pair, n, TPB - 2, kt - 1))
                                a = ps[p][:]
                            nc.gpsimd.tensor_tensor(ps[p][:], a, pr[:, kt % RING, :], ALU.add).then_inc(key_sums, 1)
                            if kt == 1 and p == 1 and n + 1 < NHEAD:
                                set_x(n + 1, i, pair)

                run(0, 0)
                with pool.Fori(1, NPAIR - 1) as i:
                    run(i, 1)
                run(NPAIR - 1, NPAIR - 1)

            @block.scalar
            def _(act):
                def exp(n, kt, i, pair):
                    act.wait_ge(s_full, num(i, pair, n, TPB, kt + 1))
                    idx = n * TPB + kt
                    if idx >= RING:
                        act.wait_ge(pv_done, num(i, pair, n, TPB, kt + 1 - RING))
                        r, adds = kt - RING, TPB - 2
                        if kt < RING - 1:
                            act.wait_ge(key_sums, num(i, pair, n - 1, adds, kt + RING))
                        elif kt < RING:
                            act.wait_ge(all_sums, num(i, pair, n - 1, 1, 1))
                        else:
                            act.wait_ge(key_sums, num(i, pair, n, adds, max(r, 1)))
                    nc.scalar.activation(pr[:, kt % RING, :], s_ps[kt % 2][:], ACT.Exp, scale=SCALE).then_inc(exp_done, 1)

                def handle(act, e, i, pair):
                    kind, m = e[0], e[1]
                    p = m % 2
                    if kind == "score":
                        if e[3] == 1:
                            exp(m, e[2], i, pair)
                        return
                    if kind == "ocopy":
                        act.wait_ge(pv_done, num(i, pair, m, TPB, TPB))
                        if m >= 2:
                            act.wait_ge(o_out[p], num(i, pair, m, 16, 0) - 16 * p)
                        nc.scalar.activation(oc[p][:], o_ps[:], ACT.Copy).then_inc(o_copied, 1)
                        return
                    if kind in ("qsplit", "ksplit"):
                        half = slice(e[2] * HALF, (e[2] + 1) * HALF)
                        act.wait_ge(act_misc, of((kind[0], m // 2 * 2, e[2]), i, pair, 1))
                        if m >= 2:
                            act.wait_ge(s_full, num(i, pair, m - 2, TPB, TPB // 2 if (kind, e[2]) == ("ksplit", 0) else TPB))
                        src = (qs if kind == "qsplit" else ks)[own[p], half]
                        second = qb[p][own[p], half] if kind == "qsplit" else ka[p][other[p], half]
                        nc.scalar.activation((qa if kind == "qsplit" else ka)[p][own[p], half], src, ACT.Copy).then_inc(hi_done, 1)
                        nc.scalar.activation(second, src, ACT.Copy).then_inc(hi_done, 1)
                        return
                    if kind == "vmove":
                        act.wait_ge(act_misc, of(("v", m, 1), i, pair, 1))
                        if m > 0:
                            act.wait_ge(pv_done, num(i, pair, m - 1, TPB, TPB))
                        nc.scalar.activation(vb[1][:], vnext[:], ACT.Copy).then_inc(v_moved, 1)
                        return
                    if kind not in ACT_OPS:
                        return
                    bank = m_ps[BANK[e]]
                    act.wait_ge(misc_full, of(e, i, pair, 0))
                    half = slice(e[2] * HALF, (e[2] + 1) * HALF) if len(e) > 2 else None
                    if kind in "qk":
                        if m > 0:
                            act.wait_ge(lo_done, num(i, pair, m - 1, 4, SPLITS[kind + "split", e[2]]))
                        nc.scalar.activation((qs if kind == "q" else ks)[:, half], bank[:], ACT.Copy).then_inc(act_misc, 1)
                    elif kind == "v":
                        if m > 0:
                            act.wait_ge(v_moved, pair_no(i, pair, m))
                        src = bank[:].rearrange("p (a b c) -> p a b c", b=2, c=DHEAD)
                        tiles = slice(e[2] * TPB // 2, (e[2] + 1) * TPB // 2)
                        nc.scalar.activation(vb[0][:, tiles, :], src[:, :, 0, :], ACT.Copy).then_inc(act_misc, 1)
                        nc.scalar.activation(vnext[:, tiles, :], src[:, :, 1, :], ACT.Copy).then_inc(act_misc, 1)
                    elif kind == "den":
                        if m > 0:
                            act.wait_ge(norm_done, num(i, pair, m, 1, 0))
                        nc.scalar.activation(dn[:], bank[:], ACT.Copy).then_inc(act_misc, 1)
                    else:
                        nc.scalar.activation(qb[p][mrows[p], half], bank[mrows[p], :], ACT.Copy).then_inc(act_misc, 1)

                each(act, handle)

            @block.vector
            def _(dve):
                def handle(dve, e, i, pair):
                    kind, m = e[0], e[1]
                    p = m % 2
                    if kind == "sum":
                        dve.wait_ge(exp_done, num(i, pair, m, TPB, TPB))
                        dve.wait_ge(key_sums, num(i, pair, m, TPB - 2, TPB - 2))
                        nc.vector.tensor_tensor(ps[p][:], ps[p][:], pr[:, (TPB - 1) % RING, :], ALU.add).then_inc(all_sums, 1)
                        return
                    if kind == "rcp":
                        if e[2] == 0:
                            dve.wait_ge(act_misc, of(("den", m), i, pair, 1))
                        cols = slice(e[2] * HALF // RCPS, (e[2] + 1) * HALF // RCPS)
                        nc.vector.reciprocal(dn[:, cols], dn[:, cols]).then_inc(rd_done, 1)
                        return
                    if kind == "norm":
                        dve.wait_ge(rd_done, num(i, pair, m, RCPS, RCPS))
                        dve.wait_ge(o_copied, num(i, pair, m, 1, 1))
                        nc.vector.tensor_tensor(oc[p][:], oc[p][:], dn[:], ALU.mult).then_inc(norm_done, 1)
                        return
                    if kind in ("qsplit", "ksplit"):
                        half = slice(e[2] * HALF, (e[2] + 1) * HALF)
                        dve.wait_ge(hi_done, num(i, pair, m, 8, 2 * SPLITS[kind, e[2]]))
                        if kind == "qsplit":
                            nc.vector.tensor_tensor(qa[p][other[p], half], qs[own[p], half], qa[p][own[p], half].bitcast(F32),
                                                    ALU.subtract).then_inc(lo_done, 1)
                        else:
                            nc.vector.tensor_tensor(kb[p][own[p], half], ks[own[p], half], ka[p][own[p], half].bitcast(F32),
                                                    ALU.subtract).then_inc(lo_done, 1)
                        return
                    if kind not in DVE_OPS:
                        return
                    bank = m_ps[BANK[e]]
                    dve.wait_ge(misc_full, of(e, i, pair, 0))
                    if kind == "max":
                        t, half = e[2], e[3]
                        if t == 0 and half == 0 and m > 0:
                            dve.wait_ge(nm_chain, num(i, pair, m - 1, 2, 2))
                        nc.vector.tensor_reduce(mx2[:, t, half:half + 1], bank[:], AX.X, ALU.max).then_inc(dve_misc, 1)
                        if (t, half) == (TPB - 1, 1):
                            dve.wait_ge(dve_misc, of(e, i, pair, 2))
                            if m > 0:
                                dve.wait_ge(nm_set, num(i, pair, m - 1, 1, 1))
                            nc.vector.tensor_reduce(mx[:], mx2[:], AX.X, ALU.max).then_inc(nm_chain, 1)
                            dve.wait_ge(nm_chain, num(i, pair, m, 2, 1))
                            if m > 0:
                                dve.wait_ge(misc_full, of(("row", m - 1, 1), i, pair, 0))
                            nc.vector.tensor_scalar(nm[:, :, 0], mx[:], -1.0, None, ALU.mult).then_inc(nm_chain, 1)
                            dve.wait_ge(nm_chain, num(i, pair, m, 2, 2))
                            nc.vector.scalar_tensor_tensor(nm[:, :, 1], mx[:], -1.0, nm[:, :, 0], ALU.mult, ALU.subtract).then_inc(nm_set, 1)

                nc.vector.memset(kb[0][DHEAD:P, :].bitcast(F32), 1.0).then_inc(kb_ones, 1)
                each(dve, handle)

            @block.tensor
            def _(pe):
                pe.wait_ge(init, 2)

                def handle(pe, e, i, pair):
                    kind, m = e[0], e[1]
                    p = m % 2
                    if kind == "score":
                        kt = e[2]
                        idx = m * TPB + kt
                        half = e[3]
                        if idx == 0 and half == 0:
                            pe.wait_ge(kb_ones, 1)
                            pe.wait_ge(kb_rows, 3)
                        if kt == 0 and half == 0:
                            pe.wait_ge(act_misc, of(("row", m, 1), i, pair, 1))
                            pe.wait_ge(lo_done, num(i, pair, m, 4, 4))
                        if idx >= 2 and half == 0:
                            pe.wait_ge(exp_done, num(i, pair, m, TPB, kt - 1))
                        keys = slice(kt * P, (kt + 1) * P)
                        cols = slice(half * HALF, (half + 1) * HALF)
                        dst = s_ps[kt % 2][:, cols]
                        nc.tensor.matmul(dst, ka[p][:, keys], qa[p][:, cols], start=True, stop=False)
                        last = nc.tensor.matmul(dst, kb[p][kk[p], keys], qb[p][kk[p], cols], start=False, stop=True)
                        if half == 1:
                            last.then_inc(s_full, 1)
                        return
                    if kind == "pv":
                        kt = e[2]
                        pe.wait_ge(exp_done, num(i, pair, m, TPB, kt + 1))
                        if kt == 0:
                            if p == 0:
                                pe.wait_ge(act_misc, of(("v", m, 1), i, pair, 1))
                            else:
                                pe.wait_ge(v_moved, pair_no(i, pair, m) + 1)
                            if m > 0:
                                pe.wait_ge(o_copied, num(i, pair, m, 1, 0))
                        for half in two:
                            last = nc.tensor.matmul(o_ps[half * DHEAD:(half + 1) * DHEAD, :], vb[p][:, kt, :],
                                                    pr[:, kt % RING, half * HALF:(half + 1) * HALF],
                                                    start=(kt == 0), stop=(kt == TPB - 1))
                        last.then_inc(pv_done, 1)
                        return
                    if kind not in MISC:
                        return
                    bank = m_ps[BANK[e]]
                    if e in BEFORE:
                        before = BEFORE[e]
                        if before[0] in ACT_OPS:
                            pe.wait_ge(act_misc, of(before, i, pair, 1))
                        if before[0] in DVE_OPS:
                            pe.wait_ge(dve_misc, of(before, i, pair, 2))
                    if kind in "qk":
                        if e[2] == 0 and kind == "k":
                            if m > 0:
                                pe.wait_ge(wd_in, pair_no(i, pair, m) * 16)
                        hi, lo = (wd[:, 0, :], wd[:, 1, :]) if kind == "q" else (wd[:, 2, :], wd[:, 3, :])
                        cols = batch_cols(i, pair, m, e[2], HALF)
                        nc.tensor.matmul(bank[:], hi, c.xh[:, cols], start=True, stop=False)
                        nc.tensor.matmul(bank[:], lo, c.xh[:, cols], start=False, stop=False)
                        last = nc.tensor.matmul(bank[:], hi, c.xl[:, cols], start=False, stop=True)
                    elif kind == "v":
                        pe.wait_ge(xf_set, pair_no(i, pair, m) + 1)
                        off = pair_no(i, pair, m) % PAIRS * 2 * DHEAD
                        cols = slice(off, off + 2 * DHEAD) if isinstance(off, int) else bass.ds(off, 2 * DHEAD)
                        for t in range(TPB // 2):
                            kt = e[2] * TPB // 2 + t
                            last = nc.tensor.matmul(bank[:, t * P:(t + 1) * P], xfs[:, kt * P:(kt + 1) * P], c.wv[:, cols],
                                                    start=True, stop=True)
                    elif kind == "max":
                        t, half = e[2], e[3]
                        if t == 0:
                            pe.wait_ge(hi_done, num(i, pair, m, 8, 2 * SPLITS["ksplit", half]))
                        if half == 0 and t % (TPB // 2) == 0:
                            pe.wait_ge(lo_done, num(i, pair, m, 4, SPLITS["qsplit", t // (TPB // 2)]))
                        last = nc.tensor.matmul(bank[:], qa[p][:, t * P:(t + 1) * P], ka[p][:, half * HALF:(half + 1) * HALF],
                                                start=True, stop=True)
                    elif kind == "row":
                        pe.wait_ge(nm_set, num(i, pair, m, 1, 1))
                        for t in range(TPB // 2):
                            last = nc.tensor.matmul(bank[mrows[p], t * P:(t + 1) * P], nm[:, e[2] * TPB // 2 + t, :], idb[:],
                                                    start=True, stop=True)
                    else:
                        if m == NHEAD - 1:
                            pe.wait_ge(exp_done, TPB * NHEAD)
                            for q in two:
                                pe.wait_ge(o_out[q], 32 * PAIRS)
                            out_project(nc, c, 0, range(TPB // 2))
                        pe.wait_ge(all_sums, num(i, pair, m, 1, 1))
                        for half in two:
                            last = nc.tensor.matmul(bank[half * DHEAD:(half + 1) * DHEAD, :], ones[:], ps[p][:, half * HALF:(half + 1) * HALF],
                                                    start=True, stop=True)
                    last.then_inc(misc_full, 1)

                each(pe, handle)
                out_project(nc, c, 0, range(TPB // 2, TPB))
                for q in two:
                    pe.wait_ge(o_out[q], 32 * 2 * PAIRS)
                out_project(nc, c, 1, range(TPB))


def phase_router(nc, c, wo, wsr, xd, experts, row_ids, pad_row, out):
    with ExitStack() as ctx:
        def sb(name, shape, dt=F32):
            return ctx.enter_context(nc.sbuf_tensor(name, shape, dt))

        ew = sb("expert_weights", [P, EXPERTS, W_END])
        te = sb("tile_expert", [P, SLOT_TILES], I32)
        first_row = sb("tile_first_row", [P, SLOT_TILES], I32)
        with ExitStack() as inner:
            def isb(name, shape, dt=F32):
                return inner.enter_context(nc.sbuf_tensor(name, shape, dt))

            def ipb(name, shape, dt=F32):
                return inner.enter_context(nc.psum_tensor(name, shape, dt))

            def isem(name):
                return inner.enter_context(nc.semaphore(name))

            two, ACT_TILES = range(2), 4
            rows = isb("token_rows", [P, TILES, ROW])
            pad = isb("pad_row_s", [P, ROW])
            ids_s = isb("row_ids_s", [P, TILES], I32)
            slot = isb("slot", [P, TILES], I32)
            pad_first = isb("pad_first", [P, EXPERTS], I32)
            xt = [isb(f"xt{p}", [P, SEQ]) for p in two]
            st = isb("st2", [P, TPB, 6])
            mv = [isb(f"mv2{p}", [P, TPB, 2]) for p in two]
            rs = [isb(f"rs2{p}", [P, 8, TPB]) for p in two]
            lg = isb("logits", [P, TPB, EXPERTS])
            lm = [isb(f"logits_less_max{p}", [P, TPB, EXPERTS]) for p in two]
            ex = [isb(f"ex{p}", [P, TPB, EXPERTS]) for p in two]
            pri = isb("prio", [P, TPB, EXPERTS])
            ohb = [isb(f"onehot_b{p}", [P, TPB, EXPERTS], BF16) for p in two]
            t1 = isb("t1", [P, TPB])
            first = [isb(f"first{p}", [P, TPB]) for p in two]
            z = isb("z", [P, TPB])
            mine = isb("mine", [P, BATCH, EXPERTS])
            acc = isb("acc", [P, BATCH, EXPERTS], BF16)
            slf = isb("slf", [P, TPB, EXPERTS])
            cnt = isb("cnt", [P, EXPERTS])
            ntile = isb("ntile", [P, EXPERTS])
            nti = isb("nti", [P, EXPERTS], I32)
            be = [isb(f"be{p}", [P, 2 * EXPERTS]) for p in two]
            base = isb("base", [P, EXPERTS])
            cmp = isb("cmp", [P, SLOT_TILES, EXPERTS])
            tef = isb("tef", [P, SLOT_TILES])
            tbase = isb("tbase", [P, SLOT_TILES])
            up = isb("upper", [P, P], BF16)
            on = isb("ones_b", [P, P], BF16)
            ps_a = [c.s_ps[p][:].rearrange("p (t d) -> p t d", d=DIM) for p in two]
            ps_x = ipb("ps_x2", [P, SEQ])
            ps_l = ipb("ps_l", [P, TPB, EXPERTS])
            ps_r = ipb("ps_r", [P, 3, TPB * EXPERTS])

            w_in, a_full, h_done = isem("w2_in"), isem("a_full"), isem("h2_done")
            scale_ready, xn_dve = isem("scale2_ready"), isem("xn2_dve")
            var_ready, std_ready, xn_ready = isem("var2_ready"), isem("std2_ready"), isem("xn2_ready")
            xt_full, xt_ready, l_full, l_done = isem("xt2_full"), isem("xt2_ready"), isem("l_full"), isem("l_done")
            ex_in, ex_done, oh_done, r_full, consts = isem("ex_in"), isem("ex_done"), isem("oh_done"), isem("r_full"), isem("consts")
            acc_done, slot_done, pad_ready, scattered, ew_in = isem("acc_done"), isem("slot_done"), isem("pad_ready"), isem("scattered"), isem("ew_in")
            pad_out, slots_read = isem("pad_out"), isem("slots_read")
            chain = Count(isem("router_chain"))

            with nc.Block() as block:
                @block.sync
                def _(sp):
                    for dst, src in ((ids_s[:], row_ids), (pad[:], pad_row)):
                        sp.dma_start(dst, src).then_inc(w_in, 16)
                    for e in range(EXPERTS):
                        sp.dma_start(ew[:, e, :], experts[e]).then_inc(ew_in, 16)
                    sp.wait_ge(w_in, 32)
                    sp.dma_start(xd[0:P, :], pad[:]).then_inc(pad_out, 16)
                    sp.wait_ge(ew_in, 16 * EXPERTS)
                    sp.wait_ge(pad_ready, 1)
                    for e in range(EXPERTS):
                        row = sp.value_load(pad_first[0:1, e:e + 1], min_val=(EXPERTS - e) * REGION, max_val=(EXPERTS - e) * REGION + TOKENS)
                        sp.dma_start(xd[bass.ds(row, P), :], pad[:]).then_inc(pad_out, 16)
                    sp.wait_ge(pad_out, 16 * (EXPERTS + 1))

                @block.gpsimd
                def _(pool):
                    nc.gpsimd.memset(on[:], 1.0).then_inc(consts, 1)
                    for p in two:
                        nc.gpsimd.memset(be[p][:, 0:EXPERTS], 0.0).then_inc(consts, 1)
                    pool.wait_ge(consts, 3)
                    nc.gpsimd.affine_select(out=up[:], in_=on[:], compare_op=ALU.is_gt, fill=0.0, base=0,
                                            pattern=[[1, P]], channel_multiplier=-1).then_inc(consts, 1)
                    pool.wait_ge(w_in, 32)
                    for b in range(BATCH):
                        pool.wait_ge(slot_done, b + 1)
                        pool.wait_ge(xn_ready, ACT_TILES * (b + 1))
                        pool.wait_ge(xn_dve, (TPB - ACT_TILES) * (b + 1))
                        for t in range(b * TPB, (b + 1) * TPB):
                            nc.gpsimd.indirect_dma_start(xd, bass.IndirectOffsetOnAxis(slot[:, t:t + 1].bitcast(U32), 0),
                                                         rows[:, t, :], None).then_inc(scattered, 16)
                    pool.wait_ge(scattered, 16 * TILES)

                @block.scalar
                def _(act):
                    def root(b):
                        act.wait_ge(var_ready, b + 1)
                        nc.scalar.activation(rs[b % 2][:, 1, :], rs[b % 2][:, 0, :], ACT.Sqrt).then_inc(std_ready, 1)

                    def norm(b):
                        tiles = slice(b * TPB, (b + 1) * TPB)
                        norm_rows(nc, act, rows[:, tiles, 0:DIM], rows[:, tiles, ROW_H:ROW_H + DIM], rs[b % 2], scale_ready, xn_ready, b, ACT_TILES)

                    root(0)
                    norm(0)
                    for b in range(BATCH):
                        act.wait_ge(xt_full, b + 1)
                        if b >= 2:
                            act.wait_ge(l_full, b - 1)
                        nc.scalar.activation(xt[b % 2][:], ps_x[:], ACT.Copy).then_inc(xt_ready, 1)
                        if b + 1 < BATCH:
                            root(b + 1)
                        act.wait_ge(ex_in, b + 1)
                        nc.scalar.activation(ex[b % 2][:], lm[b % 2][:], ACT.Exp).then_inc(ex_done, 1)
                        if b + 1 < BATCH:
                            norm(b + 1)

                @block.tensor
                def _(pe):
                    def ranks(b):
                        pe.wait_ge(oh_done, b + 1)
                        if b >= 1:
                            pe.wait_ge(acc_done, b)
                        if b >= 1:
                            pe.wait_ge(slot_done, b)
                        dst, one = ps_r[:, b % 2, :], ohb[b % 2]
                        last = nc.tensor.matmul(dst, up[:], one[:].rearrange("p a b -> p (a b)"), start=True, stop=False)
                        for d in range(1, TPB):
                            last = nc.tensor.matmul(dst[:, d * EXPERTS:], on[:], one[:, 0:TPB - d, :].rearrange("p a b -> p (a b)"),
                                                    start=False, stop=(b == 0 and d == TPB - 1))
                        if b > 0:
                            for t in range(TPB):
                                last = nc.tensor.matmul(dst[:, t * EXPERTS:(t + 1) * EXPERTS], on[:], acc[:, b - 1, :],
                                                        start=False, stop=(t == TPB - 1))
                        last.then_inc(r_full, 1)

                    pe.wait_ge(consts, 4)
                    for b in range(BATCH):
                        if b + 2 < BATCH:
                            pe.wait_ge(h_done, b + 1)
                            out_project(nc, c, b + 2, range(TPB // 2))
                        if b >= 1:
                            pe.wait_ge(xt_ready, b)
                        for t in range(TPB):
                            if t < ACT_TILES:
                                pe.wait_ge(xn_ready, b * ACT_TILES + t + 1)
                            else:
                                pe.wait_ge(xn_dve, b * (TPB - ACT_TILES) + t - ACT_TILES + 1)
                            last = nc.tensor.transpose(ps_x[:, t * P:(t + 1) * P], rows[:, b * TPB + t, 0:DIM], c.ident[:])
                        last.then_inc(xt_full, 1)
                        if b + 2 < BATCH:
                            out_project(nc, c, b + 2, range(TPB // 2, TPB)).then_inc(a_full, 1)
                        pe.wait_ge(xt_ready, b + 1)
                        if b >= 1:
                            pe.wait_ge(l_done, b)
                        for t in range(TPB):
                            last = nc.tensor.matmul(ps_l[:, t, :], xt[b % 2][:, t * P:(t + 1) * P], c.wsr[:], start=True, stop=True)
                        last.then_inc(l_full, 1)
                        ranks(b)
                    pe.wait_ge(acc_done, BATCH)
                    pe.wait_ge(slot_done, BATCH)
                    nc.tensor.matmul(ps_r[:, 2, 0:EXPERTS], on[:], acc[:, BATCH - 1, :], start=True, stop=True).then_inc(r_full, 1)

                @block.vector
                def _(dve):
                    def link(ins):
                        ins.then_inc(chain.sem, 1)
                        chain.add(1)
                        dve.wait_ge(chain.sem, chain.n)

                    def tiles_of(b):
                        return slice(b * TPB, (b + 1) * TPB)

                    def front(b):
                        if b >= 2:
                            dve.wait_ge(a_full, b - 1)
                        nc.vector.tensor_tensor(rows[:, tiles_of(b), ROW_H:ROW_H + DIM], c.h[:, tiles_of(b), :], ps_a[b % 2], ALU.add).then_inc(h_done, 1)
                        dve.wait_ge(h_done, b + 1)
                        if b >= 2:
                            dve.wait_ge(xn_ready, ACT_TILES * (b - 1))
                        norm_stats(nc, dve, chain, rows[:, tiles_of(b), ROW_H:ROW_H + DIM], st, mv[b % 2], rs[b % 2], var_ready)

                    def norm(b):
                        norm_scale(nc, dve, chain, mv[b % 2], rs[b % 2], std_ready, b, scale_ready)
                        dve.wait_ge(scale_ready, b + 1)
                        for t in range(ACT_TILES, TPB):
                            u = b * TPB + t
                            nc.vector.tensor_scalar(rows[:, u, 0:DIM], rows[:, u, ROW_H:ROW_H + DIM], rs[b % 2][:, 6, t:t + 1], rs[b % 2][:, 7, t:t + 1],
                                                    ALU.mult, ALU.add).then_inc(xn_dve, 1)

                    def over_e(ap, n=TPB):
                        return ap.unsqueeze(2).to_broadcast([P, n, EXPERTS])

                    def over_t(ap, n=TPB):
                        return bcast(ap, 1, n)

                    def const(at, n=EXPERTS):
                        return c.small[:, at:at + n]

                    def choose(b):
                        p = b % 2
                        dve.wait_ge(l_full, b + 1)
                        nc.vector.tensor_tensor(lg[:], ps_l[:], over_t(const(SM_BS)), ALU.add).then_inc(l_done, 1)
                        dve.wait_ge(l_done, b + 1)
                        link(nc.vector.tensor_reduce(t1[:], lg[:], AX.X, ALU.max))
                        nc.vector.tensor_tensor(lm[p][:], lg[:], over_e(t1[:]), ALU.subtract).then_inc(ex_in, 1)
                        dve.wait_ge(ex_in, b + 1)
                        link(nc.vector.scalar_tensor_tensor(pri[:], lm[p][:], 0.0, over_t(const(SM_PRIO)), ALU.is_ge, ALU.mult))
                        link(nc.vector.tensor_reduce(first[p][:], pri[:], AX.X, ALU.max))
                        nc.vector.tensor_tensor(ohb[p][:], pri[:], over_e(first[p][:]), ALU.is_equal).then_inc(oh_done, 1)
                        dve.wait_ge(oh_done, b + 1)
                        link(nc.vector.tensor_reduce(mine[:, b, :], ohb[p][:].rearrange("p t e -> p e t"), AX.X, ALU.add))
                        if b == 0:
                            nc.vector.tensor_copy(acc[:, 0, :], mine[:, 0, :]).then_inc(acc_done, 1)
                        else:
                            nc.vector.tensor_tensor(acc[:, b, :], mine[:, b, :], acc[:, b - 1, :], ALU.add).then_inc(acc_done, 1)
                        dve.wait_ge(acc_done, b + 1)

                    def place(b):
                        p = b % 2
                        dve.wait_ge(ex_done, b + 1)
                        link(nc.vector.tensor_reduce(z[:], ex[p][:], AX.X, ALU.add))
                        link(nc.vector.reciprocal(rows[:, tiles_of(b), ROW_P], z[:]))
                        dve.wait_ge(r_full, b + 1)
                        link(nc.vector.tensor_tensor(slf[:], ps_r[:, p, :].rearrange("p (a b) -> p a b", b=EXPERTS), ohb[p][:], ALU.mult))
                        link(nc.vector.tensor_reduce(t1[:], slf[:], AX.X, ALU.add))
                        nc.vector.scalar_tensor_tensor(slot[:, tiles_of(b)], first[p][:], float(REGION), t1[:], ALU.mult, ALU.add).then_inc(slot_done, 1)
                        dve.wait_ge(slot_done, b + 1)

                    front(0)
                    norm(0)
                    dve.wait_ge(w_in, 32)
                    nc.vector.tensor_copy(rows[:, :, ROW_ID].bitcast(I32), ids_s[:]).then_inc(chain.sem, 1)
                    chain.add(1)
                    for b in range(BATCH):
                        if b + 1 < BATCH:
                            front(b + 1)
                        choose(b)
                        if b + 1 < BATCH:
                            norm(b + 1)
                        place(b)
                    dve.wait_ge(r_full, BATCH + 1)
                    dve.wait_ge(consts, 4)
                    link(nc.vector.tensor_copy(cnt[:], ps_r[:, 2, 0:EXPERTS]))
                    nc.vector.tensor_tensor(pad_first[:], cnt[:], const(SM_REGION), ALU.add).then_inc(pad_ready, 1)
                    link(nc.vector.tensor_scalar(nti[:], cnt[:], float(P - 1), None, ALU.add))
                    link(nc.vector.tensor_scalar(nti[:], nti[:], P.bit_length() - 1, None, ALU.arith_shift_right))
                    link(nc.vector.tensor_copy(ntile[:], nti[:]))
                    link(nc.vector.tensor_copy(be[0][:, EXPERTS:], ntile[:]))
                    s, k = 1, 0
                    while s < EXPERTS:
                        a, d = be[k % 2], be[(k + 1) % 2]
                        link(nc.vector.tensor_tensor(d[:, EXPERTS:], a[:, EXPERTS:], a[:, EXPERTS - s:2 * EXPERTS - s], ALU.add))
                        s, k = 2 * s, k + 1
                    total = be[k % 2][:, 2 * EXPERTS - 1:2 * EXPERTS]
                    link(nc.vector.tensor_tensor(base[:], be[k % 2][:, EXPERTS:], ntile[:], ALU.subtract))
                    tile = const(SM_TILE, SLOT_TILES)
                    link(nc.vector.tensor_tensor(cmp[:], over_e(tile, SLOT_TILES), over_t(base[:], SLOT_TILES), ALU.is_ge))
                    link(nc.vector.tensor_reduce(tef[:], cmp[:], AX.X, ALU.add))
                    link(nc.vector.tensor_scalar(tef[:], tef[:], -1.0, None, ALU.add))
                    link(nc.vector.tensor_copy(te[:], tef[:]))
                    link(nc.vector.tensor_tensor(cmp[:], cmp[:], over_t(base[:], SLOT_TILES), ALU.mult))
                    link(nc.vector.tensor_reduce(tbase[:], cmp[:], AX.X, ALU.max))
                    link(nc.vector.tensor_tensor(tbase[:], tile, tbase[:], ALU.subtract))
                    link(nc.vector.tensor_scalar(tbase[:], tbase[:], float(P), float(EXPERTS * REGION), ALU.mult, ALU.add))
                    link(nc.vector.scalar_tensor_tensor(tbase[:], tef[:], float(-REGION), tbase[:], ALU.mult, ALU.add))
                    link(nc.vector.scalar_tensor_tensor(first_row[:], tile, total, tbase[:], ALU.is_lt, ALU.mult))
        phase_experts(nc, c, ew, te, first_row, xd, out)


def phase_experts(nc, c, ew, te, first_row, xd, out):
    with ExitStack() as ctx:
        def sb(name, shape, dt=F32):
            return ctx.enter_context(nc.sbuf_tensor(name, shape, dt))

        def pb(name, shape):
            return ctx.enter_context(nc.psum_tensor(name, shape, F32))

        def sem(name):
            return ctx.enter_context(nc.semaphore(name))

        RING, W_RING, two = 8, 4, range(2)
        w = [sb(f"w_tile{r}", [P, W_END]) for r in range(W_RING)]
        xs = [sb(f"xs{r}", [P, ROW]) for r in range(RING)]
        xt = [sb(f"xst{p}", [P, P]) for p in two]
        hid = [sb(f"hid{p}", [P, FC, P]) for p in two]
        yb = [sb(f"yb{p}", [P, DIM]) for p in two]
        ro = [sb(f"row_out{r}", [P, DIM]) for r in range(RING)]
        rid = [sb(f"row_id{r}", [P, 1], I32) for r in range(RING)]
        none = sb("none", [P, 1], I32)
        ps_x = [pb(f"ps_xs{p}", [P, P]) for p in two]
        ps_h = [c.s_ps[p][:, 0:FFN].rearrange("p (f t) -> p f t", t=P) for p in two]
        ps_y = [c.s_ps[p][:, FFN:FFN + DIM] for p in two]

        x_in, y_out = [sem(f"ex_in{r}") for r in range(RING)], [sem(f"ey_out{r}") for r in range(RING)]
        id_done, none_set = sem("eid_done"), sem("none_set")
        w_ready, xt_full, xt_ready = sem("w_ready"), sem("ext_full"), sem("ext_ready")
        h_full, hid_ready, y_full, y_sum, y_ready = sem("eh_full"), sem("hid_ready"), sem("ey_full"), sem("ey_sum"), sem("ey_ready")

        def each(eng, step):
            groups = -(-SLOT_TILES // RING)
            for r in range(RING):
                step(r, r, 0)
            with eng.Fori(1, groups - 1) as i:
                for r in range(RING):
                    step(RING * i + r, r, i)
            for r in range(SLOT_TILES - RING * (groups - 1)):
                step(RING * (groups - 1) + r, r, groups - 1)

        def isn(s):
            return isinstance(s, int)

        def has(s, ahead):
            return not isn(s) or s + ahead < SLOT_TILES

        def past(s, back):
            return not isn(s) or s >= back

        def pick(table, s):
            return table[0:1, s:s + 1] if isn(s) else table[0:1, bass.ds(s, 1)]

        with nc.Block() as block:
            @block.sync
            def _(sp):
                def load(s, r, i):
                    if past(s, RING):
                        sp.wait_ge(y_ready, s + 1 - RING)
                        sp.wait_ge(id_done, s + 1 - RING)
                    row = sp.value_load(pick(first_row, s), min_val=0, max_val=EXPERTS * REGION + TOKENS)
                    sp.dma_start(xs[r][:], xd[bass.ds(row, P), :]).then_inc(x_in[r], 16)

                each(sp, load)

            @block.gpsimd
            def _(pool):
                last_token = pool.alloc_register("last_token")
                pool.reg_mov(last_token, TOKENS - 1)

                def take_ids(s, r, i):
                    pool.wait_ge(x_in[r], i * 16 + 16)
                    if past(s, RING):
                        pool.wait_ge(y_out[r], i * 16)
                    if past(s, 1):
                        pool.wait_ge(id_done, s)
                        pool.wait_ge(y_ready, s)
                    nc.gpsimd.tensor_tensor(rid[r][:], xs[r][:, ROW_ID:ROW_ID + 1].bitcast(I32), none[:], ALU.add).then_inc(id_done, 1)

                def give(s, r, i):
                    if has(s, 1):
                        take_ids(s + 1, (r + 1) % RING, i + (r + 1) // RING)
                    else:
                        pool.wait_ge(id_done, SLOT_TILES)
                        pool.wait_ge(y_ready, SLOT_TILES)
                    nc.gpsimd.indirect_dma_start(out.rearrange("b t d -> (b t) d"), bass.IndirectOffsetOnAxis(rid[r][:].bitcast(U32), 0),
                                                 ro[r][:], None, bounds_check=last_token, oob_is_err=False).then_inc(y_out[r], 16)

                nc.gpsimd.memset(none[:], 0).then_inc(none_set, 1)
                pool.wait_ge(none_set, 1)
                take_ids(0, 0, 0)
                each(pool, give)
                for r in range(RING):
                    pool.wait_ge(y_out[r], 16 * len(range(r, SLOT_TILES, RING)))

            @block.scalar
            def _(act):
                def transposed(s, p):
                    act.wait_ge(xt_full, s + 1)
                    if past(s, 2):
                        act.wait_ge(h_full, s + -1)
                    nc.scalar.activation(xt[p][:], ps_x[p][:], ACT.Copy).then_inc(xt_ready, 1)

                def gelu(s, r):
                    p, wr = r % 2, w[r % W_RING]
                    act.wait_ge(h_full, s + 1)
                    act.wait_ge(w_ready, s + 1)
                    if past(s, 2):
                        act.wait_ge(y_full, s + -1)
                    for f in range(FC):
                        last = nc.scalar.activation(hid[p][:, f, :], ps_h[p][:, f, :], ACT.Gelu, bias=wr[:, W_B1 + f:W_B1 + f + 1])
                    last.then_inc(hid_ready, 1)

                def step(s, r, i):
                    if has(s, 2):
                        transposed(s + 2, r % 2)
                    if has(s, 1):
                        gelu(s + 1, r + 1)

                transposed(0, 0)
                gelu(0, 0)
                transposed(1, 1)
                each(act, step)

            @block.vector
            def _(dve):
                def take_w(s, r):
                    e = dve.value_load(pick(te, s), min_val=0, max_val=EXPERTS - 1)
                    if past(s, W_RING):
                        dve.wait_ge(y_sum, s + 1 - W_RING)
                    nc.vector.tensor_copy(w[r % W_RING][:], ew[:, bass.ds(e, 1), :].rearrange("p a b -> p (a b)")).then_inc(w_ready, 1)

                def step(s, r, i):
                    p = r % 2
                    if has(s, 2):
                        take_w(s + 2, r + 2)
                    dve.wait_ge(y_full, s + 1)
                    dve.wait_ge(w_ready, s + 1)
                    if past(s, 2):
                        dve.wait_ge(y_ready, s + -1)
                    nc.vector.tensor_tensor(yb[p][:], ps_y[p], w[r % W_RING][:, W_B2:], ALU.add).then_inc(y_sum, 1)
                    dve.wait_ge(y_sum, s + 1)
                    dve.wait_ge(x_in[r], i * 16 + 16)
                    if past(s, RING):
                        dve.wait_ge(y_out[r], i * 16)
                    nc.vector.scalar_tensor_tensor(ro[r][:], yb[p][:], xs[r][:, ROW_P:ROW_P + 1], xs[r][:, ROW_H:ROW_H + DIM],
                                                   ALU.mult, ALU.add).then_inc(y_ready, 1)

                take_w(0, 0)
                take_w(1, 1)
                each(dve, step)

            @block.tensor
            def _(pe):
                def transpose(s, r, i):
                    pe.wait_ge(x_in[r], i * 16 + 16)
                    if past(s, 2):
                        pe.wait_ge(xt_ready, s + -1)
                    nc.tensor.transpose(ps_x[r % 2][:], xs[r][:, 0:DIM], c.ident[:]).then_inc(xt_full, 1)

                def hidden(s, r):
                    p, wr = r % 2, w[r % W_RING]
                    pe.wait_ge(xt_ready, s + 1)
                    pe.wait_ge(w_ready, s + 1)
                    if past(s, 2):
                        pe.wait_ge(hid_ready, s + -1)
                    for f in range(FC):
                        last = nc.tensor.matmul(ps_h[p][:, f, :], wr[:, f * P:(f + 1) * P], xt[p][:], start=True, stop=True)
                    last.then_inc(h_full, 1)

                def output(s, r):
                    p, wr = r % 2, w[r % W_RING]
                    pe.wait_ge(hid_ready, s + 1)
                    pe.wait_ge(w_ready, s + 1)
                    if past(s, 2):
                        pe.wait_ge(y_sum, s + -1)
                    for f in range(FC):
                        last = nc.tensor.matmul(ps_y[p], hid[p][:, f, :], wr[:, W_W2 + f * DIM:W_W2 + (f + 1) * DIM],
                                                start=(f == 0), stop=(f == FC - 1))
                    last.then_inc(y_full, 1)

                def step(s, r, i):
                    if has(s, 2):
                        transpose(s + 2, (r + 2) % RING, i + (r + 2) // RING)
                    if has(s, 1):
                        hidden(s + 1, r + 1)
                    output(s, r)

                transpose(0, 0, 0)
                hidden(0, 0)
                transpose(1, 1, 0)
                each(pe, step)


def constants():
    pos = np.arange(SEQ)
    sums = np.exp(-np.abs(pos[:, None] - pos[None, :]) / np.e).sum(-1)
    inv_sums = np.broadcast_to((1.0 / sums).astype(np.float32), (P, SEQ))
    q = np.arange(P)
    small = np.zeros((P, SM_END), np.float32)
    small[:, SM_PRIO:SM_PRIO + EXPERTS] = np.arange(EXPERTS, 0, -1)
    small[:, SM_TILE:SM_TILE + SLOT_TILES] = np.arange(SLOT_TILES)
    small[:, SM_REGION:SM_REGION + EXPERTS] = np.arange(EXPERTS, 0, -1) * REGION
    row_ids = (np.arange(BATCH)[None, :, None] * SEQ + q[:, None, None] * TPB + np.arange(TPB)).astype(np.int32).reshape(P, TILES)
    pad_row = np.zeros((P, ROW), np.float32)
    pad_row[:, ROW_ID] = (TOKENS + q).astype(np.int32).view(np.float32)
    return inv_sums, small, row_ids, pad_row


def kernel(x, L0_tok_conv_w, L0_attn_W_qkv, L0_attn_W_out, L0_attn_b_out, L0_ffn_Ws, L0_ffn_bs,
           L0_ffn_W1, L0_ffn_b1, L0_ffn_W2, L0_ffn_b2):
    import numpy as np
    import concourse.bacc as bacc
    from concourse import mybir
    from concourse.bass_utils import run_bass_kernel_spmd

    x = np.asarray(x)
    inv_sums, small, row_ids, pad_row = constants()
    ids = x.reshape(BATCH, P, TPB).transpose(1, 0, 2)
    table = np.asarray(L0_tok_conv_w).transpose(1, 2, 0).reshape(VOCAB, TAPS * DIM)
    wq, wk, wv, wt = np.split(np.asarray(L0_attn_W_qkv), 4, axis=1)
    wqk = np.stack([wq.reshape(DIM, PAIRS, 2 * DHEAD), wk.reshape(DIM, PAIRS, 2 * DHEAD)], 2).reshape(DIM, 2 * PAIRS, 2 * DHEAD)
    wt_t = wt.T.reshape(PAIRS, P, DIM).transpose(1, 0, 2)
    wo = np.asarray(L0_attn_W_out).reshape(PAIRS, 2, 2, DHEAD, DIM).transpose(1, 3, 2, 0, 4).reshape(P, 2, PAIRS, DIM)
    b_out = np.broadcast_to(np.asarray(L0_attn_b_out), (P, DIM))
    small[:, SM_BS:SM_BS + EXPERTS] = np.asarray(L0_ffn_bs)[None, :]
    w2 = np.asarray(L0_ffn_W2).reshape(EXPERTS, FC, P, DIM).transpose(0, 2, 1, 3).reshape(EXPERTS, P, FC * DIM)
    b1 = np.asarray(L0_ffn_b1).reshape(EXPERTS, FC, P).transpose(0, 2, 1)
    b2 = np.broadcast_to(np.asarray(L0_ffn_b2)[:, None, :], (EXPERTS, P, DIM))
    experts = np.concatenate([np.asarray(L0_ffn_W1), b1, w2, b2], axis=2)

    arrays = {"ids": ids, "table": table, "wqk": wqk, "wv": wv, "wt_t": wt_t, "wo": wo, "wsr": np.asarray(L0_ffn_Ws),
              "small_in": small, "ident_in": np.eye(P, dtype=np.float32), "inv_sums": inv_sums, "experts": experts,
              "b_out": b_out, "row_ids": row_ids, "pad_row": pad_row}
    arrays = {name: np.ascontiguousarray(a) for name, a in arrays.items()}
    nc = bacc.Bacc("TRN2", target_bir_lowering=False, num_devices=1)
    aps = [nc.dram_tensor(name, a.shape, mybir.dt.from_np(a.dtype), kind="ExternalInput").ap() for name, a in arrays.items()]
    out = nc.dram_tensor("out", (BATCH, SEQ, DIM), mybir.dt.float32, kind="ExternalOutput").ap()
    build(nc, *aps, out)
    r = run_bass_kernel_spmd(nc, [arrays], core_ids=[0])
    return r.results[0]["out"]
```
